# Optimizing a Trainium2 kernel written in Bass

```python
import numpy as np
import jax
import jax.numpy as jnp

def _softmax(x, axis=-1):
    return jax.nn.softmax(x, axis=axis)

def _gelu(x):
    return jax.nn.gelu(x, approximate=True)

def _silu(x):
    return jax.nn.silu(x)

def _sigmoid(x):
    return jax.nn.sigmoid(x)

def _layernorm(x, axis=-1, eps=1e-05):
    m = jnp.mean(x, axis=axis, keepdims=True)
    v = jnp.var(x, axis=axis, keepdims=True)
    return (x - m) / jnp.sqrt(v + eps)

def _scatter_add(tgt, idx, src, axis=0):
    return tgt.at[idx].add(src)

def _segment_sum(src, seg, n):
    return jax.ops.segment_sum(src, seg, n)
kernel_name = 'mk_sandwich_d2_jaxref_r8_7d4318'

def setup_inputs(seed: int=0):
    np.random.seed(seed)
    _w = jnp.asarray

    def _L0_attn_setup():
        import jax, jax.numpy as jnp
        import numpy as np
        H = 512
        D_IN = 1024
        N = 16
        K = 4
        R = 32
        EPS = 1e-06

        def rms_forward(x, eps=EPS):
            xf = x.astype(jnp.float32)
            var = jnp.mean(xf * xf, axis=-1, keepdims=True)
            return (xf * jax.lax.rsqrt(var + eps)).astype(x.dtype)
        key = jax.random.key(seed)
        ks = jax.random.split(key, 10)
        s = 0.02
        hidden_states = jax.random.normal(ks[0], (2, 128, H), dtype=jnp.float32)
        W_in = jax.random.normal(ks[1], (2 * D_IN, H), dtype=jnp.float32) * s
        conv_w = jax.random.normal(ks[2], (D_IN, K), dtype=jnp.float32) * 0.2
        conv_b = jax.random.normal(ks[3], (D_IN,), dtype=jnp.float32) * 0.02
        W_x = jax.random.normal(ks[4], (R + 2 * N, D_IN), dtype=jnp.float32) * s
        W_dt = jax.random.normal(ks[5], (D_IN, R), dtype=jnp.float32) * s
        b_dt = jax.random.normal(ks[6], (D_IN,), dtype=jnp.float32) * 0.02
        A_log = jnp.log(jnp.broadcast_to(jnp.arange(1, N + 1, dtype=jnp.float32)[None, :], (D_IN, N)))
        D = jnp.ones((D_IN,), dtype=jnp.float32)
        W_out = jax.random.normal(ks[7], (H, D_IN), dtype=jnp.float32) * s
        return {'hidden_states': hidden_states, 'W_in': W_in, 'conv_w': conv_w, 'conv_b': conv_b, 'W_x': W_x, 'W_dt': W_dt, 'b_dt': b_dt, 'A_log': A_log, 'D': D, 'W_out': W_out}
    _L0_attn_in = _L0_attn_setup()

    def _L0_ffn_setup():
        import jax, jax.numpy as jnp
        import numpy as np
        D_MODEL = 512
        D_FF = 1376

        def _dequant_linear(x, w_int, scale):
            return jnp.einsum('bsd,fd->bsf', x, w_int.astype(x.dtype)) * scale
        key = jax.random.key(seed)
        ks = jax.random.split(key, 7)
        x = jax.random.normal(ks[0], (2, 256, D_MODEL), dtype=jnp.float32)
        gate_w = jax.random.randint(ks[1], (D_FF, D_MODEL), -127, 127, dtype=jnp.int32)
        up_w = jax.random.randint(ks[2], (D_FF, D_MODEL), -127, 127, dtype=jnp.int32)
        down_w = jax.random.randint(ks[3], (D_MODEL, D_FF), -127, 127, dtype=jnp.int32)
        gate_s = jax.random.uniform(ks[4], (D_FF,), dtype=jnp.float32) * 0.01 + 0.001
        up_s = jax.random.uniform(ks[5], (D_FF,), dtype=jnp.float32) * 0.01 + 0.001
        down_s = jax.random.uniform(ks[6], (D_MODEL,), dtype=jnp.float32) * 0.01 + 0.001
        return {'x': x, 'gate_w': gate_w, 'gate_s': gate_s, 'up_w': up_w, 'up_s': up_s, 'down_w': down_w, 'down_s': down_s}
    _L0_ffn_in = _L0_ffn_setup()

    def _L1_attn_setup():
        import jax, jax.numpy as jnp
        import numpy as np
        HIDDEN = 512
        N_HEADS = 32
        KV_HEADS = 8
        HEAD_DIM = 128
        LOW_RANK = 64
        TOP_K_ROPE = 32
        ROPE_THETA = 10000.0
        B, S = (2, 256)
        GROUPS = N_HEADS // KV_HEADS
        _half = HEAD_DIM // 2
        _m = np.ones(_half, dtype=bool)
        _m[:TOP_K_ROPE] = False
        _m = np.concatenate([_m, _m])
        NOPE_MASK = np.tile(_m, KV_HEADS)
        ROPE_IDX = jnp.asarray(np.where(~NOPE_MASK)[0])
        NOPE_IDX = jnp.asarray(np.where(NOPE_MASK)[0])
        R_DIM = int((~NOPE_MASK).sum())
        C_DIM = LOW_RANK * KV_HEADS

        def _rope_tables(seq_len, dtype):
            inv_freq = 1.0 / ROPE_THETA ** (np.arange(0, HEAD_DIM, 2, dtype=np.float32) / HEAD_DIM)
            pos = np.arange(seq_len, dtype=np.float32)
            freqs = np.outer(pos, inv_freq)
            emb = np.concatenate([freqs, freqs], axis=-1)
            return (jnp.asarray(np.cos(emb), dtype), jnp.asarray(np.sin(emb), dtype))

        def _rotate_half(x):
            x1, x2 = (x[..., :HEAD_DIM // 2], x[..., HEAD_DIM // 2:])
            return jnp.concatenate([-x2, x1], axis=-1)
        key = jax.random.key(seed)
        ks = jax.random.split(key, 7)
        s = 0.02
        return {'hidden_states': jax.random.normal(ks[0], (B, S, HIDDEN), jnp.float32), 'Wq': jax.random.normal(ks[1], (N_HEADS * HEAD_DIM, HIDDEN), jnp.float32) * s, 'Wkr': jax.random.normal(ks[2], (R_DIM, HIDDEN), jnp.float32) * s, 'Wdk': jax.random.normal(ks[3], (C_DIM, HIDDEN), jnp.float32) * s, 'Wupk': jax.random.normal(ks[4], (KV_HEADS * HEAD_DIM - R_DIM, C_DIM), jnp.float32) * s, 'Wupv': jax.random.normal(ks[5], (KV_HEADS * HEAD_DIM, C_DIM), jnp.float32) * s, 'Wo': jax.random.normal(ks[6], (HIDDEN, N_HEADS * HEAD_DIM), jnp.float32) * s}
    _L1_attn_in = _L1_attn_setup()

    def _L1_ffn_setup():
        import jax, jax.numpy as jnp
        import numpy as np
        HID, INTER = (512, 1792)
        B, S = (2, 256)

        def _binary_diff_weight(w, base):
            d = w - base
            coeff = jnp.mean(jnp.abs(d))
            return base + coeff * jnp.sign(d)
        key = jax.random.key(seed)
        ks = jax.random.split(key, 7)
        return {'hidden_states': jax.random.normal(ks[0], (B, S, HID), dtype=jnp.float32), 'w1': jax.random.normal(ks[1], (INTER, HID), dtype=jnp.float32) * 0.02, 'mean_w1': jax.random.normal(ks[2], (INTER, HID), dtype=jnp.float32) * 0.02, 'w2': jax.random.normal(ks[3], (HID, INTER), dtype=jnp.float32) * 0.02, 'mean_w2': jax.random.normal(ks[4], (HID, INTER), dtype=jnp.float32) * 0.02, 'w3': jax.random.normal(ks[5], (INTER, HID), dtype=jnp.float32) * 0.02, 'mean_w3': jax.random.normal(ks[6], (INTER, HID), dtype=jnp.float32) * 0.02}
    _L1_ffn_in = _L1_ffn_setup()
    _d = {'L0_attn_hidden_states': _L0_attn_in['hidden_states'], 'L0_attn_W_in': _L0_attn_in['W_in'], 'L0_attn_conv_w': _L0_attn_in['conv_w'], 'L0_attn_conv_b': _L0_attn_in['conv_b'], 'L0_attn_W_x': _L0_attn_in['W_x'], 'L0_attn_W_dt': _L0_attn_in['W_dt'], 'L0_attn_b_dt': _L0_attn_in['b_dt'], 'L0_attn_A_log': _L0_attn_in['A_log'], 'L0_attn_D': _L0_attn_in['D'], 'L0_attn_W_out': _L0_attn_in['W_out'], 'L0_ffn_gate_w': _L0_ffn_in['gate_w'], 'L0_ffn_gate_s': _L0_ffn_in['gate_s'], 'L0_ffn_up_w': _L0_ffn_in['up_w'], 'L0_ffn_up_s': _L0_ffn_in['up_s'], 'L0_ffn_down_w': _L0_ffn_in['down_w'], 'L0_ffn_down_s': _L0_ffn_in['down_s'], 'L1_attn_Wq': _L1_attn_in['Wq'], 'L1_attn_Wkr': _L1_attn_in['Wkr'], 'L1_attn_Wdk': _L1_attn_in['Wdk'], 'L1_attn_Wupk': _L1_attn_in['Wupk'], 'L1_attn_Wupv': _L1_attn_in['Wupv'], 'L1_attn_Wo': _L1_attn_in['Wo'], 'L1_ffn_w1': _L1_ffn_in['w1'], 'L1_ffn_mean_w1': _L1_ffn_in['mean_w1'], 'L1_ffn_w2': _L1_ffn_in['w2'], 'L1_ffn_mean_w2': _L1_ffn_in['mean_w2'], 'L1_ffn_w3': _L1_ffn_in['w3'], 'L1_ffn_mean_w3': _L1_ffn_in['mean_w3']}
    _x0 = _d['L0_attn_hidden_states']
    _d['L0_attn_hidden_states'] = jax.random.normal(jax.random.fold_in(jax.random.key(seed), 1), (4, 256, 512), dtype=_x0.dtype)
    del _x0
    return _d

def reference(L0_attn_hidden_states, L0_attn_W_in, L0_attn_conv_w, L0_attn_conv_b, L0_attn_W_x, L0_attn_W_dt, L0_attn_b_dt, L0_attn_A_log, L0_attn_D, L0_attn_W_out, L0_ffn_gate_w, L0_ffn_gate_s, L0_ffn_up_w, L0_ffn_up_s, L0_ffn_down_w, L0_ffn_down_s, L1_attn_Wq, L1_attn_Wkr, L1_attn_Wdk, L1_attn_Wupk, L1_attn_Wupv, L1_attn_Wo, L1_ffn_w1, L1_ffn_mean_w1, L1_ffn_w2, L1_ffn_mean_w2, L1_ffn_w3, L1_ffn_mean_w3):

    def _L0_attn_ref(hidden_states, W_in, conv_w, conv_b, W_x, W_dt, b_dt, A_log, D, W_out):
        import jax, jax.numpy as jnp
        import numpy as np
        H = 512
        D_IN = 1024
        N = 16
        K = 4
        R = 32
        EPS = 1e-06

        def rms_forward(x, eps=EPS):
            xf = x.astype(jnp.float32)
            var = jnp.mean(xf * xf, axis=-1, keepdims=True)
            return (xf * jax.lax.rsqrt(var + eps)).astype(x.dtype)
        b, L, _ = hidden_states.shape
        proj = hidden_states @ W_in.T
        x, gate = (proj[..., :D_IN], proj[..., D_IN:])
        xpad = jnp.pad(x, ((0, 0), (K - 1, 0), (0, 0)))
        xc = conv_b
        for j in range(K):
            xc = xc + conv_w[:, j] * xpad[:, j:j + L, :]
        x = jax.nn.silu(xc)
        ssm = x @ W_x.T
        ts, Bm, Cm = (ssm[..., :R], ssm[..., R:R + N], ssm[..., R + N:])
        ts = rms_forward(ts)
        Bm = rms_forward(Bm)
        Cm = rms_forward(Cm)
        dt = jax.nn.softplus(ts @ W_dt.T + b_dt)
        A = -jnp.exp(A_log.astype(jnp.float32))

        def step(state, inp):
            dt_t, B_t, C_t, u_t = inp
            dA = jnp.exp(dt_t[..., None] * A)
            state = state * dA + (dt_t * u_t)[..., None] * B_t[:, None, :]
            y = jnp.einsum('bdn,bn->bd', state, C_t)
            return (state, y)
        init = jnp.zeros((b, D_IN, N), dtype=jnp.float32)
        xs = (dt.transpose(1, 0, 2), Bm.transpose(1, 0, 2), Cm.transpose(1, 0, 2), x.transpose(1, 0, 2))
        _, ys = jax.lax.scan(step, init, xs)
        y = ys.transpose(1, 0, 2) + x * D
        y = y * jax.nn.silu(gate)
        return y @ W_out.T

    def _L0_ffn_ref(x, gate_w, gate_s, up_w, up_s, down_w, down_s):
        import jax, jax.numpy as jnp
        import numpy as np
        D_MODEL = 512
        D_FF = 1376

        def _dequant_linear(x, w_int, scale):
            return jnp.einsum('bsd,fd->bsf', x, w_int.astype(x.dtype)) * scale
        gate = jax.nn.silu(_dequant_linear(x, gate_w, gate_s))
        up = _dequant_linear(x, up_w, up_s)
        h = gate * up
        return _dequant_linear(h, down_w, down_s)

    def _L1_attn_ref(hidden_states, Wq, Wkr, Wdk, Wupk, Wupv, Wo):
        import jax, jax.numpy as jnp
        import numpy as np
        HIDDEN = 512
        N_HEADS = 32
        KV_HEADS = 8
        HEAD_DIM = 128
        LOW_RANK = 64
        TOP_K_ROPE = 32
        ROPE_THETA = 10000.0
        B, S = (2, 256)
        GROUPS = N_HEADS // KV_HEADS
        _half = HEAD_DIM // 2
        _m = np.ones(_half, dtype=bool)
        _m[:TOP_K_ROPE] = False
        _m = np.concatenate([_m, _m])
        NOPE_MASK = np.tile(_m, KV_HEADS)
        ROPE_IDX = jnp.asarray(np.where(~NOPE_MASK)[0])
        NOPE_IDX = jnp.asarray(np.where(NOPE_MASK)[0])
        R_DIM = int((~NOPE_MASK).sum())
        C_DIM = LOW_RANK * KV_HEADS

        def _rope_tables(seq_len, dtype):
            inv_freq = 1.0 / ROPE_THETA ** (np.arange(0, HEAD_DIM, 2, dtype=np.float32) / HEAD_DIM)
            pos = np.arange(seq_len, dtype=np.float32)
            freqs = np.outer(pos, inv_freq)
            emb = np.concatenate([freqs, freqs], axis=-1)
            return (jnp.asarray(np.cos(emb), dtype), jnp.asarray(np.sin(emb), dtype))

        def _rotate_half(x):
            x1, x2 = (x[..., :HEAD_DIM // 2], x[..., HEAD_DIM // 2:])
            return jnp.concatenate([-x2, x1], axis=-1)
        bsz, q_len, _ = hidden_states.shape
        dt = hidden_states.dtype
        q = (hidden_states @ Wq.T).reshape(bsz, q_len, N_HEADS, HEAD_DIM).transpose(0, 2, 1, 3)
        k_r0 = hidden_states @ Wkr.T
        key_flat = jnp.zeros((bsz, q_len, KV_HEADS * HEAD_DIM), dt).at[..., ROPE_IDX].set(k_r0)
        k = key_flat.reshape(bsz, q_len, KV_HEADS, HEAD_DIM).transpose(0, 2, 1, 3)
        cos, sin = _rope_tables(q_len, dt)
        cos, sin = (cos[None, None], sin[None, None])
        q = q * cos + _rotate_half(q) * sin
        k = k * cos + _rotate_half(k) * sin
        k_r = k.transpose(0, 2, 1, 3).reshape(bsz, q_len, KV_HEADS * HEAD_DIM)[..., ROPE_IDX]
        c_kv = hidden_states @ Wdk.T
        k_c = c_kv @ Wupk.T
        v = (c_kv @ Wupv.T).reshape(bsz, q_len, KV_HEADS, HEAD_DIM).transpose(0, 2, 1, 3)
        key_full = jnp.zeros((bsz, q_len, KV_HEADS * HEAD_DIM), dt).at[..., NOPE_IDX].set(k_c).at[..., ROPE_IDX].set(k_r)
        k = key_full.reshape(bsz, q_len, KV_HEADS, HEAD_DIM).transpose(0, 2, 1, 3)
        k = jnp.repeat(k, GROUPS, axis=1)
        v = jnp.repeat(v, GROUPS, axis=1)
        scale = 1.0 / jnp.sqrt(jnp.asarray(HEAD_DIM, dt))
        scores = jnp.einsum('bhqd,bhkd->bhqk', q, k) * scale
        causal = jnp.tril(jnp.ones((q_len, q_len), bool))
        scores = jnp.where(causal[None, None], scores, jnp.asarray(-1000000000.0, dt))
        attn = jax.nn.softmax(scores, axis=-1)
        out = jnp.einsum('bhqk,bhkd->bhqd', attn, v)
        out = out.transpose(0, 2, 1, 3).reshape(bsz, q_len, N_HEADS * HEAD_DIM)
        return out @ Wo.T

    def _L1_ffn_ref(hidden_states, w1, mean_w1, w2, mean_w2, w3, mean_w3):
        import jax, jax.numpy as jnp
        import numpy as np
        HID, INTER = (512, 1792)
        B, S = (2, 256)

        def _binary_diff_weight(w, base):
            d = w - base
            coeff = jnp.mean(jnp.abs(d))
            return base + coeff * jnp.sign(d)
        W1 = _binary_diff_weight(w1, mean_w1)
        W2 = _binary_diff_weight(w2, mean_w2)
        W3 = _binary_diff_weight(w3, mean_w3)
        gate = jnp.einsum('bsh,ih->bsi', hidden_states, W1)
        up = jnp.einsum('bsh,ih->bsi', hidden_states, W3)
        h = jax.nn.silu(gate) * up
        return jnp.einsum('bsi,hi->bsh', h, W2)
    x = L0_attn_hidden_states
    x = x + _layernorm(_L0_attn_ref(_layernorm(x, axis=-1), L0_attn_W_in, L0_attn_conv_w, L0_attn_conv_b, L0_attn_W_x, L0_attn_W_dt, L0_attn_b_dt, L0_attn_A_log, L0_attn_D, L0_attn_W_out), axis=-1)
    x = x + _layernorm(_L0_ffn_ref(_layernorm(x, axis=-1), L0_ffn_gate_w, L0_ffn_gate_s, L0_ffn_up_w, L0_ffn_up_s, L0_ffn_down_w, L0_ffn_down_s), axis=-1)
    x = x + _layernorm(_L1_attn_ref(_layernorm(x, axis=-1), L1_attn_Wq, L1_attn_Wkr, L1_attn_Wdk, L1_attn_Wupk, L1_attn_Wupv, L1_attn_Wo), axis=-1)
    x = x + _layernorm(_L1_ffn_ref(_layernorm(x, axis=-1), L1_ffn_w1, L1_ffn_mean_w1, L1_ffn_w2, L1_ffn_mean_w2, L1_ffn_w3, L1_ffn_mean_w3), axis=-1)
    return x

_drawn_inputs = setup_inputs


def setup_inputs(seed=0):
    import zlib

    import numpy as np

    out = dict(_drawn_inputs(seed))
    spreads = {'L0_attn_D': (1.0, 0.2)}
    factors = {'L0_attn_b_dt': 3.561}
    for name, (base, spread) in spreads.items():
        noise = np.random.default_rng([zlib.crc32(name.encode()), seed]).standard_normal(out[name].shape)
        drawn = base * np.exp(spread * noise) if base else spread * noise
        out[name] = jnp.asarray(drawn.astype(out[name].dtype))
    for name, factor in factors.items():
        out[name] = (out[name] * factor).astype(out[name].dtype)
    return out
```

```python
import numpy as np
import concourse.bass as bass
from concourse import mybir

F32 = mybir.dt.float32
F32R = mybir.dt.float32r
I32 = mybir.dt.int32
ALU = mybir.AluOpType
ACT = mybir.ActivationFunctionType
AX_X = mybir.AxisListType.X

P = 128
BATCH, SEQ, DM = 4, 256, 512
TOK = BATCH * SEQ
TT = TOK // P
KM = DM // P
HALF = 512
D_IN, N_ST, K_CONV, RANK = 1024, 16, 4, 32
KI = D_IN // P
NX = RANK + 2 * N_ST
F0 = 11
F1 = 14
FF0, FF1 = 1376, 1792
HEADS, GROUPS, HD = 32, 8, 128
HPG = HEADS // GROUPS
QT = SEQ // P
ROPE_HALF = 32
RMS_EPS, LN_EPS = 1e-6, 1e-5
N_DIFF = FF1 * DM
DIFF_COLS = N_DIFF // P
NEG = -1.0e30

C_ID, C_COS, C_SIN = 0, P, P + SEQ
C_COSK, C_SINK, C_MASK, C_END = P + 2 * SEQ, P + 3 * SEQ, P + 4 * SEQ, 2 * P + 4 * SEQ
V_CW = 0
V_CB = V_CW + KI * K_CONV
V_BDT = V_CB + KI
V_AL = V_BDT + KI
V_D = V_AL + BATCH * KI * N_ST
V_END = V_D + BATCH * KI

N_SUMS = 8
KB = 1024


class Places:

    def __init__(self, nc, tag, start, end):
        self.nc, self.tag, self.at, self.end = nc, tag, start, end

    def __call__(self, name, shape, dt=F32):
        size = int(np.prod(shape[1:])) * 4
        t = self.nc.alloc_sbuf_tensor_at(f"{self.tag}_{name}", list(shape), dt, offset=self.at)
        self.at += (size + 31) // 32 * 32
        assert self.at <= self.end, (self.tag, name, self.at - self.end)
        return t


class Signals:

    def __init__(self, nc):
        self.nc, self.held = nc, []

    def __call__(self, name):
        self.held.append(self.nc.alloc_semaphore(name))
        return self.held[-1]

    def close(self):
        self.nc.clear_and_free_semaphores(self.held)
        self.nc.all_engine_barrier()


def at_least(eng, sem, value):
    if isinstance(value, int) and value <= 0:
        return
    eng.wait_ge(sem, value)


def paired_steps(eng, n, step, head=3, tail=0):
    pairs = (n - max(2, tail) - head) // 2
    for i in range(head):
        step(i, i % 2)
    if pairs > 0:
        with eng.Fori(0, pairs) as j:
            step(j * 2 + head, 1)
            step(j * 2 + head + 1, 0)
    for i in range(head + 2 * max(pairs, 0), n):
        step(i, i % 2)


def exists(i, n):
    return not isinstance(i, int) or 0 <= i < n


def f32(ap):
    return ap.bitcast(F32)


def by_batch(ap):
    return ap.rearrange("p (b t) -> p b t", b=BATCH)


def cols(i, width):
    return bass.ds(i * width, width)


def load_inputs(nc, M, x_in, consts, vectors):
    signals = Signals(nc)
    loaded = signals("inputs_loaded")
    made = signals("small_consts_made")
    with nc.Block() as block:
        @block.sync
        def _(sp):
            xv = x_in.rearrange("(t p) c -> p t c", p=P)
            sp.dma_start(M.x[:, 0:4, :], xv[:, 0:4, :]).then_inc(loaded, 16)
            sp.dma_start(M.const[:, :], consts).then_inc(loaded, 16)
            sp.wait_ge(loaded, 64)

        @block.scalar
        def _(act):
            xv = x_in.rearrange("(t p) c -> p t c", p=P)
            act.dma_start(M.x[:, 4:8, :], xv[:, 4:8, :]).then_inc(loaded, 16)
            act.dma_start(M.vec[:, :], vectors).then_inc(loaded, 16)

        @block.gpsimd
        def _(pool):
            nc.gpsimd.memset(M.half[:, :], -0.5).then_inc(made, 1)
            nc.gpsimd.memset(M.ones[:, :], 1.0).then_inc(made, 1)
            pool.wait_ge(made, 2)
    signals.close()


def finish_phase(nc, tag, M, place, K, hidden=None, gate=None, w_raw=None, acc=None,
                 out_scale=None, last_out=None, norm_only=False):
    signals = Signals(nc)
    sem = lambda n: signals(f"{tag}_{n}")
    proj = hidden is not None
    split_w, split_wl = sem("w_hi"), sem("w_lo")
    gated, h_hi, h_lo = sem("hidden_gated"), sem("hidden_hi"), sem("hidden_lo")
    y_ready, scaled = sem("y_ready"), sem("y_scaled")
    y_stats, y_moments, y_var, y_rstd, y_normed = (sem("y_stats"), sem("y_moments"), sem("y_var"),
                                                   sem("y_rstd"), sem("y_normed"))
    x_new, x_stats, x_moments, x_var, x_rstd, xn_ready = (sem("x_new"), sem("x_stats"), sem("x_moments"),
                                                          sem("x_var"), sem("x_rstd"), sem("xn_ready"))
    transposed, x_hi, x_lo, stored = sem("transposed"), sem("x_hi"), sem("x_lo"), sem("stored")
    if proj:
        wh = place("wh", [P, K, DM], F32R)
        wl = place("wl", [P, K, DM], F32R)
        hh = [place(f"hh{i}", [P, K, P], F32R) for i in range(2)]
        hl = [place(f"hl{i}", [P, K, P], F32R) for i in range(2)]
        hg = [place(f"hg{i}", [P, K, P]) for i in range(2)] if gate is not None else None
    if out_scale is not None:
        ys = place("ys", [P, DM])
    small = place("small", [P, 2, 32])
    tmp = place("tmp", [P, DM])
    xn = [place(f"xn{i}", [P, DM]) for i in range(2)]
    ident = M.const[:, C_ID:C_ID + P]
    ps_y = [M.ps[:, i, :] for i in range(2)]
    ps_t = [M.ps[:, 2 + i, :] for i in range(2)]
    store = last_out is not None

    def y_of(t, s):
        if not proj:
            return acc[:, bass.ds(t, 1), :].rearrange("p a c -> p (a c)")
        return ys[:, :] if out_scale is not None else ps_y[s]

    def x_of(t):
        return M.x[:, bass.ds(t, 1), :].rearrange("p a c -> p (a c)")

    with nc.Block() as block:
        @block.tensor
        def _(pe):
            def transposes(t, s):
                at_least(pe, xn_ready, t + 1)
                at_least(pe, x_lo, t - 1)
                for c in range(KM):
                    mm = nc.tensor.transpose(ps_t[s][:, c * P:(c + 1) * P], xn[s][:, c * P:(c + 1) * P], ident)
                mm.then_inc(transposed, 1)

            def step(t, s):
                if proj:
                    at_least(pe, h_hi, t + 1)
                    at_least(pe, h_lo, t + 1)
                    at_least(pe, scaled if out_scale is not None else y_normed, t - 1)
                    for k in range(K):
                        if isinstance(t, int) and t == 0:
                            pe.wait_ge(split_w, k + 1)
                            pe.wait_ge(split_wl, k + 1)
                        nc.tensor.matmul(ps_y[s], hh[s][:, k, :], wh[:, k, :], start=(k == 0), stop=False)
                        nc.tensor.matmul(ps_y[s], hh[s][:, k, :], wl[:, k, :], start=False, stop=False)
                        mm = nc.tensor.matmul(ps_y[s], hl[s][:, k, :], wh[:, k, :], start=False, stop=(k == K - 1))
                    mm.then_inc(y_ready, 1)
                if not store and exists(t - 1, TT):
                    transposes(t - 1, 1 - s)

            paired_steps(pe, TT, step)
            if not store:
                transposes(TT - 1, (TT - 1) % 2)

        @block.scalar
        def _(act):
            def hidden_hi(t, s):
                at_least(act, y_ready, t - 1)
                src = hidden(t, s)
                if gate is not None:
                    at_least(act, gated, t + 1)
                    src = hg[s][:, :, :]
                nc.scalar.activation(hh[s][:, :, :], src, ACT.Copy).then_inc(h_hi, 1)

            def x_high(t, s):
                at_least(act, transposed, t + 1)
                nc.scalar.activation(M.xh[:, :, cols(t, P)], ps_t[s].rearrange("p (c q) -> p c q", c=KM), ACT.Copy).then_inc(x_hi, 1)

            def step(t, s):
                if proj and exists(t + 1, TT):
                    hidden_hi(t + 1, 1 - s)
                if not store and exists(t - 1, TT):
                    x_high(t - 1, 1 - s)

            if proj:
                hidden_hi(0, 0)
                for k in range(K):
                    nc.scalar.activation(wh[:, k, :], w_raw[:, k, :], ACT.Copy).then_inc(split_w, 1)
            paired_steps(act, TT, step)
            if not store:
                x_high(TT - 1, (TT - 1) % 2)

        @block.gpsimd
        def _(pool):
            def hidden_low(t, s):
                if gate is not None:
                    at_least(pool, h_lo, t - 1)
                    nc.gpsimd.tensor_tensor(hg[s][:, :, :], hidden(t, s), gate(t, s),
                                            ALU.mult).then_inc(gated, 1)
                    src = hg[s][:, :, :]
                else:
                    src = hidden(t, s)
                at_least(pool, y_ready, t - 1)
                at_least(pool, h_hi, t + 1)
                nc.gpsimd.tensor_tensor(hl[s][:, :, :], src, f32(hh[s][:, :, :]), ALU.subtract).then_inc(h_lo, 1)

            def rstd(var, done, out, t, s, col):
                at_least(pool, var, t + 1)
                nc.gpsimd.tensor_tensor(small[:, s, out:out + 1], small[:, s, col:col + 1], M.half[:, :],
                                        ALU.pow).then_inc(done, 1)

            def step(t, s):
                if not norm_only:
                    rstd(y_var, y_rstd, 9, t, s, 8)
                rstd(x_var, x_rstd, 25, t, s, 24) if not store else None
                if proj and exists(t + 2, TT):
                    hidden_low(t + 2, s)

            if proj:
                hidden_low(0, 0)
                hidden_low(1, 1)
            paired_steps(pool, TT, step)

        @block.vector
        def _(dve):
            def x_norm(t, s):
                at_least(dve, x_rstd, t + 1)
                at_least(dve, transposed, t - 1)
                nc.vector.tensor_scalar(xn[s][:, :], x_of(t), small[:, s, 22:23], small[:, s, 25:26],
                                        ALU.subtract, ALU.mult).then_inc(xn_ready, 1)

            def x_low(t, s):
                at_least(dve, x_hi, t + 1)
                nc.vector.tensor_tensor(M.xl[:, :, cols(t, P)], ps_t[s].rearrange("p (c q) -> p c q", c=KM),
                                        f32(M.xh[:, :, cols(t, P)]), ALU.subtract).then_inc(x_lo, 1)

            def step(t, s):
                if not norm_only:
                    if proj:
                        at_least(dve, y_ready, t + 1)
                    y = y_of(t, s)
                    if out_scale is not None:
                        at_least(dve, y_normed, t)
                        nc.vector.tensor_tensor(y, ps_y[s], out_scale[:, :], ALU.mult).then_inc(scaled, 1)
                        at_least(dve, scaled, t + 1)
                    nc.vector.bn_stats(small[:, s, 0:6], y).then_inc(y_stats, 1)
                    at_least(dve, y_stats, t + 1)
                    nc.vector.bn_aggr(small[:, s, 6:8], small[:, s, 0:6]).then_inc(y_moments, 1)
                    at_least(dve, y_moments, t + 1)
                    nc.vector.tensor_scalar(small[:, s, 8:9], small[:, s, 7:8], LN_EPS, None, ALU.add).then_inc(y_var, 1)
                if not store and exists(t - 1, TT):
                    x_norm(t - 1, 1 - s)
                if not norm_only:
                    at_least(dve, y_rstd, t + 1)
                    at_least(dve, x_new, t)
                    nc.vector.tensor_scalar(tmp[:, :], y, small[:, s, 6:7], small[:, s, 9:10],
                                            ALU.subtract, ALU.mult).then_inc(y_normed, 1)
                    at_least(dve, y_normed, t + 1)
                    nc.vector.tensor_tensor(x_of(t), x_of(t), tmp[:, :], ALU.add).then_inc(x_new, 1)
                    if not store:
                        at_least(dve, x_new, t + 1)
                if not store:
                    nc.vector.bn_stats(small[:, s, 16:22], x_of(t)).then_inc(x_stats, 1)
                    at_least(dve, x_stats, t + 1)
                    if norm_only:
                        at_least(dve, xn_ready, t - 1)
                    nc.vector.bn_aggr(small[:, s, 22:24], small[:, s, 16:22]).then_inc(x_moments, 1)
                    at_least(dve, x_moments, t + 1)
                    nc.vector.tensor_scalar(small[:, s, 24:25], small[:, s, 23:24], LN_EPS, None, ALU.add).then_inc(x_var, 1)
                    if exists(t - 1, TT):
                        x_low(t - 1, 1 - s)

            if proj:
                for k in range(K):
                    dve.wait_ge(split_w, k + 1)
                    nc.vector.tensor_tensor(wl[:, k, :], w_raw[:, k, :], f32(wh[:, k, :]), ALU.subtract).then_inc(split_wl, 1)
            paired_steps(dve, TT, step)
            if not store:
                x_norm(TT - 1, (TT - 1) % 2)
                x_low(TT - 1, (TT - 1) % 2)

        if store:
            @block.sync
            def _(sp):
                for t in range(TT):
                    sp.wait_ge(x_new, t + 1)
                    sp.dma_start(last_out[t * P:(t + 1) * P, :], M.x[:, t, :]).then_inc(stored, 16)
                sp.wait_ge(stored, 16 * TT)
    signals.close()


def widen_phase(nc, tag, M, place, F, kind, raw_dram, base_dram=None, hidden=None,
                x_conv=None, gate=None, scales=None, coeff=None, second=None, diff=None):
    signals = Signals(nc)
    sem = lambda n: signals(f"{tag}_{n}")
    raw_in, down_in = [sem("raw_in0"), sem("raw_in1")], sem("down_in")
    w_diff, w_sign, w_full, w_hi, w_lo = (sem("w_diff"), sem("w_sign"), sem("w_full"),
                                                  sem("w_hi"), sem("w_lo"))
    prod, first_done, second_done = sem("products"), sem("first_done"), sem("second_done")
    tap = sem("tap")
    d_in, d_sub, d_abs = [sem("diff_in0"), sem("diff_in1")], sem("diff_sub"), sem("diff_abs")
    WC = 2 * KM * P
    RC = WC + DM if kind == "diff" else WC
    raw = [place(f"raw{i}", [P, RC], I32 if kind == "int" else F32) for i in range(2)]
    wh = [place(f"wh{i}", [P, 2, KM, P], F32R) for i in range(2)]
    wl = [place(f"wl{i}", [P, 2, KM, P], F32R) for i in range(2)]
    mid = [place(f"mid{i}", [P, TOK]) for i in range(2 if kind != "diff" else 1)]
    if kind == "diff":
        base = [place(f"base{i}", [P, RC]) for i in range(2)]
        full = [place(f"full{i}", [P, RC]) for i in range(2)]
    if diff is not None:
        DC = DIFF_COLS // N_SUMS
        dw = [place(f"dw{i}", [P, 3, DC]) for i in range(2)]
        dm = [place(f"dm{i}", [P, 3, DC]) for i in range(2)]
        tail = F - N_SUMS + 1
    else:
        tail = 0
    flat = lambda t: t[:, :, :, :].rearrange("p a k o -> p (a k o)")
    ps = [[M.ps[:, 4 * s + 2 * a:4 * s + 2 * a + 2, :].rearrange("p a c -> p (a c)") for a in range(2)] for s in range(2)]

    with nc.Block() as block:
        @block.sync
        def _(sp):
            def step(f, s):
                at_least(sp, w_lo, f - 1)
                if kind == "diff":
                    at_least(sp, w_full, f - 1)
                sp.dma_start(raw[s][:, :], raw_dram[:, cols(f, RC)]).then_inc(raw_in[s], 16)
                if kind == "diff":
                    sp.dma_start(base[s][:, :], base_dram[:, cols(f, RC)]).then_inc(raw_in[s], 16)
                if diff is not None and exists(f, N_SUMS):
                    at_least(sp, d_abs, f * 3 - 3)
                    for a, (w, m) in enumerate(diff["pairs"]):
                        sp.dma_start(dw[s][:, a, :], w[:, cols(f, DC)]).then_inc(d_in[s], 16)
                        sp.dma_start(dm[s][:, a, :], m[:, cols(f, DC)]).then_inc(d_in[s], 16)

            if second is not None and kind == "int":
                sp.dma_start(second[0][:, :, :], second[1]).then_inc(down_in, 16)
            paired_steps(sp, F, step, tail=tail)
            if second is not None and kind == "int":
                sp.wait_ge(down_in, 16)
            if diff is not None:
                sp.wait_ge(d_abs, 3 * N_SUMS)

        @block.tensor
        def _(pe):
            def step(f, s):
                at_least(pe, w_hi, f + 1)
                at_least(pe, w_lo, f + 1)
                at_least(pe, first_done, f - 1)
                at_least(pe, second_done, f - 1)
                for a in range(2):
                    for k in range(KM):
                        for w, x in ((wh, M.xh), (wh, M.xl), (wl, M.xh)):
                            for h in range(2):
                                mm = nc.tensor.matmul(ps[s][a][:, h * HALF:(h + 1) * HALF], w[s][:, a, k, :],
                                                      x[:, k, h * HALF:(h + 1) * HALF],
                                                      start=(k == 0 and w is wh and x is M.xh),
                                                      stop=(k == KM - 1 and w is wl))
                    mm.then_inc(prod, 1)

            paired_steps(pe, F, step)

        @block.scalar
        def _(act):
            def prepare(f, s):
                if kind == "diff":
                    at_least(act, w_diff, f + 1)
                    nc.scalar.activation(full[s][:, :], full[s][:, :], ACT.Sign).then_inc(w_sign, 1)
                    at_least(act, w_full, f + 1)
                    src = full[s][:, 0:WC]
                else:
                    at_least(act, raw_in[s], (f - s) * 8 + 16)
                    src = raw[s][:, 0:WC]
                at_least(act, prod, 2 * (f - 1))
                nc.scalar.activation(flat(wh[s]), src, ACT.Copy).then_inc(w_hi, 1)

            def differences(f, s):
                for a in range(3):
                    at_least(act, d_sub, 3 * f + a + 1)
                    nc.scalar.activation(dw[s][:, a, :], dw[s][:, a, :], ACT.Abs,
                                         accum_out=diff["sums"][:, a, bass.ds(f, 1)]).then_inc(d_abs, 1)

            def step(f, s):
                if exists(f + 1, F):
                    prepare(f + 1, 1 - s)
                if diff is not None and exists(f, N_SUMS):
                    differences(f, s)
                if kind == "ssm":
                    at_least(act, prod, 2 * f + 1)
                    at_least(act, first_done, f - 1)
                    nc.scalar.activation(mid[s][:, :], ps[s][0], ACT.Identity, bias=M.vec[:, bass.ds(f + V_CB, 1)],
                                         scale=M.vec[:, bass.ds(f * K_CONV + V_CW + K_CONV - 1, 1)]).then_inc(tap, 1)
                    at_least(act, prod, 2 * f + 2)
                    nc.scalar.activation(gate[:, :, cols(f, SEQ)], by_batch(ps[s][1]),
                                         ACT.Silu).then_inc(second_done, 1)
                    at_least(act, tap, 4 * f + 4)
                    nc.scalar.activation(x_conv[:, :, cols(f, SEQ)], by_batch(mid[s][:, :]),
                                         ACT.Silu).then_inc(first_done, 1)
                else:
                    m = mid[s % len(mid)]
                    at_least(act, prod, 2 * f + 1)
                    at_least(act, second_done, f - len(mid) + 1)
                    sc = scales[0][:, bass.ds(f, 1)] if kind == "int" else 1.0
                    nc.scalar.activation(m[:, :], ps[s][0], ACT.Silu, scale=sc).then_inc(first_done, 1)

            prepare(0, 0)
            paired_steps(act, F, step, tail=tail)

        @block.gpsimd
        def _(pool):
            def lows(f, s):
                if kind == "diff":
                    at_least(pool, w_full, f + 1)
                at_least(pool, w_hi, f + 1)
                src = full[s][:, 0:WC] if kind == "diff" else raw[s][:, 0:WC]
                nc.gpsimd.tensor_tensor(flat(wl[s]), src, f32(flat(wh[s])), ALU.subtract).then_inc(w_lo, 1)

            def difference(f, s):
                at_least(pool, raw_in[s], (f - s) * 16 + 32)
                at_least(pool, w_lo, f - 1)
                nc.gpsimd.tensor_tensor(full[s][:, :], raw[s][:, :], base[s][:, :], ALU.subtract).then_inc(w_diff, 1)

            def step(f, s):
                if kind == "diff":
                    if exists(f + 1, F):
                        difference(f + 1, 1 - s)
                if kind != "int":
                    lows(f, s)
                if diff is not None and exists(f, N_SUMS):
                    at_least(pool, d_in[s], (f - s) * 48 + 96)
                    for a in range(3):
                        nc.gpsimd.tensor_tensor(dw[s][:, a, :], dw[s][:, a, :], dm[s][:, a, :], ALU.subtract).then_inc(d_sub, 1)

            if kind == "diff":
                difference(0, 0)
            if kind != "int" or diff is not None:
                paired_steps(pool, F, step, tail=tail)

        @block.vector
        def _(dve):
            def int_lows(f, s):
                at_least(dve, w_hi, f + 1)
                nc.vector.tensor_tensor(flat(wl[s]), raw[s][:, :], f32(flat(wh[s])), ALU.subtract).then_inc(w_lo, 1)

            def whole(f, s):
                at_least(dve, w_sign, f + 1)
                for a, lo, hi in ((0, 0, WC // 2), (1, WC // 2, WC), (2, WC, RC)):
                    src = full[s][:, lo:hi]
                    dst = second[0][:, bass.ds(f, 1), :].rearrange("p a c -> p (a c)") if a == 2 else src
                    ins = nc.vector.scalar_tensor_tensor(dst, src, coeff[:, a:a + 1], base[s][:, lo:hi], ALU.mult, ALU.add)
                ins.then_inc(w_full, 1)

            def step(f, s):
                if kind == "int" and exists(f + 1, F):
                    int_lows(f + 1, 1 - s)
                if kind == "diff" and exists(f + 1, F):
                    whole(f + 1, 1 - s)
                if kind == "ssm":
                    m = mid[s][:, :].rearrange("p (b t) -> p b t", b=BATCH)
                    src = ps[s][0].rearrange("p (b t) -> p b t", b=BATCH)
                    for j in range(1, K_CONV):
                        at_least(dve, tap, 4 * f + j)
                        nc.vector.scalar_tensor_tensor(m[:, :, j:SEQ], src[:, :, 0:SEQ - j],
                                                       M.vec[:, bass.ds(f * K_CONV + V_CW + K_CONV - 1 - j, 1)],
                                                       m[:, :, j:SEQ], ALU.mult, ALU.add).then_inc(tap, 1)
                else:
                    at_least(dve, prod, 2 * f + 2)
                    at_least(dve, first_done, f + 1)
                    sc = scales[1][:, bass.ds(f, 1)] if kind == "int" else 1.0
                    nc.vector.scalar_tensor_tensor(hidden[:, bass.ds(f, 1), :].rearrange("p a c -> p (a c)"), ps[s][1],
                                                   sc, mid[s % len(mid)][:, :], ALU.mult, ALU.mult).then_inc(second_done, 1)

            if kind == "diff":
                whole(0, 0)
            if kind == "int":
                int_lows(0, 0)
            paired_steps(dve, F, step)
            if kind != "ssm":
                dve.wait_ge(second_done, F)
    signals.close()


def ssm_parameters(nc, M, place, x_conv, dt, bc_dram, wx_dram, wdt_dram, block_mean_dram):
    signals = Signals(nc)
    sem = lambda n: signals(f"par_{n}")
    loaded, raw_ready, squared, mean_ready, eps_added, rooted, inverse, normed = (
        sem("loaded"), sem("raw_ready"), sem("squared"), sem("mean_ready"), sem("eps_added"), sem("rooted"),
        sem("inverse"), sem("normed"))
    kept, stored = sem("kept"), sem("bc_stored")
    pre, magnitude, exped, logged, positive, dt_done = (sem("pre"), sem("magnitude"), sem("exped"), sem("logged"),
                                                        sem("positive"), sem("dt_done"))
    wx = place("wx", [P, KI, NX])
    wdt = place("wdt", [RANK, D_IN])
    block_mean = place("block_mean", [NX, NX])
    raw = place("raw", [NX, TOK])
    sq = place("sq", [NX, TOK])
    ssm = place("ssm", [NX, TOK])
    log1p = M.scratch32
    ps_x = M.ps[0:NX, 0:2, :].rearrange("p a c -> p (a c)")
    ps_m = M.ps[0:NX, 2:4, :].rearrange("p a c -> p (a c)")
    ps_dt = [M.ps[:, 4 + 2 * s:6 + 2 * s, :].rearrange("p a c -> p (a c)") for s in range(2)]
    with nc.Block() as block:
        @block.sync
        def _(sp):
            sp.dma_start(wx[:, :, :], wx_dram).then_inc(loaded, 16)
            sp.dma_start(wdt[:, :], wdt_dram).then_inc(loaded, 16)
            sp.dma_start(block_mean[:, :], block_mean_dram).then_inc(loaded, 16)
            sp.wait_ge(normed, 1)
            for b in range(BATCH):
                sp.dma_start(bc_dram[b, :, :], ssm[RANK:NX, b * SEQ:(b + 1) * SEQ]).then_inc(stored, 16)
            sp.wait_ge(stored, 16 * BATCH)

        @block.tensor
        def _(pe):
            pe.wait_ge(loaded, 48)
            for h in range(2):
                for k in range(KI):
                    mm = nc.tensor.matmul(ps_x[:, h * HALF:(h + 1) * HALF], wx[:, k, :],
                                          x_conv[:, 2 * h:2 * h + 2, k * SEQ:(k + 1) * SEQ],
                                          start=(k == 0), stop=(k == KI - 1))
                mm.then_inc(raw_ready, 1)
            pe.wait_ge(squared, 1)
            for h in range(2):
                mm = nc.tensor.matmul(ps_m[:, h * HALF:(h + 1) * HALF], block_mean[:, :],
                                      sq[:, h * HALF:(h + 1) * HALF], start=True, stop=True)
            mm.then_inc(mean_ready, 1)
            pe.wait_ge(normed, 1)
            for f in range(KI):
                at_least(pe, magnitude, f - 1)
                at_least(pe, positive, f - 1)
                for h in range(2):
                    mm = nc.tensor.matmul(ps_dt[f % 2][:, h * HALF:(h + 1) * HALF], wdt[:, f * P:(f + 1) * P],
                                          ssm[0:RANK, h * HALF:(h + 1) * HALF], start=True, stop=True)
                mm.then_inc(pre, 1)

        @block.scalar
        def _(act):
            act.wait_ge(raw_ready, 2)
            nc.scalar.activation(raw[:, :], ps_x, ACT.Copy).then_inc(kept, 1)
            nc.scalar.activation(sq[:, :], ps_x, ACT.Square).then_inc(squared, 1)
            act.wait_ge(eps_added, 1)
            nc.scalar.activation(sq[:, :], sq[:, :], ACT.Sqrt).then_inc(rooted, 1)
            for f in range(KI):
                act.wait_ge(pre, f + 1)
                nc.scalar.activation(log1p[:, f * TOK:(f + 1) * TOK], ps_dt[f % 2], ACT.Abs,
                                     bias=M.vec[:, V_BDT + f:V_BDT + f + 1]).then_inc(magnitude, 1)
                act.wait_ge(magnitude, f + 1)
                nc.scalar.activation(log1p[:, f * TOK:(f + 1) * TOK], log1p[:, f * TOK:(f + 1) * TOK],
                                     ACT.Exp, scale=-1.0).then_inc(exped, 1)
            for f in range(KI):
                act.wait_ge(exped, f + 1)
                nc.scalar.activation(log1p[:, f * TOK:(f + 1) * TOK], log1p[:, f * TOK:(f + 1) * TOK],
                                     ACT.Ln, bias=1.0).then_inc(logged, 1)
            nc.scalar.activation(M.vec[:, V_AL:V_D], M.vec[:, V_AL:V_D], ACT.Exp).then_inc(kept, 1)

        @block.vector
        def _(dve):
            dve.wait_ge(mean_ready, 1)
            dve.wait_ge(squared, 1)
            nc.vector.tensor_scalar(sq[:, :], ps_m, RMS_EPS, None, ALU.add).then_inc(eps_added, 1)
            dve.wait_ge(rooted, 1)
            nc.vector.reciprocal(sq[:, :], sq[:, :]).then_inc(inverse, 1)
            dve.wait_ge(inverse, 1)
            dve.wait_ge(kept, 1)
            nc.vector.tensor_tensor(ssm[:, :], raw[:, :], sq[:, :], ALU.mult).then_inc(normed, 1)
            for f in range(KI):
                dve.wait_ge(magnitude, f + 1)
                bias = M.vec[:, V_BDT + f:V_BDT + f + 1]
                nc.vector.tensor_scalar(dt[:, :, f * SEQ:(f + 1) * SEQ], by_batch(ps_dt[f % 2]), bias, 0.0,
                                        ALU.add, ALU.max).then_inc(positive, 1)
            for f in range(KI):
                dve.wait_ge(logged, f + 1)
                dve.wait_ge(positive, f + 1)
                part = dt[:, :, f * SEQ:(f + 1) * SEQ]
                nc.vector.tensor_tensor(part, part, by_batch(log1p[:, f * TOK:(f + 1) * TOK]), ALU.add).then_inc(dt_done, 1)
            dve.wait_ge(kept, 2)
            nc.vector.tensor_scalar(M.vec[:, V_AL:V_D], M.vec[:, V_AL:V_D], -1.0, None, ALU.mult).then_inc(dt_done, 1)
    signals.close()


def scan_phase(nc, M, place, x_conv, dt, bc_dram):
    signals = Signals(nc)
    sem = lambda n: signals(f"scan_{n}")
    NH = N_ST // 2
    W = NH * SEQ
    SLOTS = 4
    b_in, c_in = [sem("b_in0"), sem("b_in1")], [sem("c_in0"), sem("c_in1")]
    heads_zero, inflow_in, decayed, u_ready = sem("heads_zero"), sem("inflow"), sem("decayed"), sem("u_ready")
    scanned, weighted, slots_free, finished = sem("scanned"), sem("weighted"), sem("slots_free"), sem("finished")
    bm = place("bm", [P, N_ST, SEQ])
    cm = place("cm", [P, N_ST, SEQ])
    decay = [place(f"decay{i}", [P, NH, SEQ]) for i in range(2)]
    u = [place(f"u{i}", [P, SEQ]) for i in range(2)]
    state = [M.scratch32[:, i * W:(i + 1) * W] for i in range(SLOTS)]
    ident = M.const[:, C_ID:C_ID + P]
    ps_y = [M.ps[:, i, 0:SEQ] for i in range(2)]
    flat_x = x_conv[:, :, :].rearrange("p b c -> p (b c)")
    flat_dt = dt[:, :, :].rearrange("p b c -> p (b c)")

    def pairs(eng, body):
        body(0, 0)
        with eng.Fori(1, KI // 2) as j:
            body(0, j)
        with eng.Fori(1, BATCH) as b:
            with eng.Fori(0, KI // 2) as j:
                body(b, j)

    with nc.Block() as block:
        @block.sync
        def _(sp):
            def load(b):
                for h in range(2):
                    at_least(sp, inflow_in, b * 2 * KI - 1 + h)
                    sp.dma_start(bm[:, h * NH:(h + 1) * NH, :],
                                 bc_dram[bass.ds(b, 1), h * NH:(h + 1) * NH, :].broadcast_to((P, NH, SEQ))).then_inc(b_in[h], 16)
                for h in range(2):
                    at_least(sp, weighted, b * 2 * KI - 1 + h)
                    sp.dma_start(cm[:, h * NH:(h + 1) * NH, :],
                                 bc_dram[bass.ds(b, 1), N_ST + h * NH:N_ST + (h + 1) * NH, :].broadcast_to((P, NH, SEQ))).then_inc(c_in[h], 16)
            load(0)
            with sp.Fori(1, BATCH) as b:
                load(b)

        @block.gpsimd
        def _(pool):
            for i in range(2):
                nc.gpsimd.memset(decay[i][:, :, 0:1], 0.0).then_inc(heads_zero, 1)
            pool.wait_ge(heads_zero, 2)
            pool.sem_inc(slots_free, SLOTS)

            def body(b, j):
                for r in range(2):
                    s = b * KI + j * 2 + r
                    at_least(pool, inflow_in, s * 2 - 2)
                    nc.gpsimd.tensor_tensor(u[r][:, :], flat_dt[:, cols(s, SEQ)], flat_x[:, cols(s, SEQ)],
                                            ALU.mult).then_inc(u_ready, 1)
                    pool.wait_ge(u_ready, s + 1)
                    for h in range(2):
                        pool.wait_ge(b_in[h], b * 16 + 16)
                        pool.wait_ge(slots_free, s * 2 + h + 1)
                        nc.gpsimd.tensor_tensor(state[2 * r + h].rearrange("p (n t) -> p n t", n=NH),
                                                bm[:, h * NH:(h + 1) * NH, :],
                                                u[r][:, :].rearrange("p (a t) -> p a t", a=1).broadcast_to((P, NH, SEQ)),
                                                ALU.mult).then_inc(inflow_in, 1)
            pairs(pool, body)

        @block.scalar
        def _(act):
            act.wait_ge(heads_zero, 2)

            def body(b, j):
                for r in range(2):
                    s = b * KI + j * 2 + r
                    for h in range(2):
                        at_least(act, scanned, s * 2 + h - 1)
                        for n in range(NH):
                            ins = nc.scalar.activation(decay[h][:, n, 1:SEQ], flat_dt[:, bass.ds(s * SEQ + 1, SEQ - 1)], ACT.Exp,
                                                       scale=M.vec[:, bass.ds(s * N_ST + V_AL + h * NH + n, 1)])
                        ins.then_inc(decayed, 1)
            pairs(act, body)

        @block.vector
        def _(dve):
            def finish(s, r):
                dve.wait_ge(slots_free, s * 2 + 2 + SLOTS)
                nc.vector.scalar_tensor_tensor(flat_x[:, cols(s, SEQ)], flat_x[:, cols(s, SEQ)],
                                               M.vec[:, bass.ds(s + V_D, 1)], ps_y[r], ALU.mult, ALU.add).then_inc(finished, 1)

            def body(b, j):
                for r in range(2):
                    s = b * KI + j * 2 + r
                    for h in range(2):
                        q = state[2 * r + h]
                        dve.wait_ge(decayed, s * 2 + h + 1)
                        dve.wait_ge(inflow_in, s * 2 + h + 1)
                        nc.vector.tensor_tensor_scan(q, decay[h][:, :, :].rearrange("p n t -> p (n t)"), q, 0.0,
                                                     ALU.mult, ALU.add).then_inc(scanned, 1)
                        dve.wait_ge(scanned, s * 2 + h + 1)
                        dve.wait_ge(c_in[h], b * 16 + 16)
                        nc.vector.tensor_tensor(q, q, cm[:, h * NH:(h + 1) * NH, :].rearrange("p n t -> p (n t)"),
                                                ALU.mult).then_inc(weighted, 1)
                        if h == 0 and not (isinstance(s, int) and s == 0):
                            finish(s - 1, 1 - r)
            pairs(dve, body)
            finish(BATCH * KI - 1, 1)

        @block.tensor
        def _(pe):
            def body(b, j):
                for r in range(2):
                    s = b * KI + j * 2 + r
                    at_least(pe, finished, s - 1)
                    for h in range(2):
                        pe.wait_ge(weighted, s * 2 + h + 1)
                        for n in range(NH):
                            mm = nc.tensor.matmul(ps_y[r], ident, state[2 * r + h][:, n * SEQ:(n + 1) * SEQ],
                                                  start=(h == 0 and n == 0), stop=(h == 1 and n == NH - 1))
                        mm.then_inc(slots_free, 1)
            pairs(pe, body)
    signals.close()


def project_phase(nc, tag, M, place, F, w_dram, xh, xl, evacuate):
    signals = Signals(nc)
    sem = lambda n: signals(f"{tag}_{n}")
    S = type("S", (), {})()
    raw_in = [sem("raw_in0"), sem("raw_in1")]
    w_hi, w_lo, S.prod = sem("w_hi"), sem("w_lo"), sem("products")
    S.act_done, S.dve_done, S.pool_done = sem("act_done"), sem("dve_done"), sem("pool_done")
    raw = [place(f"raw{i}", [P, KM * P]) for i in range(2)]
    wh = [place(f"wh{i}", [P, KM, P], F32R) for i in range(2)]
    wl = [place(f"wl{i}", [P, KM, P], F32R) for i in range(2)]
    flat = lambda t: t[:, :, :].rearrange("p k o -> p (k o)")
    S.ps = [M.ps[:, 2 * s:2 * s + 2, :].rearrange("p a c -> p (a c)") for s in range(2)]
    acts, dves, pools, per_act, per_dve = evacuate
    with nc.Block() as block:
        @block.sync
        def _(sp):
            for f in range(F):
                at_least(sp, w_lo, f - 1)
                sp.dma_start(raw[f % 2][:, :], w_dram[:, f * KM * P:(f + 1) * KM * P]).then_inc(raw_in[f % 2], 16)

        @block.tensor
        def _(pe):
            for f in range(F):
                pe.wait_ge(w_hi, f + 1)
                pe.wait_ge(w_lo, f + 1)
                at_least(pe, S.act_done, per_act * (f - 1))
                at_least(pe, S.dve_done, per_dve * (f - 1))
                for k in range(KM):
                    for w, x in ((wh, xh), (wh, xl), (wl, xh)):
                        for h in range(2):
                            mm = nc.tensor.matmul(S.ps[f % 2][:, h * HALF:(h + 1) * HALF], w[f % 2][:, k, :],
                                                  x[:, k, h * HALF:(h + 1) * HALF],
                                                  start=(k == 0 and w is wh and x is xh), stop=(k == KM - 1 and w is wl))
                mm.then_inc(S.prod, 1)

        @block.scalar
        def _(act):
            for f in range(F + 1):
                if f < F:
                    act.wait_ge(raw_in[f % 2], (f // 2 + 1) * 16)
                    at_least(act, S.prod, f - 1)
                    nc.scalar.activation(flat(wh[f % 2]), raw[f % 2][:, :], ACT.Copy).then_inc(w_hi, 1)
                if f >= 1:
                    acts(act, S, f - 1)

        @block.gpsimd
        def _(pool):
            for f in range(F + 1):
                if f < F:
                    pool.wait_ge(w_hi, f + 1)
                    nc.gpsimd.tensor_tensor(flat(wl[f % 2]), raw[f % 2][:, :], f32(flat(wh[f % 2])), ALU.subtract).then_inc(w_lo, 1)
                if f >= 1:
                    pools(pool, S, f - 1)

        @block.vector
        def _(dve):
            for f in range(F):
                dves(dve, S, f)
    signals.close()


def key_value_phases(nc, M, place_at, K, V, ch, cl, wdk, wkr, wupk, wupv):
    def act_c(act, S, f):
        act.wait_ge(S.prod, f + 1)
        nc.scalar.activation(ch[:, f, :], S.ps[f % 2], ACT.Copy).then_inc(S.act_done, 1)

    def dve_c(dve, S, f):
        dve.wait_ge(S.act_done, f + 1)
        nc.vector.tensor_tensor(cl[:, f, :], S.ps[f % 2], f32(ch[:, f, :]), ALU.subtract).then_inc(S.dve_done, 1)

    project_phase(nc, "lat", M, place_at("lat"), KM, wdk, M.xh, M.xl, (act_c, dve_c, lambda *a: None, 1, 1))

    place = place_at("rot")
    turned = [place(f"turned{i}", [P, TOK]) for i in range(2)]
    direct = [place(f"direct{i}", [P, TOK]) for i in range(2)]
    R = ROPE_HALF
    table = lambda c: M.const[:, c:c + SEQ].rearrange("p (b t) -> p b t", b=1).broadcast_to((P, BATCH, SEQ))

    def act_r(act, S, f):
        act.wait_ge(S.prod, f + 1)
        at_least(act, S.dve_done, 5 * (f - 1))
        for q in range(4):
            o = (q ^ 1) * R
            nc.scalar.activation(turned[f % 2][q * R:(q + 1) * R, :], S.ps[f % 2][o:o + R, :], ACT.Copy).then_inc(S.act_done, 1)

    def pool_r(pool, S, f):
        pool.wait_ge(S.act_done, 4 * f + 4)
        nc.gpsimd.tensor_tensor(by_batch(turned[f % 2][:, :]), by_batch(turned[f % 2][:, :]), table(C_SINK), ALU.mult).then_inc(S.pool_done, 1)

    def dve_r(dve, S, f):
        dve.wait_ge(S.act_done, 4 * f + 4)
        at_least(dve, S.dve_done, 5 * (f - 1))
        nc.vector.tensor_tensor(by_batch(direct[f % 2][:, :]), by_batch(S.ps[f % 2]), table(C_COSK), ALU.mult).then_inc(S.dve_done, 1)
        dve.wait_ge(S.dve_done, 5 * f + 1)
        dve.wait_ge(S.pool_done, f + 1)
        for q in range(4):
            rows = slice(q * R, (q + 1) * R)
            to = (q % 2) * 2 * R
            nc.vector.tensor_tensor(K[to:to + R, 2 * f + q // 2, :], direct[f % 2][rows, :], turned[f % 2][rows, :], ALU.add).then_inc(S.dve_done, 1)

    project_phase(nc, "krot", M, place, KM, wkr, M.xh, M.xl, (act_r, dve_r, pool_r, 4, 5))

    def act_n(act, S, f):
        act.wait_ge(S.prod, f + 1)
        for q in range(2):
            to = (q % 2) * 2 * R + R
            nc.scalar.activation(K[to:to + R, 2 * f, :], S.ps[f % 2][q * R:(q + 1) * R, :], ACT.Copy).then_inc(S.act_done, 1)

    def dve_n(dve, S, f):
        dve.wait_ge(S.prod, f + 1)
        for q in range(2, 4):
            to = (q % 2) * 2 * R + R
            nc.vector.tensor_copy(K[to:to + R, 2 * f + 1, :], S.ps[f % 2][q * R:(q + 1) * R, :]).then_inc(S.dve_done, 1)

    project_phase(nc, "kplain", M, place_at("kplain"), KM, wupk, ch, cl, (act_n, dve_n, lambda *a: None, 2, 2))

    place = place_at("val")
    signals = Signals(nc)
    sem = lambda n: signals(f"val_{n}")
    raw_in, w_hi, w_lo, c_hi, c_lo, prod, kept = (sem("raw_in"), sem("w_hi"), sem("w_lo"), sem("c_hi"), sem("c_lo"),
                                                  sem("products"), sem("kept"))
    VC = GROUPS * HD
    raw = place("raw", [P, KM, VC])
    wh, wl = place("wh", [P, KM, VC], F32R), place("wl", [P, KM, VC], F32R)
    th = [place(f"th{i}", [P, KM, P], F32R) for i in range(2)]
    tl = [place(f"tl{i}", [P, KM, P], F32R) for i in range(2)]
    ps = [M.ps[:, 2 * s:2 * s + 2, :].rearrange("p a c -> p (a c)") for s in range(2)]
    with nc.Block() as block:
        @block.sync
        def _(sp):
            for k in range(KM):
                sp.dma_start(raw[:, k, :], wupv[:, k, :]).then_inc(raw_in, 16)

        @block.tensor
        def _(pe):
            def step(t, s):
                pe.wait_ge(c_hi, t + 1)
                pe.wait_ge(c_lo, t + 1)
                at_least(pe, kept, t - 1)
                for k in range(KM):
                    if isinstance(t, int) and t == 0:
                        pe.wait_ge(w_lo, k + 1)
                    for c, w in ((th, wh), (th, wl), (tl, wh)):
                        for h in range(2):
                            mm = nc.tensor.matmul(ps[s][:, h * HALF:(h + 1) * HALF], c[s][:, k, :], w[:, k, h * HALF:(h + 1) * HALF],
                                                  start=(k == 0 and w is wh and c is th), stop=(k == KM - 1 and c is tl))
                mm.then_inc(prod, 1)
            paired_steps(pe, TT, step)

        @block.scalar
        def _(act):
            for k in range(KM):
                act.wait_ge(raw_in, 16 * KM)
                nc.scalar.activation(wh[:, k, :], raw[:, k, :], ACT.Copy).then_inc(w_hi, 1)

            def step(t, s):
                act.wait_ge(prod, t + 1)
                nc.scalar.activation(V[:, bass.ds(t, 1), :].rearrange("p a c -> p (a c)"), ps[s], ACT.Copy).then_inc(kept, 1)
            paired_steps(act, TT, step)

        @block.vector
        def _(dve):
            def step(t, s):
                at_least(dve, prod, t - 1)
                nc.vector.tensor_copy(th[s][:, :, :], f32(ch[:, :, cols(t, P)])).then_inc(c_hi, 1)
                nc.vector.tensor_copy(tl[s][:, :, :], f32(cl[:, :, cols(t, P)])).then_inc(c_lo, 1)

            for k in range(KM):
                dve.wait_ge(w_hi, k + 1)
                nc.vector.tensor_tensor(wl[:, k, :], raw[:, k, :], f32(wh[:, k, :]), ALU.subtract).then_inc(w_lo, 1)
            paired_steps(dve, TT, step)
    signals.close()


def attention_phase(nc, M, place, K, V, acc, wq, wo):
    signals = Signals(nc)
    sem = lambda n: signals(f"att_{n}")
    U = GROUPS * BATCH
    SCALE = float(HD) ** -0.5
    raw_in, wq_hi, wq_lo, wo_hi, wo_lo = sem("raw_in"), sem("wq_hi"), sem("wq_lo"), sem("wo_hi"), sem("wo_lo")
    q_prod, q_turned, q_sine, q_cosine, q_done = (sem("q_prod"), sem("q_turned"), sem("q_sine"), sem("q_cosine"), sem("q_done"))
    scored, masked, maxed, neg_max, exped, inverse, normed = (sem("scored"), sem("masked"), sem("maxed"), sem("neg_max"),
                                                              sem("exped"), sem("inverse"), sem("normed"))
    flipped, p_kept_act, p_kept_dve, v_here, summed, o_hi, o_lo, o_prod, added = (
        sem("flipped"), sem("p_kept_act"), sem("p_kept_dve"), sem("v_here"), sem("summed"), sem("o_hi"), sem("o_lo"),
        sem("o_prod"), sem("added"))
    zeroed = sem("acc_zeroed")
    QC = HPG * HD
    raw = place("raw", [P, KM * QC])
    wqh, wql = place("wqh", [P, KM, QC], F32R), place("wql", [P, KM, QC], F32R)
    woh, wol = place("woh", [P, HPG, DM], F32R), place("wol", [P, HPG, DM], F32R)
    q = place("q", [P, HPG, SEQ])
    direct, turned = place("direct", [P, HPG * SEQ]), place("turned", [P, HPG * SEQ])
    pa, pb = place("pa", [P, HPG, P]), place("pb", [P, HPG, SEQ])
    pt = place("pt", [P, 3, HALF])
    vs = place("vs", [P, QT, HD])
    oh, ol = place("oh", [P, QT, HALF], F32R), place("ol", [P, QT, HALF], F32R)
    mx, nm, sums, inv = (place(n, [P, 8]) for n in ("mx", "nm", "sums", "inv"))
    ident = M.const[:, C_ID:C_ID + P]
    ps_q = M.ps[:, 0:2, :].rearrange("p a c -> p (a c)")
    s0 = M.ps[:, 2, :].rearrange("p (h k) -> p h k", h=HPG)
    s1 = M.ps[:, 3:5, :].rearrange("p a (h k) -> p (a h) k", k=SEQ)
    X = [M.ps[:, 5 + i, :] for i in range(3)]
    flat = lambda t: t[:, :, :].rearrange("p a c -> p (a c)")
    heads = lambda ap: ap.rearrange("p (h t) -> p h t", h=HPG)
    over_heads = lambda c, w: M.const[:, c:c + w].rearrange("p (h t) -> p h t", h=1).broadcast_to((P, HPG, w))

    def groups(eng, body):
        for b in range(BATCH):
            body(0, b)
        with eng.Fori(1, GROUPS - 1) as g:
            for b in range(BATCH):
                body(g, b)
        for b in range(BATCH):
            body(GROUPS - 1, b)

    def more(g, b):
        return not (isinstance(g, int) and g == GROUPS - 1 and b == BATCH - 1)

    def after(g, b):
        return (g, b + 1) if b < BATCH - 1 else (g + 1, 0)

    with nc.Block() as block:
        @block.sync
        def _(sp):
            def load(g):
                at_least(sp, wo_lo, g)
                sp.dma_start(raw[:, :], wq[:, cols(g, KM * QC)]).then_inc(raw_in, 16)
                sp.wait_ge(wq_lo, g + 1)
                sp.dma_start(raw[:, :], wo[:, cols(g, HPG * DM)]).then_inc(raw_in, 16)
            load(0)
            with sp.Fori(1, GROUPS) as g:
                load(g)

        @block.tensor
        def _(pe):
            def queries(g, b):
                v = g * BATCH + b
                if b == 0:
                    pe.wait_ge(wq_hi, g + 1)
                    pe.wait_ge(wq_lo, g + 1)
                at_least(pe, q_turned, v)
                at_least(pe, q_cosine, v)
                for h in range(HPG):
                    for k in range(KM):
                        for w, x in ((wqh, M.xh), (wqh, M.xl), (wql, M.xh)):
                            mm = nc.tensor.matmul(ps_q[:, h * SEQ:(h + 1) * SEQ], w[:, k, h * HD:(h + 1) * HD],
                                                  x[:, k, b * SEQ:(b + 1) * SEQ],
                                                  start=(k == 0 and w is wqh and x is M.xh), stop=(k == KM - 1 and w is wql))
                mm.then_inc(q_prod, 1)

            def scores(g, b):
                v = g * BATCH + b
                pe.wait_ge(q_done, v + 1)
                at_least(pe, exped, v)
                keys = K[:, bass.ds(g, 1), :].rearrange("p a t -> p (a t)")
                for h in range(HPG):
                    nc.tensor.matmul(s0[:, h, :], q[:, h, 0:P], keys[:, b * SEQ:b * SEQ + P], start=True, stop=True)
                for h in range(HPG):
                    mm = nc.tensor.matmul(s1[:, h, :], q[:, h, P:SEQ], keys[:, b * SEQ:(b + 1) * SEQ], start=True, stop=True)
                mm.then_inc(scored, 1)

            def output(g, b):
                v = g * BATCH + b
                if b == 0:
                    pe.wait_ge(wo_hi, g + 1)
                    pe.wait_ge(wo_lo, g + 1)
                pe.wait_ge(o_lo, v * 2 + 2)
                for t in range(QT):
                    for h in range(HPG):
                        part = slice(h * P, (h + 1) * P)
                        nc.tensor.matmul(X[t], oh[:, t, part], woh[:, h, :], start=(h == 0), stop=False)
                        nc.tensor.matmul(X[t], oh[:, t, part], wol[:, h, :], start=False, stop=False)
                        mm = nc.tensor.matmul(X[t], ol[:, t, part], woh[:, h, :], start=False, stop=(h == HPG - 1))
                mm.then_inc(o_prod, 1)

            def attend(g, b):
                v = g * BATCH + b
                pe.wait_ge(normed, v + 1)
                for h in range(HPG):
                    mm = nc.tensor.transpose(X[2][:, h * P:(h + 1) * P], pa[:, h, :], ident)
                mm.then_inc(flipped, 1)
                at_least(pe, added, v)
                for i in range(QT):
                    for h in range(HPG):
                        mm = nc.tensor.transpose(X[i][:, h * P:(h + 1) * P], pb[:, h, i * P:(i + 1) * P], ident)
                    mm.then_inc(flipped, 1)
                pe.wait_ge(v_here, v + 1)
                pe.wait_ge(p_kept_act, v * 2 + 1)
                nc.tensor.matmul(X[2], vs[:, 0, :], pt[:, 0, :], start=True, stop=True).then_inc(summed, 1)
                pe.wait_ge(p_kept_dve, v + 1)
                nc.tensor.matmul(X[0], vs[:, 0, :], pt[:, 1, :], start=True, stop=False)
                pe.wait_ge(p_kept_act, v * 2 + 2)
                nc.tensor.matmul(X[0], vs[:, 1, :], pt[:, 2, :], start=False, stop=True).then_inc(summed, 1)

            def body(g, b):
                if more(g, b):
                    queries(*after(g, b))
                if b > 0:
                    output(g, b - 1)
                elif not (isinstance(g, int) and g == 0):
                    output(g - 1, BATCH - 1)
                attend(g, b)
                if more(g, b):
                    scores(*after(g, b))

            queries(0, 0)
            scores(0, 0)
            groups(pe, body)
            output(GROUPS - 1, BATCH - 1)

        @block.scalar
        def _(act):
            def turn(g, b):
                v = g * BATCH + b
                act.wait_ge(q_prod, v + 1)
                at_least(act, q_done, v)
                nc.scalar.activation(turned[0:64, :], ps_q[64:128, :], ACT.Copy)
                nc.scalar.activation(turned[64:128, :], ps_q[0:64, :], ACT.Copy).then_inc(q_turned, 1)

            def exps(g, b):
                v = g * BATCH + b
                act.wait_ge(neg_max, v + 1)
                at_least(act, flipped, v * 3)
                at_least(act, inverse, v)
                for h in range(HPG):
                    nc.scalar.activation(pa[:, h, :], s0[:, h, :], ACT.Exp, bias=nm[:, h:h + 1], scale=SCALE,
                                         accum_out=sums[:, h:h + 1])
                for h in range(HPG):
                    ins = nc.scalar.activation(pb[:, h, :], s1[:, h, :], ACT.Exp, bias=nm[:, 4 + h:5 + h], scale=SCALE,
                                               accum_out=sums[:, 4 + h:5 + h])
                ins.then_inc(exped, 1)

            def query_weights(g):
                act.wait_ge(raw_in, g * 32 + 16)
                at_least(act, q_prod, g * BATCH)
                nc.scalar.activation(flat(wqh), raw[:, :], ACT.Copy).then_inc(wq_hi, 1)

            def output_weights(g):
                act.wait_ge(raw_in, g * 32 + 32)
                at_least(act, o_prod, g * BATCH)
                nc.scalar.activation(flat(woh), raw[:, :], ACT.Copy).then_inc(wo_hi, 1)

            def body(g, b):
                v = g * BATCH + b
                if more(g, b):
                    turn(*after(g, b))
                if b == 2 and not (isinstance(g, int) and g == GROUPS - 1):
                    query_weights(g + 1)
                at_least(act, summed, v * 2)
                act.wait_ge(flipped, v * 3 + 1)
                nc.scalar.activation(pt[:, 0, :], X[2], ACT.Copy).then_inc(p_kept_act, 1)
                act.wait_ge(flipped, v * 3 + 3)
                nc.scalar.activation(pt[:, 2, :], X[1], ACT.Copy).then_inc(p_kept_act, 1)
                at_least(act, o_prod, v)
                for t, x in ((0, X[2]), (1, X[0])):
                    act.wait_ge(summed, v * 2 + t + 1)
                    nc.scalar.activation(oh[:, t, :], x, ACT.Copy).then_inc(o_hi, 1)
                if b == 0:
                    output_weights(g)
                if more(g, b):
                    exps(*after(g, b))

            query_weights(0)
            turn(0, 0)
            exps(0, 0)
            groups(act, body)

        @block.gpsimd
        def _(pool):
            def sine(g, b):
                v = g * BATCH + b
                pool.wait_ge(q_turned, v + 1)
                nc.gpsimd.tensor_tensor(heads(turned[:, :]), heads(turned[:, :]), over_heads(C_SIN, SEQ), ALU.mult).then_inc(q_sine, 1)

            def query_weights(g):
                pool.wait_ge(wq_hi, g + 1)
                nc.gpsimd.tensor_tensor(flat(wql), raw[:, :], f32(flat(wqh)), ALU.subtract).then_inc(wq_lo, 1)

            def output_weights(g):
                pool.wait_ge(wo_hi, g + 1)
                nc.gpsimd.tensor_tensor(flat(wol), raw[:, :], f32(flat(woh)), ALU.subtract).then_inc(wo_lo, 1)

            def body(g, b):
                if more(g, b):
                    sine(*after(g, b))
                if b == 2 and not (isinstance(g, int) and g == GROUPS - 1):
                    query_weights(g + 1)
                if b == 0:
                    output_weights(g)

            query_weights(0)
            sine(0, 0)
            groups(pool, body)

        @block.vector
        def _(dve):
            def rotate(g, b):
                v = g * BATCH + b
                dve.wait_ge(q_turned, v + 1)
                nc.vector.tensor_tensor(heads(direct[:, :]), heads(ps_q), over_heads(C_COS, SEQ), ALU.mult).then_inc(q_cosine, 1)
                dve.wait_ge(q_cosine, v + 1)
                dve.wait_ge(q_sine, v + 1)
                at_least(dve, scored, v)
                nc.vector.tensor_tensor(flat(q), direct[:, :], turned[:, :], ALU.add).then_inc(q_done, 1)

            def maxima(g, b):
                v = g * BATCH + b
                dve.wait_ge(scored, v + 1)
                nc.vector.tensor_tensor(s0, s0, over_heads(C_MASK, P), ALU.add).then_inc(masked, 1)
                nc.vector.tensor_tensor(s1[:, :, P:SEQ], s1[:, :, P:SEQ], over_heads(C_MASK, P), ALU.add).then_inc(masked, 1)
                dve.wait_ge(masked, v * 2 + 2)
                at_least(dve, exped, v)
                nc.vector.tensor_reduce(mx[:, 0:4], s0, AX_X, ALU.max).then_inc(maxed, 1)
                nc.vector.tensor_reduce(mx[:, 4:8], s1, AX_X, ALU.max).then_inc(maxed, 1)
                dve.wait_ge(maxed, v * 2 + 2)
                nc.vector.tensor_scalar(nm[:, :], mx[:, :], -SCALE, None, ALU.mult).then_inc(neg_max, 1)

            def probabilities(g, b):
                v = g * BATCH + b
                dve.wait_ge(exped, v + 1)
                at_least(dve, normed, v)
                nc.vector.reciprocal(inv[:, :], sums[:, :]).then_inc(inverse, 1)
                dve.wait_ge(inverse, v + 1)
                for h in range(HPG):
                    nc.vector.tensor_scalar(pa[:, h, :], pa[:, h, :], inv[:, h:h + 1], None, ALU.mult)
                for h in range(HPG):
                    ins = nc.vector.tensor_scalar(pb[:, h, :], pb[:, h, :], inv[:, 4 + h:5 + h], None, ALU.mult)
                ins.then_inc(normed, 1)

            def accumulate(v, b):
                dve.wait_ge(o_prod, v + 1)
                part = flat(acc[:, QT * b:QT * b + QT, :])
                nc.vector.tensor_tensor(part, M.ps[:, 5:7, :].rearrange("p a c -> p (a c)"), part, ALU.add).then_inc(added, 1)

            def body(g, b):
                v = g * BATCH + b
                if more(g, b):
                    rotate(*after(g, b))
                if not (isinstance(v, int) and v == 0):
                    accumulate(v - 1, (b - 1) % BATCH)
                at_least(dve, summed, v * 2)
                nc.vector.tensor_copy(vs[:, :, :], V[:, QT * b:QT * b + QT, cols(g, HD)]).then_inc(v_here, 1)
                dve.wait_ge(flipped, v * 3 + 2)
                nc.vector.tensor_copy(pt[:, 1, :], X[0]).then_inc(p_kept_dve, 1)
                for t, x in ((0, X[2]), (1, X[0])):
                    dve.wait_ge(o_hi, v * 2 + t + 1)
                    nc.vector.tensor_tensor(ol[:, t, :], x, f32(oh[:, t, :]), ALU.subtract).then_inc(o_lo, 1)
                if more(g, b):
                    maxima(*after(g, b))
                    probabilities(*after(g, b))

            nc.vector.memset(flat(acc), 0.0).then_inc(zeroed, 1)
            dve.wait_ge(zeroed, 1)
            rotate(0, 0)
            maxima(0, 0)
            probabilities(0, 0)
            groups(dve, body)
            accumulate(U - 1, BATCH - 1)
    signals.close()


def coefficients(nc, M):
    signals = Signals(nc)
    rows, total, done = (signals(f"coeff_{n}") for n in ("rows", "total", "done"))
    with nc.Block() as block:
        @block.vector
        def _(dve):
            nc.vector.tensor_reduce(M.row_sums[:, :], M.diff_sums[:, :, :], AX_X, ALU.add).then_inc(rows, 1)
            dve.wait_ge(total, 1)
            nc.vector.tensor_scalar(M.coeff[:, :], M.ps[:, 0, 0:3], 1.0 / N_DIFF, None, ALU.mult).then_inc(done, 1)
            dve.wait_ge(done, 1)

        @block.tensor
        def _(pe):
            pe.wait_ge(rows, 1)
            nc.tensor.matmul(M.ps[:, 0, 0:3], M.ones[:, :], M.row_sums[:, :], start=True, stop=True).then_inc(total, 1)
    signals.close()


def program(nc, D, out, stop_after=None, taps=None):
    M = type("Memory", (), {})()
    M.ps = nc.alloc_psum_tensor("psum", [P, 8, HALF], F32)
    base = (nc.sbuf_base + 31) // 32 * 32
    end = nc.sbuf_usable_end
    resident = Places(nc, "res", base, base + 6 * KB)
    M.const = resident("const", [P, C_END])
    M.ones = resident("ones", [P, P])
    M.half = resident("half", [P, 1])
    M.diff_sums = resident("diff_sums", [P, 3, N_SUMS])
    M.row_sums = resident("row_sums", [P, 3])
    M.coeff = resident("coeff", [P, 3])
    z = resident.at
    at = lambda tag, kb: Places(nc, tag, z + kb * KB, end)
    M.x = at("tok", 0)("x", [P, TT, DM])
    opnd = at("opnd", 16)
    M.xh, M.xl = opnd("xh", [P, KM, TOK], F32R), opnd("xl", [P, KM, TOK], F32R)
    M.scratch32 = at("scratch", 16)("s", [P, 8 * TOK])

    mamba = at("ssm", 48)
    x_conv = mamba("x_conv", [P, BATCH, KI * SEQ])
    gate = mamba("gate", [P, BATCH, KI * SEQ])
    dt = mamba("dt", [P, BATCH, KI * SEQ])
    M.vec = mamba("vec", [P, V_END])
    free = (mamba.at - z + KB - 1) // KB
    load_inputs(nc, M, D["x"], D["const"], D["vec"])
    if stop_after == "load": return M
    finish_phase(nc, "n0", M, at("n0", free), 0, norm_only=True)
    if stop_after == "n0": return M
    widen_phase(nc, "in", M, at("in", free), KI, "ssm", D["w_in"], x_conv=x_conv, gate=gate)
    M.x_conv, M.gate, M.dt = x_conv, gate, dt
    if stop_after == "in": return M
    ssm_parameters(nc, M, at("par", free), x_conv, dt, D["bc"], D["w_x"], D["w_dt"], D["block_mean"])
    if stop_after == "par": return M
    scan_phase(nc, M, at("scan", free), x_conv, dt, D["bc"])
    if stop_after == "scan": return M
    tile_of = lambda a: (lambda t, s: a[:, :, :].rearrange("p b (d c) -> p (b d c)", d=KI)[:, bass.ds((t - s) * (KI * P), KI * SEQ)]
                         .rearrange("p (d c) -> p d c", d=KI)[:, :, s * P:(s + 1) * P])
    w_res = at("wout", 112)("raw", [P, KI, DM])
    load_weight(nc, "wout", w_res, D["w_out"])
    finish_phase(nc, "fa", M, at("fa", 128), KI, hidden=tile_of(x_conv), gate=tile_of(gate), w_raw=w_res)
    if stop_after == "fa": return M

    mlp = at("mlp0", 48)
    hidden = mlp("hidden", [P, F0, TOK])
    down = mlp("down", [P, F0, DM], I32)
    sc = [mlp("gate_s", [P, F0]), mlp("up_s", [P, F0])]
    scale_row = mlp("down_s", [P, DM])
    mlp0 = (mlp.at - z + KB - 1) // KB
    load_scales(nc, sc, scale_row, D["gate_s"], D["up_s"], D["down_s"])
    widen_phase(nc, "mi", M, at("mi", mlp0), F0, "int", D["w_gu"], hidden=hidden, scales=sc, second=(down, D["w_down"]),
                diff=dict(pairs=[(D["dw1"], D["dm1"]), (D["dw3"], D["dm3"]), (D["dw2"], D["dm2"])], sums=M.diff_sums))
    plain = lambda a: (lambda t, s: a[:, :, cols(t, P)])
    finish_phase(nc, "fb", M, at("fb", mlp0), F0, hidden=plain(hidden), w_raw=down, out_scale=scale_row)
    if stop_after == "fb": return M

    att = at("att", 48)
    ch, cl = att("ch", [P, KM, TOK], F32R), att("cl", [P, KM, TOK], F32R)
    K, V = att("k", [P, GROUPS, TOK]), att("v", [P, TT, GROUPS * HD])
    M.K, M.V, M.ch = K, V, ch
    key_value_phases(nc, M, lambda tag: at(tag, 144), K, V, ch, cl, D["w_dk"], D["w_kr"], D["w_upk"], D["w_upv"])
    if stop_after == "kv": return M
    acc = at("acc", 48)("acc", [P, TT, DM])
    att2 = at("att2", 64)
    place = split_places(nc, z + 64 * KB, z + 80 * KB, z + 144 * KB, end)
    attention_phase(nc, M, place, K, V, acc, D["w_q"], D["w_o"])
    M.acc = acc
    if stop_after == "att": return M
    finish_phase(nc, "fc", M, at("fc", 80), 0, acc=acc)
    if stop_after == "fc": return M

    coefficients(nc, M)
    mlp = at("mlp1", 48)
    hidden = mlp("hidden", [P, F1, TOK])
    down = mlp("down", [P, F1, DM])
    widen_phase(nc, "md", M, mlp, F1, "diff", D["w_mlp"], D["b_mlp"], hidden=hidden, coeff=M.coeff, second=(down,))
    M.hidden, M.down = hidden, down
    if stop_after == "md": return M
    last = split_places(nc, z + 16 * KB, z + 48 * KB, z + 132 * KB, end)
    finish_phase(nc, "fd", M, last, F1, hidden=plain(hidden), w_raw=down, last_out=out)
    return M


def split_places(nc, a0, a1, b0, b1):
    first, rest = Places(nc, "low", a0, a1), Places(nc, "high", b0, b1)

    def place(name, shape, dt=F32):
        size = int(np.prod(shape[1:])) * 4
        return (first if first.at + size <= first.end else rest)(name, shape, dt)
    return place


def load_weight(nc, tag, dst, src):
    signals = Signals(nc)
    loaded = signals(f"{tag}_loaded")
    with nc.Block() as block:
        @block.sync
        def _(sp):
            sp.dma_start(dst[:, :, :], src).then_inc(loaded, 16)
            sp.wait_ge(loaded, 16)
    signals.close()


def load_scales(nc, sc, row, gate_s, up_s, down_s):
    signals = Signals(nc)
    loaded = signals("scales_loaded")
    with nc.Block() as block:
        @block.sync
        def _(sp):
            sp.dma_start(sc[0][:, :], gate_s).then_inc(loaded, 16)
            sp.dma_start(sc[1][:, :], up_s).then_inc(loaded, 16)
            sp.dma_start(row[:, :], down_s.broadcast_to((P, DM))).then_inc(loaded, 16)
            sp.wait_ge(loaded, 48)
    signals.close()




def shape_constants():
    c = np.zeros((P, C_END), np.float32)
    c[:, C_ID:C_ID + P] = np.eye(P, dtype=np.float32)
    inv = 1.0 / 10000.0 ** (np.arange(0, HD, 2, dtype=np.float32) / HD)
    freqs = np.outer(np.arange(SEQ, dtype=np.float32), inv.astype(np.float32)).astype(np.float32)
    cos, sin = np.cos(freqs).T.astype(np.float32), np.sin(freqs).T.astype(np.float32)
    c[:, C_COS:C_COS + SEQ] = np.concatenate([cos, cos])
    c[:, C_SIN:C_SIN + SEQ] = np.concatenate([-sin, sin])
    kc, ks = cos[:ROPE_HALF], sin[:ROPE_HALF]
    c[:, C_COSK:C_COSK + SEQ] = np.concatenate([kc, kc, kc, kc])
    c[:, C_SINK:C_SINK + SEQ] = np.concatenate([-ks, ks, -ks, ks])
    c[:, C_MASK:C_MASK + P] = np.where(np.arange(P)[None, :] > np.arange(P)[:, None], NEG, 0.0)
    m = np.zeros((NX, NX), np.float32)
    for lo, hi in ((0, RANK), (RANK, RANK + N_ST), (RANK + N_ST, NX)):
        m[lo:hi, lo:hi] = 1.0 / (hi - lo)
    return c, m


def stationary(w, tiles=None):
    o, i = w.shape
    return w.reshape(o // P, P, i // P, P).transpose(3, 0, 2, 1)


def rows_padded(w, n):
    return np.concatenate([w, np.zeros((n - w.shape[0],) + w.shape[1:], w.dtype)])


def contraction_major(w):
    o, i = w.shape
    return np.ascontiguousarray(w.T.reshape(i // P, P, o).transpose(1, 0, 2))


def lay_out(a):
    flat = lambda w: np.ascontiguousarray(w.reshape(P, -1))
    per_channel = lambda v: v.reshape(KI, P, -1).transpose(1, 0, 2).reshape(P, -1)
    c, m = shape_constants()
    L = {"x": a["L0_attn_hidden_states"].reshape(TOK, DM), "const": c, "block_mean": m}
    L["vec"] = np.ascontiguousarray(np.concatenate(
        [per_channel(a["L0_attn_conv_w"]), per_channel(a["L0_attn_conv_b"]), per_channel(a["L0_attn_b_dt"])]
        + [per_channel(a["L0_attn_A_log"])] * BATCH + [per_channel(a["L0_attn_D"])] * BATCH, axis=1))
    w = a["L0_attn_W_in"]
    L["w_in"] = flat(np.stack([stationary(w[:D_IN]), stationary(w[D_IN:])], axis=2))
    L["w_x"] = contraction_major(a["L0_attn_W_x"])
    L["w_dt"] = np.ascontiguousarray(a["L0_attn_W_dt"].T)
    L["w_out"] = contraction_major(a["L0_attn_W_out"])
    g, u = (rows_padded(a[f"L0_ffn_{n}_w"], F0 * P) for n in ("gate", "up"))
    L["w_gu"] = flat(np.stack([stationary(g), stationary(u)], axis=2))
    L["w_down"] = contraction_major(rows_padded(a["L0_ffn_down_w"].T, F0 * P).T)
    for n in ("gate", "up"):
        L[f"{n}_s"] = np.ascontiguousarray(rows_padded(a[f"L0_ffn_{n}_s"], F0 * P).reshape(F0, P).T)
    L["down_s"] = a["L0_ffn_down_s"].reshape(1, DM)
    L["w_dk"], L["w_kr"], L["w_upk"] = (flat(stationary(a[f"L1_attn_{n}"])) for n in ("Wdk", "Wkr", "Wupk"))
    L["w_upv"] = contraction_major(a["L1_attn_Wupv"])
    L["w_q"] = np.ascontiguousarray(a["L1_attn_Wq"].reshape(GROUPS, HPG * HD, KM, P).transpose(3, 0, 2, 1)).reshape(P, -1)
    L["w_o"] = np.ascontiguousarray(a["L1_attn_Wo"].T.reshape(GROUPS, HPG, P, DM).transpose(2, 0, 1, 3)).reshape(P, -1)
    for name, w1, w3, w2 in (("w_mlp", "w1", "w3", "w2"), ("b_mlp", "mean_w1", "mean_w3", "mean_w2")):
        s1, s3 = (stationary(a[f"L1_ffn_{n}"]).reshape(P, F1, -1) for n in (w1, w3))
        s2 = contraction_major(a[f"L1_ffn_{w2}"])
        L[name] = np.ascontiguousarray(np.concatenate([s1, s3, s2], axis=2)).reshape(P, -1)
    for n in ("1", "2", "3"):
        L[f"dw{n}"] = a[f"L1_ffn_w{n}"].reshape(P, -1)
        L[f"dm{n}"] = a[f"L1_ffn_mean_w{n}"].reshape(P, -1)
    return L


def kernel(**inputs):
    import concourse.bacc as bacc
    from concourse.bass_utils import run_bass_kernel_spmd

    nc = bacc.Bacc("TRN2", target_bir_lowering=False, num_devices=1)
    arrays = lay_out({n: np.asarray(v) for n, v in inputs.items()})
    D = {n: nc.dram_tensor(f"in_{n}", v.shape, mybir.dt.from_np(v.dtype), kind="ExternalInput").ap() for n, v in arrays.items()}
    D["bc"] = nc.dram_tensor("bc_rows", (BATCH, 2 * N_ST, SEQ), F32).ap()
    out = nc.dram_tensor("out", (TOK, DM), F32, kind="ExternalOutput").ap()
    program(nc, D, out)
    r = run_bass_kernel_spmd(nc, [{f"in_{n}": v for n, v in arrays.items()}], core_ids=[0])
    return r.results[0]["out"].reshape(BATCH, SEQ, DM)
```

```python
import numpy as np
import concourse.bass as bass
from concourse import mybir

F32 = mybir.dt.float32
F32R = mybir.dt.float32r
I32 = mybir.dt.int32
ALU = mybir.AluOpType
ACT = mybir.ActivationFunctionType
AX_X = mybir.AxisListType.X

P = 128
BATCH, SEQ, DM = 4, 256, 512
TOK = BATCH * SEQ
TT = TOK // P
KM = DM // P
HALF = 512
D_IN, N_ST, K_CONV, RANK = 1024, 16, 4, 32
KI = D_IN // P
NX = RANK + 2 * N_ST
F0 = 11
F1 = 14
FF0, FF1 = 1376, 1792
HEADS, GROUPS, HD = 32, 8, 128
HPG = HEADS // GROUPS
QT = SEQ // P
ROPE_HALF = 32
RMS_EPS, LN_EPS = 1e-6, 1e-5
N_DIFF = FF1 * DM
DIFF_COLS = N_DIFF // P
NEG = -1.0e30

C_ID, C_COS, C_SIN = 0, P, P + SEQ
C_COSK, C_SINK, C_MASK, C_END = P + 2 * SEQ, P + 3 * SEQ, P + 4 * SEQ, 2 * P + 4 * SEQ
V_CW = 0
V_CB = V_CW + KI * K_CONV
V_BDT = V_CB + KI
V_AL = V_BDT + KI
V_D = V_AL + BATCH * KI * N_ST
V_END = V_D + BATCH * KI

N_SUMS = 8
KB = 1024


class Places:

    def __init__(self, nc, tag, start, end):
        self.nc, self.tag, self.at, self.end = nc, tag, start, end

    def __call__(self, name, shape, dt=F32):
        size = int(np.prod(shape[1:])) * 4
        t = self.nc.alloc_sbuf_tensor_at(f"{self.tag}_{name}", list(shape), dt, offset=self.at)
        self.at += (size + 31) // 32 * 32
        assert self.at <= self.end, (self.tag, name, self.at - self.end)
        return t


class Signals:

    def __init__(self, nc):
        self.nc, self.held = nc, []

    def __call__(self, name):
        self.held.append(self.nc.alloc_semaphore(name))
        return self.held[-1]

    def close(self):
        self.nc.clear_and_free_semaphores(self.held)
        self.nc.all_engine_barrier()


def at_least(eng, sem, value):
    if isinstance(value, int) and value <= 0:
        return
    eng.wait_ge(sem, value)


def paired_steps(eng, n, step, head=3, tail=0):
    pairs = (n - max(2, tail) - head) // 2
    for i in range(head):
        step(i, i % 2)
    if pairs > 0:
        with eng.Fori(0, pairs) as j:
            step(j * 2 + head, 1)
            step(j * 2 + head + 1, 0)
    for i in range(head + 2 * max(pairs, 0), n):
        step(i, i % 2)


def exists(i, n):
    return not isinstance(i, int) or 0 <= i < n


def f32(ap):
    return ap.bitcast(F32)


def by_batch(ap):
    return ap.rearrange("p (b t) -> p b t", b=BATCH)


def cols(i, width):
    return bass.ds(i * width, width)


def load_inputs(nc, M, x_in, consts, vectors):
    signals = Signals(nc)
    loaded = signals("inputs_loaded")
    made = signals("small_consts_made")
    with nc.Block() as block:
        @block.sync
        def _(sp):
            xv = x_in.rearrange("(t p) c -> p t c", p=P)
            sp.dma_start(M.x[:, 0:4, :], xv[:, 0:4, :]).then_inc(loaded, 16)
            sp.dma_start(M.const[:, :], consts).then_inc(loaded, 16)
            sp.wait_ge(loaded, 64)

        @block.scalar
        def _(act):
            xv = x_in.rearrange("(t p) c -> p t c", p=P)
            act.dma_start(M.x[:, 4:8, :], xv[:, 4:8, :]).then_inc(loaded, 16)
            act.dma_start(M.vec[:, :], vectors).then_inc(loaded, 16)

        @block.gpsimd
        def _(pool):
            nc.gpsimd.memset(M.half[:, :], -0.5).then_inc(made, 1)
            nc.gpsimd.memset(M.ones[:, :], 1.0).then_inc(made, 1)
            pool.wait_ge(made, 2)
    signals.close()


def finish_phase(nc, tag, M, place, K, hidden=None, gate=None, w_raw=None, acc=None,
                 out_scale=None, last_out=None, norm_only=False):
    signals = Signals(nc)
    sem = lambda n: signals(f"{tag}_{n}")
    proj = hidden is not None
    split_w, split_wl = sem("w_hi"), sem("w_lo")
    gated, h_hi, h_lo = sem("hidden_gated"), sem("hidden_hi"), sem("hidden_lo")
    y_ready, scaled = sem("y_ready"), sem("y_scaled")
    y_stats, y_moments, y_var, y_rstd, y_normed = (sem("y_stats"), sem("y_moments"), sem("y_var"),
                                                   sem("y_rstd"), sem("y_normed"))
    x_new, x_stats, x_moments, x_var, x_rstd, xn_ready = (sem("x_new"), sem("x_stats"), sem("x_moments"),
                                                          sem("x_var"), sem("x_rstd"), sem("xn_ready"))
    transposed, x_hi, x_lo, stored = sem("transposed"), sem("x_hi"), sem("x_lo"), sem("stored")
    if proj:
        wh = place("wh", [P, K, DM], F32R)
        wl = place("wl", [P, K, DM], F32R)
        hh = [place(f"hh{i}", [P, K, P], F32R) for i in range(2)]
        hl = [place(f"hl{i}", [P, K, P], F32R) for i in range(2)]
        hg = [place(f"hg{i}", [P, K, P]) for i in range(2)] if gate is not None else None
    if out_scale is not None:
        ys = place("ys", [P, DM])
    small = place("small", [P, 2, 32])
    tmp = place("tmp", [P, DM])
    xn = [place(f"xn{i}", [P, DM]) for i in range(2)]
    ident = M.const[:, C_ID:C_ID + P]
    ps_y = [M.ps[:, i, :] for i in range(2)]
    ps_t = [M.ps[:, 2 + i, :] for i in range(2)]
    store = last_out is not None

    def y_of(t, s):
        if not proj:
            return acc[:, bass.ds(t, 1), :].rearrange("p a c -> p (a c)")
        return ys[:, :] if out_scale is not None else ps_y[s]

    def x_of(t):
        return M.x[:, bass.ds(t, 1), :].rearrange("p a c -> p (a c)")

    with nc.Block() as block:
        @block.tensor
        def _(pe):
            def transposes(t, s):
                at_least(pe, xn_ready, t + 1)
                at_least(pe, x_lo, t - 1)
                for c in range(KM):
                    mm = nc.tensor.transpose(ps_t[s][:, c * P:(c + 1) * P], xn[s][:, c * P:(c + 1) * P], ident)
                mm.then_inc(transposed, 1)

            def step(t, s):
                if proj:
                    at_least(pe, h_hi, t + 1)
                    at_least(pe, h_lo, t + 1)
                    at_least(pe, scaled if out_scale is not None else y_normed, t - 1)
                    for k in range(K):
                        if isinstance(t, int) and t == 0:
                            pe.wait_ge(split_w, k + 1)
                            pe.wait_ge(split_wl, k + 1)
                        nc.tensor.matmul(ps_y[s], hh[s][:, k, :], wh[:, k, :], start=(k == 0), stop=False)
                        nc.tensor.matmul(ps_y[s], hh[s][:, k, :], wl[:, k, :], start=False, stop=False)
                        mm = nc.tensor.matmul(ps_y[s], hl[s][:, k, :], wh[:, k, :], start=False, stop=(k == K - 1))
                    mm.then_inc(y_ready, 1)
                if not store and exists(t - 1, TT):
                    transposes(t - 1, 1 - s)

            paired_steps(pe, TT, step)
            if not store:
                transposes(TT - 1, (TT - 1) % 2)

        @block.scalar
        def _(act):
            def hidden_hi(t, s):
                at_least(act, y_ready, t - 1)
                src = hidden(t, s)
                if gate is not None:
                    at_least(act, gated, t + 1)
                    src = hg[s][:, :, :]
                nc.scalar.activation(hh[s][:, :, :], src, ACT.Copy).then_inc(h_hi, 1)

            def x_high(t, s):
                at_least(act, transposed, t + 1)
                nc.scalar.activation(M.xh[:, :, cols(t, P)], ps_t[s].rearrange("p (c q) -> p c q", c=KM), ACT.Copy).then_inc(x_hi, 1)

            def step(t, s):
                if proj and exists(t + 1, TT):
                    hidden_hi(t + 1, 1 - s)
                if not store and exists(t - 1, TT):
                    x_high(t - 1, 1 - s)

            if proj:
                hidden_hi(0, 0)
                for k in range(K):
                    nc.scalar.activation(wh[:, k, :], w_raw[:, k, :], ACT.Copy).then_inc(split_w, 1)
            paired_steps(act, TT, step)
            if not store:
                x_high(TT - 1, (TT - 1) % 2)

        @block.gpsimd
        def _(pool):
            def hidden_low(t, s):
                if gate is not None:
                    at_least(pool, h_lo, t - 1)
                    nc.gpsimd.tensor_tensor(hg[s][:, :, :], hidden(t, s), gate(t, s),
                                            ALU.mult).then_inc(gated, 1)
                    src = hg[s][:, :, :]
                else:
                    src = hidden(t, s)
                at_least(pool, y_ready, t - 1)
                at_least(pool, h_hi, t + 1)
                nc.gpsimd.tensor_tensor(hl[s][:, :, :], src, f32(hh[s][:, :, :]), ALU.subtract).then_inc(h_lo, 1)

            def rstd(var, done, out, t, s, col):
                at_least(pool, var, t + 1)
                nc.gpsimd.tensor_tensor(small[:, s, out:out + 1], small[:, s, col:col + 1], M.half[:, :],
                                        ALU.pow).then_inc(done, 1)

            def step(t, s):
                if not norm_only:
                    rstd(y_var, y_rstd, 9, t, s, 8)
                rstd(x_var, x_rstd, 25, t, s, 24) if not store else None
                if proj and exists(t + 2, TT):
                    hidden_low(t + 2, s)

            if proj:
                hidden_low(0, 0)
                hidden_low(1, 1)
            paired_steps(pool, TT, step)

        @block.vector
        def _(dve):
            def x_norm(t, s):
                at_least(dve, x_rstd, t + 1)
                at_least(dve, transposed, t - 1)
                nc.vector.tensor_scalar(xn[s][:, :], x_of(t), small[:, s, 22:23], small[:, s, 25:26],
                                        ALU.subtract, ALU.mult).then_inc(xn_ready, 1)

            def x_low(t, s):
                at_least(dve, x_hi, t + 1)
                nc.vector.tensor_tensor(M.xl[:, :, cols(t, P)], ps_t[s].rearrange("p (c q) -> p c q", c=KM),
                                        f32(M.xh[:, :, cols(t, P)]), ALU.subtract).then_inc(x_lo, 1)

            def step(t, s):
                if not norm_only:
                    if proj:
                        at_least(dve, y_ready, t + 1)
                    y = y_of(t, s)
                    if out_scale is not None:
                        at_least(dve, y_normed, t)
                        nc.vector.tensor_tensor(y, ps_y[s], out_scale[:, :], ALU.mult).then_inc(scaled, 1)
                        at_least(dve, scaled, t + 1)
                    nc.vector.bn_stats(small[:, s, 0:6], y).then_inc(y_stats, 1)
                    at_least(dve, y_stats, t + 1)
                    nc.vector.bn_aggr(small[:, s, 6:8], small[:, s, 0:6]).then_inc(y_moments, 1)
                    at_least(dve, y_moments, t + 1)
                    nc.vector.tensor_scalar(small[:, s, 8:9], small[:, s, 7:8], LN_EPS, None, ALU.add).then_inc(y_var, 1)
                if not store and exists(t - 1, TT):
                    x_norm(t - 1, 1 - s)
                if not norm_only:
                    at_least(dve, y_rstd, t + 1)
                    at_least(dve, x_new, t)
                    nc.vector.tensor_scalar(tmp[:, :], y, small[:, s, 6:7], small[:, s, 9:10],
                                            ALU.subtract, ALU.mult).then_inc(y_normed, 1)
                    at_least(dve, y_normed, t + 1)
                    nc.vector.tensor_tensor(x_of(t), x_of(t), tmp[:, :], ALU.add).then_inc(x_new, 1)
                    if not store:
                        at_least(dve, x_new, t + 1)
                if not store:
                    nc.vector.bn_stats(small[:, s, 16:22], x_of(t)).then_inc(x_stats, 1)
                    at_least(dve, x_stats, t + 1)
                    if norm_only:
                        at_least(dve, xn_ready, t - 1)
                    nc.vector.bn_aggr(small[:, s, 22:24], small[:, s, 16:22]).then_inc(x_moments, 1)
                    at_least(dve, x_moments, t + 1)
                    nc.vector.tensor_scalar(small[:, s, 24:25], small[:, s, 23:24], LN_EPS, None, ALU.add).then_inc(x_var, 1)
                    if exists(t - 1, TT):
                        x_low(t - 1, 1 - s)

            if proj:
                for k in range(K):
                    dve.wait_ge(split_w, k + 1)
                    nc.vector.tensor_tensor(wl[:, k, :], w_raw[:, k, :], f32(wh[:, k, :]), ALU.subtract).then_inc(split_wl, 1)
            paired_steps(dve, TT, step)
            if not store:
                x_norm(TT - 1, (TT - 1) % 2)
                x_low(TT - 1, (TT - 1) % 2)

        if store:
            @block.sync
            def _(sp):
                for t in range(TT):
                    sp.wait_ge(x_new, t + 1)
                    sp.dma_start(last_out[t * P:(t + 1) * P, :], M.x[:, t, :]).then_inc(stored, 16)
                sp.wait_ge(stored, 16 * TT)
    signals.close()


def widen_phase(nc, tag, M, place, F, kind, raw_dram, base_dram=None, hidden=None,
                x_conv=None, gate=None, scales=None, coeff=None, second=None, diff=None):
    signals = Signals(nc)
    sem = lambda n: signals(f"{tag}_{n}")
    raw_in, down_in = [sem("raw_in0"), sem("raw_in1")], sem("down_in")
    w_diff, w_sign, w_full, w_hi, w_lo = (sem("w_diff"), sem("w_sign"), sem("w_full"),
                                                  sem("w_hi"), sem("w_lo"))
    prod, first_done, second_done = sem("products"), sem("first_done"), sem("second_done")
    tap = sem("tap")
    d_in, d_sub, d_abs = [sem("diff_in0"), sem("diff_in1")], sem("diff_sub"), sem("diff_abs")
    WC = 2 * KM * P
    RC = WC + DM if kind == "diff" else WC
    raw = [place(f"raw{i}", [P, RC], I32 if kind == "int" else F32) for i in range(2)]
    wh = [place(f"wh{i}", [P, 2, KM, P], F32R) for i in range(2)]
    wl = [place(f"wl{i}", [P, 2, KM, P], F32R) for i in range(2)]
    mid = [place(f"mid{i}", [P, TOK]) for i in range(2 if kind != "diff" else 1)]
    if kind == "diff":
        base = [place(f"base{i}", [P, RC]) for i in range(2)]
        full = [place(f"full{i}", [P, RC]) for i in range(2)]
    if diff is not None:
        DC = DIFF_COLS // N_SUMS
        dw = [place(f"dw{i}", [P, 3, DC]) for i in range(2)]
        dm = [place(f"dm{i}", [P, 3, DC]) for i in range(2)]
        tail = F - N_SUMS + 1
    else:
        tail = 0
    flat = lambda t: t[:, :, :, :].rearrange("p a k o -> p (a k o)")
    ps = [[M.ps[:, 4 * s + 2 * a:4 * s + 2 * a + 2, :].rearrange("p a c -> p (a c)") for a in range(2)] for s in range(2)]

    with nc.Block() as block:
        @block.sync
        def _(sp):
            def step(f, s):
                at_least(sp, w_lo, f - 1)
                if kind == "diff":
                    at_least(sp, w_full, f - 1)
                sp.dma_start(raw[s][:, :], raw_dram[:, cols(f, RC)]).then_inc(raw_in[s], 16)
                if kind == "diff":
                    sp.dma_start(base[s][:, :], base_dram[:, cols(f, RC)]).then_inc(raw_in[s], 16)
                if diff is not None and exists(f, N_SUMS):
                    at_least(sp, d_abs, f * 3 - 3)
                    for a, (w, m) in enumerate(diff["pairs"]):
                        sp.dma_start(dw[s][:, a, :], w[:, cols(f, DC)]).then_inc(d_in[s], 16)
                        sp.dma_start(dm[s][:, a, :], m[:, cols(f, DC)]).then_inc(d_in[s], 16)

            if second is not None and kind == "int":
                sp.dma_start(second[0][:, :, :], second[1]).then_inc(down_in, 16)
            paired_steps(sp, F, step, tail=tail)
            if second is not None and kind == "int":
                sp.wait_ge(down_in, 16)
            if diff is not None:
                sp.wait_ge(d_abs, 3 * N_SUMS)

        @block.tensor
        def _(pe):
            def step(f, s):
                at_least(pe, w_hi, f + 1)
                at_least(pe, w_lo, f + 1)
                at_least(pe, first_done, f - 1)
                at_least(pe, second_done, f - 1)
                for a in range(2):
                    for k in range(KM):
                        for w, x in ((wh, M.xh), (wh, M.xl), (wl, M.xh)):
                            for h in range(2):
                                mm = nc.tensor.matmul(ps[s][a][:, h * HALF:(h + 1) * HALF], w[s][:, a, k, :],
                                                      x[:, k, h * HALF:(h + 1) * HALF],
                                                      start=(k == 0 and w is wh and x is M.xh),
                                                      stop=(k == KM - 1 and w is wl))
                    mm.then_inc(prod, 1)

            paired_steps(pe, F, step)

        @block.scalar
        def _(act):
            def prepare(f, s):
                if kind == "diff":
                    at_least(act, w_diff, f + 1)
                    nc.scalar.activation(full[s][:, :], full[s][:, :], ACT.Sign).then_inc(w_sign, 1)
                    at_least(act, w_full, f + 1)
                    src = full[s][:, 0:WC]
                else:
                    at_least(act, raw_in[s], (f - s) * 8 + 16)
                    src = raw[s][:, 0:WC]
                at_least(act, prod, 2 * (f - 1))
                nc.scalar.activation(flat(wh[s]), src, ACT.Copy).then_inc(w_hi, 1)

            def differences(f, s):
                for a in range(3):
                    at_least(act, d_sub, 3 * f + a + 1)
                    nc.scalar.activation(dw[s][:, a, :], dw[s][:, a, :], ACT.Abs,
                                         accum_out=diff["sums"][:, a, bass.ds(f, 1)]).then_inc(d_abs, 1)

            def step(f, s):
                if exists(f + 1, F):
                    prepare(f + 1, 1 - s)
                if diff is not None and exists(f, N_SUMS):
                    differences(f, s)
                if kind == "ssm":
                    at_least(act, prod, 2 * f + 1)
                    at_least(act, first_done, f - 1)
                    nc.scalar.activation(mid[s][:, :], ps[s][0], ACT.Identity, bias=M.vec[:, bass.ds(f + V_CB, 1)],
                                         scale=M.vec[:, bass.ds(f * K_CONV + V_CW + K_CONV - 1, 1)]).then_inc(tap, 1)
                    at_least(act, prod, 2 * f + 2)
                    nc.scalar.activation(gate[:, :, cols(f, SEQ)], by_batch(ps[s][1]),
                                         ACT.Silu).then_inc(second_done, 1)
                    at_least(act, tap, 4 * f + 4)
                    nc.scalar.activation(x_conv[:, :, cols(f, SEQ)], by_batch(mid[s][:, :]),
                                         ACT.Silu).then_inc(first_done, 1)
                else:
                    m = mid[s % len(mid)]
                    at_least(act, prod, 2 * f + 1)
                    at_least(act, second_done, f - len(mid) + 1)
                    sc = scales[0][:, bass.ds(f, 1)] if kind == "int" else 1.0
                    nc.scalar.activation(m[:, :], ps[s][0], ACT.Silu, scale=sc).then_inc(first_done, 1)

            prepare(0, 0)
            paired_steps(act, F, step, tail=tail)

        @block.gpsimd
        def _(pool):
            def lows(f, s):
                if kind == "diff":
                    at_least(pool, w_full, f + 1)
                at_least(pool, w_hi, f + 1)
                src = full[s][:, 0:WC] if kind == "diff" else raw[s][:, 0:WC]
                nc.gpsimd.tensor_tensor(flat(wl[s]), src, f32(flat(wh[s])), ALU.subtract).then_inc(w_lo, 1)

            def difference(f, s):
                at_least(pool, raw_in[s], (f - s) * 16 + 32)
                at_least(pool, w_lo, f - 1)
                nc.gpsimd.tensor_tensor(full[s][:, :], raw[s][:, :], base[s][:, :], ALU.subtract).then_inc(w_diff, 1)

            def step(f, s):
                if kind == "diff":
                    if exists(f + 1, F):
                        difference(f + 1, 1 - s)
                if kind != "int":
                    lows(f, s)
                if diff is not None and exists(f, N_SUMS):
                    at_least(pool, d_in[s], (f - s) * 48 + 96)
                    for a in range(3):
                        nc.gpsimd.tensor_tensor(dw[s][:, a, :], dw[s][:, a, :], dm[s][:, a, :], ALU.subtract).then_inc(d_sub, 1)

            if kind == "diff":
                difference(0, 0)
            if kind != "int" or diff is not None:
                paired_steps(pool, F, step, tail=tail)

        @block.vector
        def _(dve):
            def int_lows(f, s):
                at_least(dve, w_hi, f + 1)
                nc.vector.tensor_tensor(flat(wl[s]), raw[s][:, :], f32(flat(wh[s])), ALU.subtract).then_inc(w_lo, 1)

            def whole(f, s):
                at_least(dve, w_sign, f + 1)
                for a, lo, hi in ((0, 0, WC // 2), (1, WC // 2, WC), (2, WC, RC)):
                    src = full[s][:, lo:hi]
                    dst = second[0][:, bass.ds(f, 1), :].rearrange("p a c -> p (a c)") if a == 2 else src
                    ins = nc.vector.scalar_tensor_tensor(dst, src, coeff[:, a:a + 1], base[s][:, lo:hi], ALU.mult, ALU.add)
                ins.then_inc(w_full, 1)

            def step(f, s):
                if kind == "int" and exists(f + 1, F):
                    int_lows(f + 1, 1 - s)
                if kind == "diff" and exists(f + 1, F):
                    whole(f + 1, 1 - s)
                if kind == "ssm":
                    m = mid[s][:, :].rearrange("p (b t) -> p b t", b=BATCH)
                    src = ps[s][0].rearrange("p (b t) -> p b t", b=BATCH)
                    for j in range(1, K_CONV):
                        at_least(dve, tap, 4 * f + j)
                        nc.vector.scalar_tensor_tensor(m[:, :, j:SEQ], src[:, :, 0:SEQ - j],
                                                       M.vec[:, bass.ds(f * K_CONV + V_CW + K_CONV - 1 - j, 1)],
                                                       m[:, :, j:SEQ], ALU.mult, ALU.add).then_inc(tap, 1)
                else:
                    at_least(dve, prod, 2 * f + 2)
                    at_least(dve, first_done, f + 1)
                    sc = scales[1][:, bass.ds(f, 1)] if kind == "int" else 1.0
                    nc.vector.scalar_tensor_tensor(hidden[:, bass.ds(f, 1), :].rearrange("p a c -> p (a c)"), ps[s][1],
                                                   sc, mid[s % len(mid)][:, :], ALU.mult, ALU.mult).then_inc(second_done, 1)

            if kind == "diff":
                whole(0, 0)
            if kind == "int":
                int_lows(0, 0)
            paired_steps(dve, F, step)
            if kind != "ssm":
                dve.wait_ge(second_done, F)
    signals.close()


def ssm_parameters(nc, M, place, x_conv, dt, bc_dram, wx_dram, wdt_dram, block_mean_dram):
    signals = Signals(nc)
    sem = lambda n: signals(f"par_{n}")
    loaded, raw_ready, squared, mean_ready, eps_added, rooted, inverse, normed = (
        sem("loaded"), sem("raw_ready"), sem("squared"), sem("mean_ready"), sem("eps_added"), sem("rooted"),
        sem("inverse"), sem("normed"))
    kept, stored = sem("kept"), sem("bc_stored")
    pre, magnitude, exped, logged, positive, dt_done = (sem("pre"), sem("magnitude"), sem("exped"), sem("logged"),
                                                        sem("positive"), sem("dt_done"))
    wx = place("wx", [P, KI, NX])
    wdt = place("wdt", [RANK, D_IN])
    block_mean = place("block_mean", [NX, NX])
    raw = place("raw", [NX, TOK])
    sq = place("sq", [NX, TOK])
    ssm = place("ssm", [NX, TOK])
    log1p = M.scratch32
    ps_x = M.ps[0:NX, 0:2, :].rearrange("p a c -> p (a c)")
    ps_m = M.ps[0:NX, 2:4, :].rearrange("p a c -> p (a c)")
    ps_dt = [M.ps[:, 4 + 2 * s:6 + 2 * s, :].rearrange("p a c -> p (a c)") for s in range(2)]
    with nc.Block() as block:
        @block.sync
        def _(sp):
            sp.dma_start(wx[:, :, :], wx_dram).then_inc(loaded, 16)
            sp.dma_start(wdt[:, :], wdt_dram).then_inc(loaded, 16)
            sp.dma_start(block_mean[:, :], block_mean_dram).then_inc(loaded, 16)
            sp.wait_ge(normed, 1)
            for b in range(BATCH):
                sp.dma_start(bc_dram[b, :, :], ssm[RANK:NX, b * SEQ:(b + 1) * SEQ]).then_inc(stored, 16)
            sp.wait_ge(stored, 16 * BATCH)

        @block.tensor
        def _(pe):
            pe.wait_ge(loaded, 48)
            for h in range(2):
                for k in range(KI):
                    mm = nc.tensor.matmul(ps_x[:, h * HALF:(h + 1) * HALF], wx[:, k, :],
                                          x_conv[:, 2 * h:2 * h + 2, k * SEQ:(k + 1) * SEQ],
                                          start=(k == 0), stop=(k == KI - 1))
                mm.then_inc(raw_ready, 1)
            pe.wait_ge(squared, 1)
            for h in range(2):
                mm = nc.tensor.matmul(ps_m[:, h * HALF:(h + 1) * HALF], block_mean[:, :],
                                      sq[:, h * HALF:(h + 1) * HALF], start=True, stop=True)
            mm.then_inc(mean_ready, 1)
            pe.wait_ge(normed, 1)
            for f in range(KI):
                at_least(pe, magnitude, f - 1)
                at_least(pe, positive, f - 1)
                for h in range(2):
                    mm = nc.tensor.matmul(ps_dt[f % 2][:, h * HALF:(h + 1) * HALF], wdt[:, f * P:(f + 1) * P],
                                          ssm[0:RANK, h * HALF:(h + 1) * HALF], start=True, stop=True)
                mm.then_inc(pre, 1)

        @block.scalar
        def _(act):
            act.wait_ge(raw_ready, 2)
            nc.scalar.activation(raw[:, :], ps_x, ACT.Copy).then_inc(kept, 1)
            nc.scalar.activation(sq[:, :], ps_x, ACT.Square).then_inc(squared, 1)
            act.wait_ge(eps_added, 1)
            nc.scalar.activation(sq[:, :], sq[:, :], ACT.Sqrt).then_inc(rooted, 1)
            for f in range(KI):
                act.wait_ge(pre, f + 1)
                nc.scalar.activation(log1p[:, f * TOK:(f + 1) * TOK], ps_dt[f % 2], ACT.Abs,
                                     bias=M.vec[:, V_BDT + f:V_BDT + f + 1]).then_inc(magnitude, 1)
                act.wait_ge(magnitude, f + 1)
                nc.scalar.activation(log1p[:, f * TOK:(f + 1) * TOK], log1p[:, f * TOK:(f + 1) * TOK],
                                     ACT.Exp, scale=-1.0).then_inc(exped, 1)
            for f in range(KI):
                act.wait_ge(exped, f + 1)
                nc.scalar.activation(log1p[:, f * TOK:(f + 1) * TOK], log1p[:, f * TOK:(f + 1) * TOK],
                                     ACT.Ln, bias=1.0).then_inc(logged, 1)
            nc.scalar.activation(M.vec[:, V_AL:V_D], M.vec[:, V_AL:V_D], ACT.Exp).then_inc(kept, 1)

        @block.vector
        def _(dve):
            dve.wait_ge(mean_ready, 1)
            dve.wait_ge(squared, 1)
            nc.vector.tensor_scalar(sq[:, :], ps_m, RMS_EPS, None, ALU.add).then_inc(eps_added, 1)
            dve.wait_ge(rooted, 1)
            nc.vector.reciprocal(sq[:, :], sq[:, :]).then_inc(inverse, 1)
            dve.wait_ge(inverse, 1)
            dve.wait_ge(kept, 1)
            nc.vector.tensor_tensor(ssm[:, :], raw[:, :], sq[:, :], ALU.mult).then_inc(normed, 1)
            for f in range(KI):
                dve.wait_ge(magnitude, f + 1)
                bias = M.vec[:, V_BDT + f:V_BDT + f + 1]
                nc.vector.tensor_scalar(dt[:, :, f * SEQ:(f + 1) * SEQ], by_batch(ps_dt[f % 2]), bias, 0.0,
                                        ALU.add, ALU.max).then_inc(positive, 1)
            for f in range(KI):
                dve.wait_ge(logged, f + 1)
                dve.wait_ge(positive, f + 1)
                part = dt[:, :, f * SEQ:(f + 1) * SEQ]
                nc.vector.tensor_tensor(part, part, by_batch(log1p[:, f * TOK:(f + 1) * TOK]), ALU.add).then_inc(dt_done, 1)
            dve.wait_ge(kept, 2)
            nc.vector.tensor_scalar(M.vec[:, V_AL:V_D], M.vec[:, V_AL:V_D], -1.0, None, ALU.mult).then_inc(dt_done, 1)
    signals.close()


def scan_phase(nc, M, place, x_conv, dt, bc_dram, w_next, w_next_dram):
    signals = Signals(nc)
    sem = lambda n: signals(f"scan_{n}")
    NH, PIECES = N_ST // 2, 8
    NP = N_ST // PIECES
    W = NH * SEQ
    SLOTS = 4
    w_in = sem("next_weight_in")
    b_in, c_in = [sem("b_in0"), sem("b_in1")], [sem("c_in0"), sem("c_in1")]
    heads_zero, inflow_in, decayed, u_ready = sem("heads_zero"), sem("inflow"), sem("decayed"), sem("u_ready")
    scanned, weighted, slots_free, finished = sem("scanned"), sem("weighted"), sem("slots_free"), sem("finished")
    bm = place("bm", [P, N_ST, SEQ])
    cm = place("cm", [P, N_ST, SEQ])
    u = [place(f"u{i}", [P, SEQ]) for i in range(2)]
    slot = [M.scratch32[:, i * W:(i + 1) * W] for i in range(SLOTS)]
    decay = [M.ps[:, 2 + i, :] for i in range(2)]
    by_state = lambda ap: ap.rearrange("p (n t) -> p n t", n=NP)
    state = [M.ps[:, 4 + i, :] for i in range(4)]
    ident = M.const[:, C_ID:C_ID + P]
    ps_y = [M.ps[:, i, 0:SEQ] for i in range(2)]
    flat_x = x_conv[:, :, :].rearrange("p b c -> p (b c)")
    flat_dt = dt[:, :, :].rearrange("p b c -> p (b c)")

    def pairs(eng, body):
        body(0, 0)
        with eng.Fori(1, KI // 2) as j:
            body(0, j)
        with eng.Fori(1, BATCH) as b:
            with eng.Fori(0, KI // 2) as j:
                body(b, j)

    with nc.Block() as block:
        @block.sync
        def _(sp):
            def load(b):
                for h in range(2):
                    at_least(sp, inflow_in, b * 2 * KI - 1 + h)
                    sp.dma_start(bm[:, h * NH:(h + 1) * NH, :],
                                 bc_dram[bass.ds(b, 1), h * NH:(h + 1) * NH, :].broadcast_to((P, NH, SEQ))).then_inc(b_in[h], 16)
                for h in range(2):
                    at_least(sp, weighted, b * PIECES * KI - 4 + 4 * h)
                    sp.dma_start(cm[:, h * NH:(h + 1) * NH, :],
                                 bc_dram[bass.ds(b, 1), N_ST + h * NH:N_ST + (h + 1) * NH, :].broadcast_to((P, NH, SEQ))).then_inc(c_in[h], 16)
            load(0)
            sp.dma_start(w_next[:, :, :], w_next_dram).then_inc(w_in, 16)
            with sp.Fori(1, BATCH) as b:
                load(b)
            sp.wait_ge(w_in, 16)

        @block.gpsimd
        def _(pool):
            pool.sem_inc(slots_free, SLOTS)

            def body(b, j):
                for r in range(2):
                    s = b * KI + j * 2 + r
                    at_least(pool, inflow_in, s * 2 - 2)
                    nc.gpsimd.tensor_tensor(u[r][:, :], flat_dt[:, cols(s, SEQ)], flat_x[:, cols(s, SEQ)],
                                            ALU.mult).then_inc(u_ready, 1)
                    pool.wait_ge(u_ready, s + 1)
                    for h in range(2):
                        pool.wait_ge(b_in[h], b * 16 + 16)
                        pool.wait_ge(slots_free, s * 2 + h + 1)
                        nc.gpsimd.tensor_tensor(slot[2 * r + h].rearrange("p (n t) -> p n t", n=NH),
                                                bm[:, h * NH:(h + 1) * NH, :],
                                                u[r][:, :].rearrange("p (a t) -> p a t", a=1).broadcast_to((P, NH, SEQ)),
                                                ALU.mult).then_inc(inflow_in, 1)
            pairs(pool, body)

        @block.scalar
        def _(act):
            act.wait_ge(heads_zero, 2)

            def body(b, j):
                for r in range(2):
                    s = b * KI + j * 2 + r
                    for c in range(PIECES):
                        at_least(act, scanned, s * PIECES + c - 1)
                        for n in range(NP):
                            ins = nc.scalar.activation(by_state(decay[c % 2])[:, n, 1:SEQ], flat_dt[:, bass.ds(s * SEQ + 1, SEQ - 1)], ACT.Exp,
                                                       scale=M.vec[:, bass.ds(s * N_ST + V_AL + c * NP + n, 1)])
                        ins.then_inc(decayed, 1)
            pairs(act, body)

        @block.vector
        def _(dve):
            def part(r, c):
                return slot[2 * r + c // 4][:, (c % 4) * NP * SEQ:(c % 4 + 1) * NP * SEQ]

            def weigh(b, s, r, c):
                dve.wait_ge(scanned, s * PIECES + c + 1)
                if c % 4 == 0:
                    dve.wait_ge(c_in[c // 4], b * 16 + 16)
                nc.vector.tensor_tensor(part(r, c), state[c % 4], cm[:, c * NP:(c + 1) * NP, :].rearrange("p n t -> p (n t)"),
                                        ALU.mult).then_inc(weighted, 1)

            def finish(s, r):
                dve.wait_ge(slots_free, s * 2 + 2 + SLOTS)
                nc.vector.scalar_tensor_tensor(flat_x[:, cols(s, SEQ)], flat_x[:, cols(s, SEQ)],
                                               M.vec[:, bass.ds(s + V_D, 1)], ps_y[r], ALU.mult, ALU.add).then_inc(finished, 1)

            def body(b, j):
                for r in range(2):
                    s = b * KI + j * 2 + r
                    for c in range(PIECES):
                        dve.wait_ge(decayed, s * PIECES + c + 1)
                        if c % 4 == 0:
                            dve.wait_ge(inflow_in, s * 2 + c // 4 + 1)
                        at_least(dve, weighted, s * PIECES + c - 3)
                        nc.vector.tensor_tensor_scan(state[c % 4], decay[c % 2], part(r, c), 0.0, ALU.mult, ALU.add).then_inc(scanned, 1)
                        if c > 0:
                            weigh(b, s, r, c - 1)
                        elif r > 0:
                            weigh(b, s - 1, 1 - r, PIECES - 1)
                        elif not (isinstance(s, int) and s == 0):
                            weigh(None, s - 1, 1 - r, PIECES - 1)
                        if c == 2 and not (isinstance(s, int) and s == 0):
                            finish(s - 1, 1 - r)
            for d in decay:
                nc.vector.memset(by_state(d)[:, :, 0:1], 0.0).then_inc(heads_zero, 1)
            dve.wait_ge(heads_zero, 2)
            pairs(dve, body)
            weigh(None, BATCH * KI - 1, 1, PIECES - 1)
            finish(BATCH * KI - 1, 1)

        @block.tensor
        def _(pe):
            def body(b, j):
                for r in range(2):
                    s = b * KI + j * 2 + r
                    at_least(pe, finished, s - 1)
                    for h in range(2):
                        for n in range(NH):
                            if n % NP == 0:
                                pe.wait_ge(weighted, s * PIECES + 4 * h + n // NP + 1)
                            mm = nc.tensor.matmul(ps_y[r], ident, slot[2 * r + h][:, n * SEQ:(n + 1) * SEQ],
                                                  start=(h == 0 and n == 0), stop=(h == 1 and n == NH - 1))
                        mm.then_inc(slots_free, 1)
            pairs(pe, body)
    signals.close()


def key_value_phase(nc, M, place, spare, K, V, ch, cl, w_kv, w_v, wq_raw, wq):
    signals = Signals(nc)
    sem = lambda n: signals(f"kv_{n}")
    R = ROPE_HALF
    NF, VC = 3 * KM, GROUPS * HD
    BUFS = 4
    kinds = ["latent"] * KM + ["rotated", "plain"] * KM
    items = [("step", f) for f in range(NF)]
    for k in range(KM):
        items.insert(6 + 3 * k, ("values", k))
    RING = 3
    raw_in, q_in = [sem(f"raw_in{i}") for i in range(RING)], sem("query_weights_in")
    w_hi, w_lo, prod = sem("w_hi"), sem("w_lo"), sem("products")
    plain_act, plain_dve, v_kept = sem("plain_kept_act"), sem("plain_kept_dve"), sem("values_kept")
    c_hi, c_lo = sem("c_hi"), sem("c_lo")
    turned_done, sine_done, cosine_done, rotated = sem("turned"), sem("sine"), sem("cosine"), sem("rotated")
    raw = [place(f"raw{i}", [P, VC]) for i in range(RING)]
    vwh, vwl = place("vwh", [P, KM, VC], F32R), place("vwl", [P, KM, VC], F32R)
    wh = [place(f"wh{i}", [P, KM * P], F32R) for i in range(RING)]
    wl = [place(f"wl{i}", [P, KM * P], F32R) for i in range(RING)]
    turned = [spare(f"turned{i}", [P, TOK]) for i in range(2)]
    direct = [spare(f"direct{i}", [P, TOK]) for i in range(2)]
    table = lambda c: M.const[:, c:c + SEQ].rearrange("p (b t) -> p b t", b=1).broadcast_to((P, BATCH, SEQ))
    ps = [M.ps[:, 2 * s:2 * s + 2, :].rearrange("p a c -> p (a c)") for s in range(BUFS)]
    item_of = {it: n for n, it in enumerate(items)}

    def weight(it):
        kind, i = items[it]
        if kind == "step":
            return raw[it % RING][:, 0:KM * P], wh[i % RING][:, :], wl[i % RING][:, :]
        return raw[it % RING][:, :], vwh[:, i, :], vwl[:, i, :]

    with nc.Block() as block:
        @block.sync
        def _(sp):
            for it, (kind, i) in enumerate(items):
                at_least(sp, w_lo, it - RING + 1)
                src, dst = (w_kv[:, i * KM * P:(i + 1) * KM * P], raw[it % RING][:, 0:KM * P]) if kind == "step" else (w_v[:, i, :], raw[it % RING][:, :])
                sp.dma_start(dst, src).then_inc(raw_in[it % RING], 16)
            sp.wait_ge(w_lo, len(items))
            sp.dma_start(wq_raw[:, :], wq[:, 0:KM * HPG * HD]).then_inc(q_in, 16)
            sp.wait_ge(q_in, 16)

        @block.tensor
        def _(pe):
            def psum_free(f):
                g = f - BUFS
                if g < 0:
                    return
                if g >= NF:
                    pe.wait_ge(v_kept, g - NF + 1)
                elif kinds[g] == "latent":
                    pe.wait_ge(c_lo, g + 1)
                elif kinds[g] == "rotated":
                    pe.wait_ge(cosine_done, (g - KM) // 2 + 1)
                else:
                    pe.wait_ge(plain_act, (g - KM) // 2 + 1)
                    pe.wait_ge(plain_dve, (g - KM) // 2 + 1)

            for f in range(NF):
                it = item_of[("step", f)]
                pe.wait_ge(w_hi, it + 1)
                pe.wait_ge(w_lo, it + 1)
                psum_free(f)
                if kinds[f] == "plain":
                    pe.wait_ge(c_lo, KM)
                xh, xl = (ch, cl) if kinds[f] == "plain" else (M.xh, M.xl)
                for k in range(KM):
                    for w, x in ((wh, xh), (wh, xl), (wl, xh)):
                        for h in range(2):
                            mm = nc.tensor.matmul(ps[f % BUFS][:, h * HALF:(h + 1) * HALF], w[f % RING][:, k * P:(k + 1) * P],
                                                  x[:, k, h * HALF:(h + 1) * HALF],
                                                  start=(k == 0 and w is wh and x is xh), stop=(k == KM - 1 and w is wl))
                mm.then_inc(prod, 1)
            pe.wait_ge(w_lo, len(items))
            for t in range(TT):
                f = NF + t
                psum_free(f)
                for k in range(KM):
                    for c, w in ((ch, vwh), (ch, vwl), (cl, vwh)):
                        for h in range(2):
                            mm = nc.tensor.matmul(ps[f % BUFS][:, h * HALF:(h + 1) * HALF], c[:, k, t * P:(t + 1) * P],
                                                  w[:, k, h * HALF:(h + 1) * HALF],
                                                  start=(k == 0 and w is vwh and c is ch), stop=(k == KM - 1 and c is cl))
                mm.then_inc(prod, 1)

        @block.scalar
        def _(act):
            def high(it):
                kind, i = items[it]
                act.wait_ge(raw_in[it % RING], (it // RING + 1) * 16)
                if kind == "step":
                    at_least(act, prod, i - RING + 1)
                src, hi, _ = weight(it)
                nc.scalar.activation(hi, src, ACT.Copy).then_inc(w_hi, 1)

            def evacuate(f):
                act.wait_ge(prod, f + 1)
                src = ps[f % BUFS]
                if f >= NF:
                    if f == NF + TT // 2:
                        act.wait_ge(rotated, 4 * KM)
                    nc.scalar.activation(V[:, f - NF, :], src, ACT.Copy).then_inc(v_kept, 1)
                elif kinds[f] == "latent":
                    nc.scalar.activation(ch[:, f, :], src, ACT.Copy).then_inc(c_hi, 1)
                elif kinds[f] == "rotated":
                    j = (f - KM) // 2
                    at_least(act, rotated, 4 * (j - 1))
                    for q in range(4):
                        o = (q ^ 1) * R
                        nc.scalar.activation(turned[j % 2][q * R:(q + 1) * R, :], src[o:o + R, :], ACT.Copy).then_inc(turned_done, 1)
                else:
                    j = (f - KM) // 2
                    nc.scalar.activation(K[R:2 * R, 2 * j, :], src[0:R, :], ACT.Copy)
                    nc.scalar.activation(K[3 * R:4 * R, 2 * j, :], src[R:2 * R, :], ACT.Copy).then_inc(plain_act, 1)

            done = 0
            for f in range(NF + TT):
                while done < len(items) and (done <= (item_of[("step", f + 1)] if f + 1 < NF else len(items) - 1)):
                    high(done)
                    done += 1
                evacuate(f)

        @block.gpsimd
        def _(pool):
            def low(it):
                pool.wait_ge(w_hi, it + 1)
                src, hi, lo = weight(it)
                nc.gpsimd.tensor_tensor(lo, src, f32(hi), ALU.subtract).then_inc(w_lo, 1)

            done = 0
            for f in range(NF):
                while done < len(items) and (done <= (item_of[("step", f + 1)] if f + 1 < NF else len(items) - 1)):
                    low(done)
                    done += 1
                if kinds[f] == "rotated":
                    j = (f - KM) // 2
                    pool.wait_ge(turned_done, 4 * j + 4)
                    nc.gpsimd.tensor_tensor(by_batch(turned[j % 2][:, :]), by_batch(turned[j % 2][:, :]), table(C_SINK),
                                            ALU.mult).then_inc(sine_done, 1)

        @block.vector
        def _(dve):
            def add_turned(j):
                dve.wait_ge(cosine_done, j + 1)
                dve.wait_ge(sine_done, j + 1)
                for q in range(4):
                    rows, to = slice(q * R, (q + 1) * R), (q % 2) * 2 * R
                    nc.vector.tensor_tensor(K[to:to + R, 2 * j + q // 2, :], direct[j % 2][rows, :], turned[j % 2][rows, :],
                                            ALU.add).then_inc(rotated, 1)

            for f in range(NF):
                src = ps[f % BUFS]
                if kinds[f] == "latent":
                    dve.wait_ge(c_hi, f + 1)
                    nc.vector.tensor_tensor(cl[:, f, :], src, f32(ch[:, f, :]), ALU.subtract).then_inc(c_lo, 1)
                elif kinds[f] == "rotated":
                    j = (f - KM) // 2
                    dve.wait_ge(turned_done, 4 * j + 4)
                    at_least(dve, rotated, 4 * (j - 1))
                    nc.vector.tensor_tensor(by_batch(direct[j % 2][:, :]), by_batch(src), table(C_COSK), ALU.mult).then_inc(cosine_done, 1)
                else:
                    j = (f - KM) // 2
                    dve.wait_ge(prod, f + 1)
                    nc.vector.tensor_copy(K[R:2 * R, 2 * j + 1, :], src[2 * R:3 * R, :])
                    nc.vector.tensor_copy(K[3 * R:4 * R, 2 * j + 1, :], src[3 * R:4 * R, :]).then_inc(plain_dve, 1)
                    add_turned(j)
            dve.wait_ge(rotated, 4 * KM)
    signals.close()


def attention_phase(nc, M, place, raw, K, V, acc, wq, wo):
    signals = Signals(nc)
    sem = lambda n: signals(f"att_{n}")
    U = GROUPS * BATCH
    SCALE = float(HD) ** -0.5
    raw_in, wq_hi, wq_lo, wo_hi, wo_lo = sem("raw_in"), sem("wq_hi"), sem("wq_lo"), sem("wo_hi"), sem("wo_lo")
    q_prod, q_turned, q_sine, q_cosine, q_done = (sem("q_prod"), sem("q_turned"), sem("q_sine"), sem("q_cosine"), sem("q_done"))
    scored, masked, maxed, neg_max, exped, inverse, normed = (sem("scored"), sem("masked"), sem("maxed"), sem("neg_max"),
                                                              sem("exped"), sem("inverse"), sem("normed"))
    flipped, p_kept_act, p_kept_dve, v_here, summed, o_hi, o_lo, o_prod, added = (
        sem("flipped"), sem("p_kept_act"), sem("p_kept_dve"), sem("v_here"), sem("summed"), sem("o_hi"), sem("o_lo"),
        sem("o_prod"), sem("added"))
    zeroed = sem("acc_zeroed")
    QC = HPG * HD
    wqh, wql = place("wqh", [P, KM, QC], F32R), place("wql", [P, KM, QC], F32R)
    woh, wol = place("woh", [P, HPG, DM], F32R), place("wol", [P, HPG, DM], F32R)
    q = place("q", [P, HPG, SEQ])
    direct, turned = place("direct", [P, HPG * SEQ]), place("turned", [P, HPG * SEQ])
    pa, pb = place("pa", [P, HPG, P]), place("pb", [P, HPG, SEQ])
    pt = place("pt", [P, 3, HALF])
    vs = place("vs", [P, QT, HD])
    oh, ol = place("oh", [P, QT, HALF], F32R), place("ol", [P, QT, HALF], F32R)
    mx, nm, sums, inv = (place(n, [P, 8]) for n in ("mx", "nm", "sums", "inv"))
    ident = M.const[:, C_ID:C_ID + P]
    ps_q = M.ps[:, 0:2, :].rearrange("p a c -> p (a c)")
    s0 = M.ps[:, 2, :].rearrange("p (h k) -> p h k", h=HPG)
    s1 = M.ps[:, 3:5, :].rearrange("p a (h k) -> p (a h) k", k=SEQ)
    X = [M.ps[:, 5 + i, :] for i in range(3)]
    flat = lambda t: t[:, :, :].rearrange("p a c -> p (a c)")
    heads = lambda ap: ap.rearrange("p (h t) -> p h t", h=HPG)
    over_heads = lambda c, w: M.const[:, c:c + w].rearrange("p (h t) -> p h t", h=1).broadcast_to((P, HPG, w))

    def groups(eng, body):
        for b in range(BATCH):
            body(0, b)
        with eng.Fori(1, GROUPS - 1) as g:
            for b in range(BATCH):
                body(g, b)
        for b in range(BATCH):
            body(GROUPS - 1, b)

    def more(g, b):
        return not (isinstance(g, int) and g == GROUPS - 1 and b == BATCH - 1)

    def after(g, b):
        return (g, b + 1) if b < BATCH - 1 else (g + 1, 0)

    with nc.Block() as block:
        @block.sync
        def _(sp):
            def load(g):
                if not isinstance(g, int):
                    sp.wait_ge(wo_lo, g)
                    sp.dma_start(raw[:, :], wq[:, cols(g, KM * QC)]).then_inc(raw_in, 16)
                sp.wait_ge(wq_lo, g + 1)
                sp.dma_start(raw[:, :], wo[:, cols(g, HPG * DM)]).then_inc(raw_in, 16)
            load(0)
            with sp.Fori(1, GROUPS) as g:
                load(g)

        @block.tensor
        def _(pe):
            def queries(g, b):
                v = g * BATCH + b
                if b == 0:
                    pe.wait_ge(wq_hi, g + 1)
                    pe.wait_ge(wq_lo, g + 1)
                at_least(pe, q_turned, v)
                at_least(pe, q_cosine, v)
                for h in range(HPG):
                    for k in range(KM):
                        for w, x in ((wqh, M.xh), (wqh, M.xl), (wql, M.xh)):
                            mm = nc.tensor.matmul(ps_q[:, h * SEQ:(h + 1) * SEQ], w[:, k, h * HD:(h + 1) * HD],
                                                  x[:, k, b * SEQ:(b + 1) * SEQ],
                                                  start=(k == 0 and w is wqh and x is M.xh), stop=(k == KM - 1 and w is wql))
                mm.then_inc(q_prod, 1)

            def scores(g, b):
                v = g * BATCH + b
                pe.wait_ge(q_done, v + 1)
                at_least(pe, exped, v)
                keys = K[:, bass.ds(g, 1), :].rearrange("p a t -> p (a t)")
                for h in range(HPG):
                    nc.tensor.matmul(s0[:, h, :], q[:, h, 0:P], keys[:, b * SEQ:b * SEQ + P], start=True, stop=True)
                for h in range(HPG):
                    mm = nc.tensor.matmul(s1[:, h, :], q[:, h, P:SEQ], keys[:, b * SEQ:(b + 1) * SEQ], start=True, stop=True)
                mm.then_inc(scored, 1)

            def output(g, b):
                v = g * BATCH + b
                if b == 0:
                    pe.wait_ge(wo_hi, g + 1)
                    pe.wait_ge(wo_lo, g + 1)
                pe.wait_ge(o_lo, v * 2 + 2)
                for t in range(QT):
                    for h in range(HPG):
                        part = slice(h * P, (h + 1) * P)
                        nc.tensor.matmul(X[t], oh[:, t, part], woh[:, h, :], start=(h == 0), stop=False)
                        nc.tensor.matmul(X[t], oh[:, t, part], wol[:, h, :], start=False, stop=False)
                        mm = nc.tensor.matmul(X[t], ol[:, t, part], woh[:, h, :], start=False, stop=(h == HPG - 1))
                    mm.then_inc(o_prod, 1)

            def attend(g, b):
                v = g * BATCH + b
                pe.wait_ge(normed, v + 1)
                for h in range(HPG):
                    mm = nc.tensor.transpose(X[2][:, h * P:(h + 1) * P], pa[:, h, :], ident)
                mm.then_inc(flipped, 1)
                for i in range(QT):
                    at_least(pe, added, v * 2 - 1 + i)
                    for h in range(HPG):
                        mm = nc.tensor.transpose(X[i][:, h * P:(h + 1) * P], pb[:, h, i * P:(i + 1) * P], ident)
                    mm.then_inc(flipped, 1)
                pe.wait_ge(v_here, v + 1)
                pe.wait_ge(p_kept_act, v * 2 + 1)
                nc.tensor.matmul(X[2], vs[:, 0, :], pt[:, 0, :], start=True, stop=True).then_inc(summed, 1)
                pe.wait_ge(p_kept_dve, v + 1)
                nc.tensor.matmul(X[0], vs[:, 0, :], pt[:, 1, :], start=True, stop=False)
                pe.wait_ge(p_kept_act, v * 2 + 2)
                nc.tensor.matmul(X[0], vs[:, 1, :], pt[:, 2, :], start=False, stop=True).then_inc(summed, 1)

            def body(g, b):
                if more(g, b):
                    queries(*after(g, b))
                if b > 0:
                    output(g, b - 1)
                elif not (isinstance(g, int) and g == 0):
                    output(g - 1, BATCH - 1)
                attend(g, b)
                if more(g, b):
                    scores(*after(g, b))

            queries(0, 0)
            scores(0, 0)
            groups(pe, body)
            output(GROUPS - 1, BATCH - 1)

        @block.scalar
        def _(act):
            def turn(g, b):
                v = g * BATCH + b
                act.wait_ge(q_prod, v + 1)
                at_least(act, q_done, v)
                nc.scalar.activation(turned[0:64, :], ps_q[64:128, :], ACT.Copy)
                nc.scalar.activation(turned[64:128, :], ps_q[0:64, :], ACT.Copy).then_inc(q_turned, 1)

            def exps(g, b):
                v = g * BATCH + b
                act.wait_ge(neg_max, v + 1)
                at_least(act, flipped, v * 3)
                at_least(act, inverse, v)
                for h in range(HPG):
                    nc.scalar.activation(pa[:, h, :], s0[:, h, :], ACT.Exp, bias=nm[:, h:h + 1], scale=SCALE,
                                         accum_out=sums[:, h:h + 1])
                for h in range(HPG):
                    ins = nc.scalar.activation(pb[:, h, :], s1[:, h, :], ACT.Exp, bias=nm[:, 4 + h:5 + h], scale=SCALE,
                                               accum_out=sums[:, 4 + h:5 + h])
                ins.then_inc(exped, 1)

            def query_weights(g):
                at_least(act, raw_in, g * 32)
                at_least(act, q_prod, g * BATCH)
                nc.scalar.activation(flat(wqh), raw[:, :], ACT.Copy).then_inc(wq_hi, 1)

            def output_weights(g):
                act.wait_ge(raw_in, g * 32 + 16)
                at_least(act, o_prod, g * BATCH * QT)
                nc.scalar.activation(flat(woh), raw[:, :], ACT.Copy).then_inc(wo_hi, 1)

            def body(g, b):
                v = g * BATCH + b
                if more(g, b):
                    turn(*after(g, b))
                if b == 2 and not (isinstance(g, int) and g == GROUPS - 1):
                    query_weights(g + 1)
                at_least(act, summed, v * 2)
                act.wait_ge(flipped, v * 3 + 1)
                nc.scalar.activation(pt[:, 0, :], X[2], ACT.Copy).then_inc(p_kept_act, 1)
                act.wait_ge(flipped, v * 3 + 3)
                nc.scalar.activation(pt[:, 2, :], X[1], ACT.Copy).then_inc(p_kept_act, 1)
                at_least(act, o_prod, v * QT)
                for t, x in ((0, X[2]), (1, X[0])):
                    act.wait_ge(summed, v * 2 + t + 1)
                    nc.scalar.activation(oh[:, t, :], x, ACT.Copy).then_inc(o_hi, 1)
                if b == 0:
                    output_weights(g)
                if more(g, b):
                    exps(*after(g, b))

            query_weights(0)
            turn(0, 0)
            exps(0, 0)
            groups(act, body)

        @block.gpsimd
        def _(pool):
            def sine(g, b):
                v = g * BATCH + b
                pool.wait_ge(q_turned, v + 1)
                nc.gpsimd.tensor_tensor(heads(turned[:, :]), heads(turned[:, :]), over_heads(C_SIN, SEQ), ALU.mult).then_inc(q_sine, 1)

            def query_weights(g):
                pool.wait_ge(wq_hi, g + 1)
                nc.gpsimd.tensor_tensor(flat(wql), raw[:, :], f32(flat(wqh)), ALU.subtract).then_inc(wq_lo, 1)

            def output_weights(g):
                pool.wait_ge(wo_hi, g + 1)
                nc.gpsimd.tensor_tensor(flat(wol), raw[:, :], f32(flat(woh)), ALU.subtract).then_inc(wo_lo, 1)

            def body(g, b):
                if more(g, b):
                    sine(*after(g, b))
                if b == 2 and not (isinstance(g, int) and g == GROUPS - 1):
                    query_weights(g + 1)
                if b == 0:
                    output_weights(g)

            query_weights(0)
            sine(0, 0)
            groups(pool, body)

        @block.vector
        def _(dve):
            def cosine(g, b):
                v = g * BATCH + b
                dve.wait_ge(q_turned, v + 1)
                nc.vector.tensor_tensor(heads(direct[:, :]), heads(ps_q), over_heads(C_COS, SEQ), ALU.mult).then_inc(q_cosine, 1)

            def rotate(g, b):
                v = g * BATCH + b
                dve.wait_ge(q_cosine, v + 1)
                dve.wait_ge(q_sine, v + 1)
                at_least(dve, scored, v)
                nc.vector.tensor_tensor(flat(q), direct[:, :], turned[:, :], ALU.add).then_inc(q_done, 1)

            def maxima(g, b):
                v = g * BATCH + b
                dve.wait_ge(scored, v + 1)
                nc.vector.tensor_tensor(s0, s0, over_heads(C_MASK, P), ALU.add).then_inc(masked, 1)
                nc.vector.tensor_tensor(s1[:, :, P:SEQ], s1[:, :, P:SEQ], over_heads(C_MASK, P), ALU.add).then_inc(masked, 1)
                dve.wait_ge(masked, v * 2 + 2)
                at_least(dve, exped, v)
                nc.vector.tensor_reduce(mx[:, 0:4], s0, AX_X, ALU.max).then_inc(maxed, 1)
                nc.vector.tensor_reduce(mx[:, 4:8], s1, AX_X, ALU.max).then_inc(maxed, 1)
                dve.wait_ge(maxed, v * 2 + 2)
                nc.vector.tensor_scalar(nm[:, :], mx[:, :], -SCALE, None, ALU.mult).then_inc(neg_max, 1)

            def probabilities(g, b):
                v = g * BATCH + b
                dve.wait_ge(exped, v + 1)
                at_least(dve, normed, v)
                nc.vector.reciprocal(inv[:, :], sums[:, :]).then_inc(inverse, 1)
                dve.wait_ge(inverse, v + 1)
                for h in range(HPG):
                    nc.vector.tensor_scalar(pa[:, h, :], pa[:, h, :], inv[:, h:h + 1], None, ALU.mult)
                for h in range(HPG):
                    ins = nc.vector.tensor_scalar(pb[:, h, :], pb[:, h, :], inv[:, 4 + h:5 + h], None, ALU.mult)
                ins.then_inc(normed, 1)

            def accumulate(v, b):
                for t in range(QT):
                    dve.wait_ge(o_prod, v * QT + t + 1)
                    nc.vector.tensor_tensor(acc[:, QT * b + t, :], X[t], acc[:, QT * b + t, :], ALU.add).then_inc(added, 1)

            def body(g, b):
                v = g * BATCH + b
                at_least(dve, summed, v * 2)
                nc.vector.tensor_copy(vs[:, :, :], V[:, QT * b:QT * b + QT, cols(g, HD)]).then_inc(v_here, 1)
                if more(g, b):
                    cosine(*after(g, b))
                if not (isinstance(v, int) and v == 0):
                    accumulate(v - 1, (b - 1) % BATCH)
                dve.wait_ge(flipped, v * 3 + 2)
                nc.vector.tensor_copy(pt[:, 1, :], X[0]).then_inc(p_kept_dve, 1)
                if more(g, b):
                    rotate(*after(g, b))
                for t, x in ((0, X[2]), (1, X[0])):
                    dve.wait_ge(o_hi, v * 2 + t + 1)
                    nc.vector.tensor_tensor(ol[:, t, :], x, f32(oh[:, t, :]), ALU.subtract).then_inc(o_lo, 1)
                if more(g, b):
                    maxima(*after(g, b))
                    probabilities(*after(g, b))

            nc.vector.memset(flat(acc), 0.0).then_inc(zeroed, 1)
            dve.wait_ge(zeroed, 1)
            cosine(0, 0)
            rotate(0, 0)
            maxima(0, 0)
            probabilities(0, 0)
            groups(dve, body)
            accumulate(U - 1, BATCH - 1)
    signals.close()


def coefficients(nc, M):
    signals = Signals(nc)
    rows, total, done = (signals(f"coeff_{n}") for n in ("rows", "total", "done"))
    with nc.Block() as block:
        @block.vector
        def _(dve):
            nc.vector.tensor_reduce(M.row_sums[:, :], M.diff_sums[:, :, :], AX_X, ALU.add).then_inc(rows, 1)
            dve.wait_ge(total, 1)
            nc.vector.tensor_scalar(M.coeff[:, :], M.ps[:, 0, 0:3], 1.0 / N_DIFF, None, ALU.mult).then_inc(done, 1)
            dve.wait_ge(done, 1)

        @block.tensor
        def _(pe):
            pe.wait_ge(rows, 1)
            nc.tensor.matmul(M.ps[:, 0, 0:3], M.ones[:, :], M.row_sums[:, :], start=True, stop=True).then_inc(total, 1)
    signals.close()


def program(nc, D, out, stop_after=None, taps=None):
    M = type("Memory", (), {})()
    M.ps = nc.alloc_psum_tensor("psum", [P, 8, HALF], F32)
    base = (nc.sbuf_base + 31) // 32 * 32
    end = nc.sbuf_usable_end
    resident = Places(nc, "res", base, base + 6 * KB)
    M.const = resident("const", [P, C_END])
    M.ones = resident("ones", [P, P])
    M.half = resident("half", [P, 1])
    M.diff_sums = resident("diff_sums", [P, 3, N_SUMS])
    M.row_sums = resident("row_sums", [P, 3])
    M.coeff = resident("coeff", [P, 3])
    z = resident.at
    at = lambda tag, kb: Places(nc, tag, z + kb * KB, end)
    M.x = at("tok", 0)("x", [P, TT, DM])
    opnd = at("opnd", 16)
    M.xh, M.xl = opnd("xh", [P, KM, TOK], F32R), opnd("xl", [P, KM, TOK], F32R)
    M.scratch32 = at("scratch", 16)("s", [P, 8 * TOK])

    mamba = at("ssm", 48)
    x_conv = mamba("x_conv", [P, BATCH, KI * SEQ])
    gate = mamba("gate", [P, BATCH, KI * SEQ])
    dt = mamba("dt", [P, BATCH, KI * SEQ])
    M.vec = mamba("vec", [P, V_END])
    free = (mamba.at - z + KB - 1) // KB
    load_inputs(nc, M, D["x"], D["const"], D["vec"])
    if stop_after == "load": return M
    finish_phase(nc, "n0", M, at("n0", free), 0, norm_only=True)
    if stop_after == "n0": return M
    widen_phase(nc, "in", M, at("in", free), KI, "ssm", D["w_in"], x_conv=x_conv, gate=gate)
    M.x_conv, M.gate, M.dt = x_conv, gate, dt
    if stop_after == "in": return M
    ssm_parameters(nc, M, at("par", free), x_conv, dt, D["bc"], D["w_x"], D["w_dt"], D["block_mean"])
    if stop_after == "par": return M
    scan_places = at("scan", free)
    w_res = scan_places("w_out", [P, KI, DM])
    scan_phase(nc, M, scan_places, x_conv, dt, D["bc"], w_res, D["w_out"])
    if stop_after == "scan": return M
    tile_of = lambda a: (lambda t, s: a[:, :, :].rearrange("p b (d c) -> p (b d c)", d=KI)[:, bass.ds((t - s) * (KI * P), KI * SEQ)]
                         .rearrange("p (d c) -> p d c", d=KI)[:, :, s * P:(s + 1) * P])
    finish_phase(nc, "fa", M, split_places(nc, z + 112 * KB, z + free * KB, z + (free + 16) * KB, end), KI, hidden=tile_of(x_conv), gate=tile_of(gate), w_raw=w_res)
    if stop_after == "fa": return M

    mlp = at("mlp0", 48)
    hidden = mlp("hidden", [P, F0, TOK])
    down = mlp("down", [P, F0, DM], I32)
    sc = [mlp("gate_s", [P, F0]), mlp("up_s", [P, F0])]
    scale_row = mlp("down_s", [P, DM])
    mlp0 = (mlp.at - z + KB - 1) // KB
    load_scales(nc, sc, scale_row, D["gate_s"], D["up_s"], D["down_s"])
    widen_phase(nc, "mi", M, at("mi", mlp0), F0, "int", D["w_gu"], hidden=hidden, scales=sc, second=(down, D["w_down"]),
                diff=dict(pairs=[(D["dw1"], D["dm1"]), (D["dw3"], D["dm3"]), (D["dw2"], D["dm2"])], sums=M.diff_sums))
    plain = lambda a: (lambda t, s: a[:, :, cols(t, P)])
    finish_phase(nc, "fb", M, at("fb", mlp0), F0, hidden=plain(hidden), w_raw=down, out_scale=scale_row)
    if stop_after == "fb": return M

    att = at("att", 48)
    ch, cl = att("ch", [P, KM, TOK], F32R), att("cl", [P, KM, TOK], F32R)
    K, V = att("k", [P, GROUPS, TOK]), att("v", [P, TT, GROUPS * HD])
    M.K, M.V, M.ch = K, V, ch
    wq_raw = at("wq", 144)("raw", [P, KM * HPG * HD])
    key_value_phase(nc, M, at("kv", 144), at("kvv", 128), K, V, ch, cl, D["w_kv"], D["w_upv"], wq_raw, D["w_q"])
    if stop_after == "kv": return M
    acc = at("acc", 48)("acc", [P, TT, DM])
    att2 = at("att2", 64)
    place = split_places(nc, z + 64 * KB, z + 80 * KB, z + 152 * KB, end)
    attention_phase(nc, M, place, wq_raw, K, V, acc, D["w_q"], D["w_o"])
    M.acc = acc
    if stop_after == "att": return M
    finish_phase(nc, "fc", M, at("fc", 80), 0, acc=acc)
    if stop_after == "fc": return M

    coefficients(nc, M)
    mlp = at("mlp1", 48)
    hidden = mlp("hidden", [P, F1, TOK])
    down = mlp("down", [P, F1, DM])
    widen_phase(nc, "md", M, mlp, F1, "diff", D["w_mlp"], D["b_mlp"], hidden=hidden, coeff=M.coeff, second=(down,))
    M.hidden, M.down = hidden, down
    if stop_after == "md": return M
    last = split_places(nc, z + 16 * KB, z + 48 * KB, z + 132 * KB, end)
    finish_phase(nc, "fd", M, last, F1, hidden=plain(hidden), w_raw=down, last_out=out)
    return M


def split_places(nc, a0, a1, b0, b1):
    first, rest = Places(nc, "low", a0, a1), Places(nc, "high", b0, b1)

    def place(name, shape, dt=F32):
        size = int(np.prod(shape[1:])) * 4
        return (first if first.at + size <= first.end else rest)(name, shape, dt)
    return place


def load_scales(nc, sc, row, gate_s, up_s, down_s):
    signals = Signals(nc)
    loaded = signals("scales_loaded")
    with nc.Block() as block:
        @block.sync
        def _(sp):
            sp.dma_start(sc[0][:, :], gate_s).then_inc(loaded, 16)
            sp.dma_start(sc[1][:, :], up_s).then_inc(loaded, 16)
            sp.dma_start(row[:, :], down_s.broadcast_to((P, DM))).then_inc(loaded, 16)
            sp.wait_ge(loaded, 48)
    signals.close()




def shape_constants():
    c = np.zeros((P, C_END), np.float32)
    c[:, C_ID:C_ID + P] = np.eye(P, dtype=np.float32)
    inv = 1.0 / 10000.0 ** (np.arange(0, HD, 2, dtype=np.float32) / HD)
    freqs = np.outer(np.arange(SEQ, dtype=np.float32), inv.astype(np.float32)).astype(np.float32)
    cos, sin = np.cos(freqs).T.astype(np.float32), np.sin(freqs).T.astype(np.float32)
    c[:, C_COS:C_COS + SEQ] = np.concatenate([cos, cos])
    c[:, C_SIN:C_SIN + SEQ] = np.concatenate([-sin, sin])
    kc, ks = cos[:ROPE_HALF], sin[:ROPE_HALF]
    c[:, C_COSK:C_COSK + SEQ] = np.concatenate([kc, kc, kc, kc])
    c[:, C_SINK:C_SINK + SEQ] = np.concatenate([-ks, ks, -ks, ks])
    c[:, C_MASK:C_MASK + P] = np.where(np.arange(P)[None, :] > np.arange(P)[:, None], NEG, 0.0)
    m = np.zeros((NX, NX), np.float32)
    for lo, hi in ((0, RANK), (RANK, RANK + N_ST), (RANK + N_ST, NX)):
        m[lo:hi, lo:hi] = 1.0 / (hi - lo)
    return c, m


def stationary(w, tiles=None):
    o, i = w.shape
    return w.reshape(o // P, P, i // P, P).transpose(3, 0, 2, 1)


def rows_padded(w, n):
    return np.concatenate([w, np.zeros((n - w.shape[0],) + w.shape[1:], w.dtype)])


def contraction_major(w):
    o, i = w.shape
    return np.ascontiguousarray(w.T.reshape(i // P, P, o).transpose(1, 0, 2))


def lay_out(a):
    flat = lambda w: np.ascontiguousarray(w.reshape(P, -1))
    per_channel = lambda v: v.reshape(KI, P, -1).transpose(1, 0, 2).reshape(P, -1)
    c, m = shape_constants()
    L = {"x": a["L0_attn_hidden_states"].reshape(TOK, DM), "const": c, "block_mean": m}
    L["vec"] = np.ascontiguousarray(np.concatenate(
        [per_channel(a["L0_attn_conv_w"]), per_channel(a["L0_attn_conv_b"]), per_channel(a["L0_attn_b_dt"])]
        + [per_channel(a["L0_attn_A_log"])] * BATCH + [per_channel(a["L0_attn_D"])] * BATCH, axis=1))
    w = a["L0_attn_W_in"]
    L["w_in"] = flat(np.stack([stationary(w[:D_IN]), stationary(w[D_IN:])], axis=2))
    L["w_x"] = contraction_major(a["L0_attn_W_x"])
    L["w_dt"] = np.ascontiguousarray(a["L0_attn_W_dt"].T)
    L["w_out"] = contraction_major(a["L0_attn_W_out"])
    g, u = (rows_padded(a[f"L0_ffn_{n}_w"], F0 * P) for n in ("gate", "up"))
    L["w_gu"] = flat(np.stack([stationary(g), stationary(u)], axis=2))
    L["w_down"] = contraction_major(rows_padded(a["L0_ffn_down_w"].T, F0 * P).T)
    for n in ("gate", "up"):
        L[f"{n}_s"] = np.ascontiguousarray(rows_padded(a[f"L0_ffn_{n}_s"], F0 * P).reshape(F0, P).T)
    L["down_s"] = a["L0_ffn_down_s"].reshape(1, DM)
    dk, kr, upk = (stationary(a[f"L1_attn_{n}"]).reshape(P, KM, -1) for n in ("Wdk", "Wkr", "Wupk"))
    L["w_kv"] = np.ascontiguousarray(np.concatenate([dk, np.stack([kr, upk], axis=2).reshape(P, 2 * KM, -1)], axis=1)).reshape(P, -1)
    L["w_upv"] = contraction_major(a["L1_attn_Wupv"])
    L["w_q"] = np.ascontiguousarray(a["L1_attn_Wq"].reshape(GROUPS, HPG * HD, KM, P).transpose(3, 0, 2, 1)).reshape(P, -1)
    L["w_o"] = np.ascontiguousarray(a["L1_attn_Wo"].T.reshape(GROUPS, HPG, P, DM).transpose(2, 0, 1, 3)).reshape(P, -1)
    for name, w1, w3, w2 in (("w_mlp", "w1", "w3", "w2"), ("b_mlp", "mean_w1", "mean_w3", "mean_w2")):
        s1, s3 = (stationary(a[f"L1_ffn_{n}"]).reshape(P, F1, -1) for n in (w1, w3))
        s2 = contraction_major(a[f"L1_ffn_{w2}"])
        L[name] = np.ascontiguousarray(np.concatenate([s1, s3, s2], axis=2)).reshape(P, -1)
    for n in ("1", "2", "3"):
        L[f"dw{n}"] = a[f"L1_ffn_w{n}"].reshape(P, -1)
        L[f"dm{n}"] = a[f"L1_ffn_mean_w{n}"].reshape(P, -1)
    return L


def kernel(**inputs):
    import concourse.bacc as bacc
    from concourse.bass_utils import run_bass_kernel_spmd

    nc = bacc.Bacc("TRN2", target_bir_lowering=False, num_devices=1)
    arrays = lay_out({n: np.asarray(v) for n, v in inputs.items()})
    D = {n: nc.dram_tensor(f"in_{n}", v.shape, mybir.dt.from_np(v.dtype), kind="ExternalInput").ap() for n, v in arrays.items()}
    D["bc"] = nc.dram_tensor("bc_rows", (BATCH, 2 * N_ST, SEQ), F32).ap()
    out = nc.dram_tensor("out", (TOK, DM), F32, kind="ExternalOutput").ap()
    program(nc, D, out)
    r = run_bass_kernel_spmd(nc, [{f"in_{n}": v for n, v in arrays.items()}], core_ids=[0])
    return r.results[0]["out"].reshape(BATCH, SEQ, DM)
```

```python
import numpy as np
import concourse.bass as bass
from concourse import mybir

F32 = mybir.dt.float32
F32R = mybir.dt.float32r
I32 = mybir.dt.int32
ALU = mybir.AluOpType
ACT = mybir.ActivationFunctionType
AX_X = mybir.AxisListType.X

P = 128
BATCH, SEQ, DM = 4, 256, 512
TOK = BATCH * SEQ
TT = TOK // P
KM = DM // P
HALF = 512
D_IN, N_ST, K_CONV, RANK = 1024, 16, 4, 32
KI = D_IN // P
NX = RANK + 2 * N_ST
F0 = 11
F1 = 14
FF0, FF1 = 1376, 1792
HEADS, GROUPS, HD = 32, 8, 128
HPG = HEADS // GROUPS
QT = SEQ // P
ROPE_HALF = 32
RMS_EPS, LN_EPS = 1e-6, 1e-5
N_DIFF = FF1 * DM
DIFF_COLS = N_DIFF // P
NEG = -1.0e30

C_ID, C_COS, C_SIN = 0, P, P + SEQ
C_COSK, C_SINK, C_MASK, C_END = P + 2 * SEQ, P + 3 * SEQ, P + 4 * SEQ, 2 * P + 4 * SEQ
V_CW = 0
V_CB = V_CW + KI * K_CONV
V_BDT = V_CB + KI
V_AL = V_BDT + KI
V_D = V_AL + BATCH * KI * N_ST
V_END = V_D + BATCH * KI

N_SUMS = 8
KB = 1024


class Places:

    def __init__(self, nc, tag, start, end):
        self.nc, self.tag, self.at, self.end = nc, tag, start, end

    def __call__(self, name, shape, dt=F32):
        size = int(np.prod(shape[1:])) * 4
        t = self.nc.alloc_sbuf_tensor_at(f"{self.tag}_{name}", list(shape), dt, offset=self.at)
        self.at += (size + 31) // 32 * 32
        assert self.at <= self.end, (self.tag, name, self.at - self.end)
        return t


class Stretches:

    def __init__(self, nc, *stretches):
        self.places = [Places(nc, f"stretch{i}", a, b) for i, (a, b) in enumerate(stretches)]

    def __call__(self, name, shape, dt=F32):
        size = int(np.prod(shape[1:])) * 4
        for p in self.places:
            if p.at + size <= p.end:
                return p(name, shape, dt)
        raise ValueError(f"no room for {name}")


class Signals:

    def __init__(self, nc):
        self.nc, self.held = nc, []

    def __call__(self, name):
        self.held.append(self.nc.alloc_semaphore(name))
        return self.held[-1]

    def close(self):
        self.nc.clear_and_free_semaphores(self.held)
        self.nc.all_engine_barrier()


def at_least(eng, sem, value):
    if isinstance(value, int) and value <= 0:
        return
    eng.wait_ge(sem, value)


def paired_steps(eng, n, step, head=3, tail=0):
    pairs = (n - max(2, tail) - head) // 2
    for i in range(head):
        step(i, i % 2)
    if pairs > 0:
        with eng.Fori(0, pairs) as j:
            step(j * 2 + head, 1)
            step(j * 2 + head + 1, 0)
    for i in range(head + 2 * max(pairs, 0), n):
        step(i, i % 2)


def exists(i, n):
    return not isinstance(i, int) or 0 <= i < n


def f32(ap):
    return ap.bitcast(F32)


def by_batch(ap):
    return ap.rearrange("p (b t) -> p b t", b=BATCH)


def cols(i, width):
    return bass.ds(i * width, width)


def load_inputs(nc, M, x_in, consts):
    signals = Signals(nc)
    loaded = signals("inputs_loaded")
    made = signals("small_consts_made")
    with nc.Block() as block:
        @block.sync
        def _(sp):
            xv = x_in.rearrange("(t p) c -> p t c", p=P)
            sp.dma_start(M.x[:, 0:1, :], xv[:, 0:1, :]).then_inc(loaded, 16)
            sp.wait_ge(loaded, 32)

        @block.scalar
        def _(act):
            act.dma_start(M.const[:, 0:P], consts[:, 0:P]).then_inc(loaded, 16)

        @block.gpsimd
        def _(pool):
            nc.gpsimd.memset(M.half[:, :], -0.5).then_inc(made, 1)
            nc.gpsimd.memset(M.ones[:, :], 1.0).then_inc(made, 1)
            pool.wait_ge(made, 2)
    signals.close()


def finish_phase(nc, tag, M, place, K, hidden=None, gate=None, w_raw=None, acc=None,
                 out_scale=None, last_out=None, norm_only=False, ahead=(), x_loads=()):
    signals = Signals(nc)
    sem = lambda n: signals(f"{tag}_{n}")
    proj = hidden is not None
    split_w, split_wl = sem("w_hi"), sem("w_lo")
    gated, h_hi, h_lo = sem("hidden_gated"), sem("hidden_hi"), sem("hidden_lo")
    y_ready, scaled = sem("y_ready"), sem("y_scaled")
    y_stats, y_moments, y_var, y_rstd, y_normed = (sem("y_stats"), sem("y_moments"), sem("y_var"),
                                                   sem("y_rstd"), sem("y_normed"))
    x_new, x_stats, x_moments, x_var, x_rstd, xn_ready = (sem("x_new"), sem("x_stats"), sem("x_moments"),
                                                          sem("x_var"), sem("x_rstd"), sem("xn_ready"))
    ahead_in, x_in = sem("ahead_in"), [sem(f"x_in{i}") for i in range(len(x_loads))]
    transposed, x_hi, x_lo, stored = sem("transposed"), sem("x_hi"), sem("x_lo"), sem("stored")
    if proj:
        wh = place("wh", [P, K, DM], F32R)
        wl = place("wl", [P, K, DM], F32R)
        hh = [place(f"hh{i}", [P, K, P], F32R) for i in range(2)]
        hl = [place(f"hl{i}", [P, K, P], F32R) for i in range(2)]
        hg = [place(f"hg{i}", [P, K, P]) for i in range(2)] if gate is not None else None
    small = place("small", [P, 2, 32])
    tmp = place("tmp", [P, DM])
    xn = [place(f"xn{i}", [P, DM]) for i in range(2)]
    ident = M.const[:, C_ID:C_ID + P]
    ps_y = [M.ps[:, i, :] for i in range(2)]
    ps_t = [M.ps[:, 2 + i, :] for i in range(2)]
    store = last_out is not None
    lag = 1 if norm_only else 2
    def y_of(t, s):
        if not proj:
            return acc[:, bass.ds(t, 1), :].rearrange("p a c -> p (a c)")
        return tmp[:, :] if out_scale is not None else ps_y[s]

    def x_of(t):
        return M.x[:, t, :]

    with nc.Block() as block:
        @block.sync
        def _(sp):
            for i, (_, dst, src) in enumerate(x_loads):
                sp.dma_start(dst, src).then_inc(x_in[i], 16)
            for dst, src in ahead:
                sp.dma_start(dst, src).then_inc(ahead_in, 16)
            for t in range(TT if store else 0):
                sp.wait_ge(x_new, t + 1)
                sp.dma_start(last_out[t * P:(t + 1) * P, :], M.x[:, t, :]).then_inc(stored, 16)
            if store:
                sp.wait_ge(stored, 16 * TT)
            if ahead:
                sp.wait_ge(ahead_in, 16 * len(ahead))

        @block.tensor
        def _(pe):
            def transposes(t, s):
                at_least(pe, xn_ready, t + 1)
                at_least(pe, x_lo, t - 1)
                for c in range(KM):
                    mm = nc.tensor.transpose(ps_t[s][:, c * P:(c + 1) * P], xn[s][:, c * P:(c + 1) * P], ident)
                mm.then_inc(transposed, 1)

            def step(t, s):
                if proj and t < TT:
                    at_least(pe, h_hi, t + 1)
                    at_least(pe, h_lo, t + 1)
                    at_least(pe, scaled if out_scale is not None else y_normed, t - 1)
                    for k in range(K):
                        if isinstance(t, int) and t == 0:
                            pe.wait_ge(split_w, k + 1)
                            pe.wait_ge(split_wl, k + 1)
                        nc.tensor.matmul(ps_y[s], hh[s][:, k, :], wh[:, k, :], start=(k == 0), stop=False)
                        nc.tensor.matmul(ps_y[s], hh[s][:, k, :], wl[:, k, :], start=False, stop=False)
                        mm = nc.tensor.matmul(ps_y[s], hl[s][:, k, :], wh[:, k, :], start=False, stop=(k == K - 1))
                    mm.then_inc(y_ready, 1)
                if not store and t >= lag:
                    transposes(t - lag, (t - lag) % 2)

            for t in range(TT + (0 if store else lag)):
                step(t, t % 2)

        @block.scalar
        def _(act):
            def hidden_hi(t, s):
                at_least(act, y_ready, t - 1)
                src = hidden(t, s)
                if gate is not None:
                    at_least(act, gated, t + 1)
                    src = hg[s][:, :, :]
                nc.scalar.activation(hh[s][:, :, :], src, ACT.Copy).then_inc(h_hi, 1)

            def x_high(t, s):
                at_least(act, transposed, t + 1)
                nc.scalar.activation(M.xh[:, :, cols(t, P)], ps_t[s].rearrange("p (c q) -> p c q", c=KM), ACT.Copy).then_inc(x_hi, 1)

            def step(t, s):
                if proj and t + 1 < TT:
                    hidden_hi(t + 1, 1 - s)
                if not store and t > lag:
                    x_high(t - lag - 1, (t - lag - 1) % 2)

            if proj:
                hidden_hi(0, 0)
                for k in range(K):
                    nc.scalar.activation(wh[:, k, :], w_raw[:, k, :], ACT.Copy).then_inc(split_w, 1)
            for t in range(TT + (0 if store else lag + 1)):
                step(t, t % 2)

        @block.gpsimd
        def _(pool):
            def gating(t, s):
                if gate is not None and t < TT:
                    at_least(pool, h_lo, t - 1)
                    nc.gpsimd.tensor_tensor(hg[s][:, :, :], hidden(t, s), gate(t, s),
                                            ALU.mult).then_inc(gated, 1)

            def hidden_low(t, s):
                src = hidden(t, s) if gate is None else hg[s][:, :, :]
                at_least(pool, y_ready, t - 1)
                at_least(pool, h_hi, t + 1)
                nc.gpsimd.tensor_tensor(hl[s][:, :, :], src, f32(hh[s][:, :, :]), ALU.subtract).then_inc(h_lo, 1)

            def rstd(var, done, out, t, s, col):
                at_least(pool, var, t + 1)
                nc.gpsimd.tensor_tensor(small[:, s, out:out + 1], small[:, s, col:col + 1], M.half[:, :],
                                        ALU.pow).then_inc(done, 1)

            to_new = 0 if proj or norm_only else 1

            def step(t, s):
                if not norm_only and t < TT:
                    rstd(y_var, y_rstd, 9, t, s, 8)
                if proj and t + 2 < TT:
                    hidden_low(t + 2, s)
                if not store and 0 <= t - to_new < TT:
                    rstd(x_var, x_rstd, 25, t - to_new, (t - to_new) % 2, 24)
                if proj:
                    gating(t + 3, 1 - s)

            if proj:
                gating(0, 0)
                gating(1, 1)
                hidden_low(0, 0)
                hidden_low(1, 1)
                gating(2, 0)
            for t in range(TT + to_new):
                step(t, t % 2)

        @block.vector
        def _(dve):
            def x_norm(t, s):
                at_least(dve, x_rstd, t + 1)
                at_least(dve, transposed, t - 1)
                nc.vector.tensor_scalar(xn[s][:, :], x_of(t), small[:, s, 22:23], small[:, s, 25:26],
                                        ALU.subtract, ALU.mult).then_inc(xn_ready, 1)

            def x_low(t, s):
                dve.wait_ge(x_hi, t + 1)
                nc.vector.tensor_tensor(M.xl[:, :, cols(t, P)], ps_t[s].rearrange("p (c q) -> p c q", c=KM),
                                        f32(M.xh[:, :, cols(t, P)]), ALU.subtract).then_inc(x_lo, 1)

            def y_moments_of(t, s):
                if proj:
                    at_least(dve, y_ready, t + 1)
                y = y_of(t, s)
                if out_scale is not None:
                    at_least(dve, x_new, t)
                    nc.vector.tensor_tensor(y, ps_y[s], out_scale[:, :], ALU.mult).then_inc(scaled, 1)
                    at_least(dve, scaled, t + 1)
                nc.vector.bn_stats(small[:, s, 0:6], y).then_inc(y_stats, 1)
                at_least(dve, y_stats, t + 1)
                nc.vector.bn_aggr(small[:, s, 6:8], small[:, s, 0:6]).then_inc(y_moments, 1)
                at_least(dve, y_moments, t + 1)
                nc.vector.tensor_scalar(small[:, s, 8:9], small[:, s, 7:8], LN_EPS, None, ALU.add).then_inc(y_var, 1)

            def residual(t, s):
                at_least(dve, y_rstd, t + 1)
                at_least(dve, x_new, t)
                nc.vector.tensor_scalar(tmp[:, :], y_of(t, s), small[:, s, 6:7], small[:, s, 9:10],
                                        ALU.subtract, ALU.mult).then_inc(y_normed, 1)
                at_least(dve, y_normed, t + 1)
                nc.vector.tensor_tensor(x_of(t), x_of(t), tmp[:, :], ALU.add).then_inc(x_new, 1)

            def x_moments_of(t, s):
                if not norm_only:
                    at_least(dve, x_new, t + 1)
                for i, (first, _, _) in enumerate(x_loads):
                    if first == t:
                        dve.wait_ge(x_in[i], 16)
                nc.vector.bn_stats(small[:, s, 16:22], x_of(t)).then_inc(x_stats, 1)
                at_least(dve, x_stats, t + 1)
                at_least(dve, xn_ready, t - 1)
                nc.vector.bn_aggr(small[:, s, 22:24], small[:, s, 16:22]).then_inc(x_moments, 1)
                at_least(dve, x_moments, t + 1)
                nc.vector.tensor_scalar(small[:, s, 24:25], small[:, s, 23:24], LN_EPS, None, ALU.add).then_inc(x_var, 1)

            to_new = 0 if proj or norm_only else 1
            to_norm, to_low = to_new + 1, lag + 1

            def step(t):
                if not norm_only and t < TT:
                    y_moments_of(t, t % 2)
                if not (store or norm_only) and 0 <= t - to_norm < TT:
                    x_norm(t - to_norm, (t - to_norm) % 2)
                if 0 <= t - to_new < TT:
                    if not norm_only:
                        residual(t - to_new, (t - to_new) % 2)
                    if not store:
                        x_moments_of(t - to_new, (t - to_new) % 2)
                if norm_only and 0 <= t - to_norm < TT:
                    x_norm(t - to_norm, (t - to_norm) % 2)
                if not store and 0 <= t - to_low < TT:
                    x_low(t - to_low, (t - to_low) % 2)

            if proj:
                for k in range(K):
                    dve.wait_ge(split_w, k + 1)
                    nc.vector.tensor_tensor(wl[:, k, :], w_raw[:, k, :], f32(wh[:, k, :]), ALU.subtract).then_inc(split_wl, 1)
            for t in range(TT + max(to_norm, to_low)):
                step(t)
    signals.close()


def widen_phase(nc, tag, M, place, F, kind, raw_dram, base_dram=None, hidden=None,
                x_conv=None, gate=None, scales=None, coeff=None, second=None, diff=None, raw=None, base=None, ahead=()):
    signals = Signals(nc)
    sem = lambda n: signals(f"{tag}_{n}")
    raw_in, ahead_in = [sem("raw_in0"), sem("raw_in1")], sem("ahead_in")
    w_diff, w_sign, w_full, w_hi, w_lo = (sem("w_diff"), sem("w_sign"), sem("w_full"),
                                                  sem("w_hi"), sem("w_lo"))
    prod, first_done, second_done = sem("products"), sem("first_done"), sem("second_done")
    tap = sem("tap")
    d_in, d_sub, d_abs = [sem("diff_in0"), sem("diff_in1")], sem("diff_sub"), sem("diff_abs")
    WC = 2 * KM * P
    RC = WC + DM if kind == "diff" else WC
    wh = [place(f"wh{i}", [P, 2, KM, P], F32R) for i in range(2)]
    wl = [place(f"wl{i}", [P, 2, KM, P], F32R) for i in range(2)]
    mid = [place(f"mid{i}", [P, TOK]) for i in range(2 if kind != "diff" else 1)]
    if kind == "diff":
        full = [place(f"full{i}", [P, RC]) for i in range(2)]
    if diff is not None:
        DC = DIFF_COLS // N_SUMS
        dw = [place(f"dw{i}", [P, 3, DC]) for i in range(2)]
        dm = [place(f"dm{i}", [P, 3, DC]) for i in range(2)]
        tail = F - N_SUMS + 1
    else:
        tail = 0
    flat = lambda t: t[:, :, :, :].rearrange("p a k o -> p (a k o)")
    ps = [[M.ps[:, 4 * s + 2 * a:4 * s + 2 * a + 2, :].rearrange("p a c -> p (a c)") for a in range(2)] for s in range(2)]

    with nc.Block() as block:
        @block.sync
        def _(sp):
            def step(f, s):
                at_least(sp, w_full if kind == "diff" else w_lo, f - 1)
                if not (isinstance(f, int) and f < 2):
                    sp.dma_start(raw[s][:, :], raw_dram[:, cols(f, RC)]).then_inc(raw_in[s], 16)
                    if kind == "diff":
                        sp.dma_start(base[s][:, :], base_dram[:, cols(f, RC)]).then_inc(raw_in[s], 16)
                if diff is not None and exists(f, N_SUMS):
                    at_least(sp, d_abs, f * 3 - 3)
                    for a, (w, m) in enumerate(diff["pairs"]):
                        sp.dma_start(dw[s][:, a, :], w[:, cols(f, DC)]).then_inc(d_in[s], 16)
                        sp.dma_start(dm[s][:, a, :], m[:, cols(f, DC)]).then_inc(d_in[s], 16)

            paired_steps(sp, F, step, tail=tail)
            for dst, src in ahead:
                sp.dma_start(dst, src).then_inc(ahead_in, 16)
            if ahead:
                sp.wait_ge(ahead_in, 16 * len(ahead))
            if diff is not None:
                sp.wait_ge(d_abs, 3 * N_SUMS)

        @block.tensor
        def _(pe):
            def step(f, s):
                at_least(pe, w_hi, f + 1)
                at_least(pe, w_lo, f + 1)
                at_least(pe, first_done, f - 1)
                at_least(pe, second_done, f - 1)
                for a in range(2):
                    for k in range(KM):
                        for w, x in ((wh, M.xh), (wh, M.xl), (wl, M.xh)):
                            for h in range(2):
                                mm = nc.tensor.matmul(ps[s][a][:, h * HALF:(h + 1) * HALF], w[s][:, a, k, :],
                                                      x[:, k, h * HALF:(h + 1) * HALF],
                                                      start=(k == 0 and w is wh and x is M.xh),
                                                      stop=(k == KM - 1 and w is wl))
                    mm.then_inc(prod, 1)

            paired_steps(pe, F, step)

        @block.scalar
        def _(act):
            def prepare(f, s):
                if kind == "diff":
                    at_least(act, w_diff, f + 1)
                    nc.scalar.activation(full[s][:, :], full[s][:, :], ACT.Sign).then_inc(w_sign, 1)
                    at_least(act, w_full, f + 1)
                    src = full[s][:, 0:WC]
                else:
                    at_least(act, raw_in[s], (f - s) * 8)
                    src = raw[s][:, 0:WC]
                at_least(act, prod, 2 * (f - 1))
                nc.scalar.activation(flat(wh[s]), src, ACT.Copy).then_inc(w_hi, 1)

            def differences(f, s):
                for a in range(3):
                    at_least(act, d_sub, 3 * f + a + 1)
                    nc.scalar.activation(dw[s][:, a, :], dw[s][:, a, :], ACT.Abs,
                                         accum_out=diff["sums"][:, a, bass.ds(f, 1)]).then_inc(d_abs, 1)

            def step(f, s):
                if exists(f + 1, F):
                    prepare(f + 1, 1 - s)
                if diff is not None and exists(f, N_SUMS):
                    differences(f, s)
                if kind == "ssm":
                    at_least(act, prod, 2 * f + 1)
                    at_least(act, first_done, f - 1)
                    nc.scalar.activation(mid[s][:, :], ps[s][0], ACT.Identity, bias=M.vec[:, bass.ds(f + V_CB, 1)],
                                         scale=M.vec[:, bass.ds(f * K_CONV + V_CW + K_CONV - 1, 1)]).then_inc(tap, 1)
                    at_least(act, prod, 2 * f + 2)
                    nc.scalar.activation(gate[:, :, cols(f, SEQ)], by_batch(ps[s][1]),
                                         ACT.Silu).then_inc(second_done, 1)
                    at_least(act, tap, 4 * f + 4)
                    nc.scalar.activation(x_conv[:, :, cols(f, SEQ)], by_batch(mid[s][:, :]),
                                         ACT.Silu).then_inc(first_done, 1)
                else:
                    m = mid[s % len(mid)]
                    at_least(act, prod, 2 * f + 1)
                    at_least(act, second_done, f - len(mid) + 1)
                    sc = scales[0][:, bass.ds(f, 1)] if kind == "int" else 1.0
                    nc.scalar.activation(m[:, :], ps[s][0], ACT.Silu, scale=sc).then_inc(first_done, 1)

            prepare(0, 0)
            paired_steps(act, F, step, tail=tail)

        @block.gpsimd
        def _(pool):
            def lows(f, s):
                if kind == "diff":
                    at_least(pool, w_full, f + 1)
                at_least(pool, w_hi, f + 1)
                src = full[s][:, 0:WC] if kind == "diff" else raw[s][:, 0:WC]
                nc.gpsimd.tensor_tensor(flat(wl[s]), src, f32(flat(wh[s])), ALU.subtract).then_inc(w_lo, 1)

            def difference(f, s):
                at_least(pool, raw_in[s], (f - s) * 16)
                at_least(pool, w_lo, f - 1)
                nc.gpsimd.tensor_tensor(full[s][:, :], raw[s][:, :], base[s][:, :], ALU.subtract).then_inc(w_diff, 1)

            def step(f, s):
                if kind != "int":
                    lows(f, s)
                if kind == "diff" and exists(f + 2, F):
                    difference(f + 2, s)
                if diff is not None and exists(f, N_SUMS):
                    at_least(pool, d_in[s], (f - s) * 48 + 96)
                    for a in range(3):
                        nc.gpsimd.tensor_tensor(dw[s][:, a, :], dw[s][:, a, :], dm[s][:, a, :], ALU.subtract).then_inc(d_sub, 1)

            if kind == "diff":
                difference(0, 0)
                difference(1, 1)
            if kind != "int" or diff is not None:
                paired_steps(pool, F, step, tail=tail)

        @block.vector
        def _(dve):
            def int_lows(f, s):
                at_least(dve, w_hi, f + 1)
                nc.vector.tensor_tensor(flat(wl[s]), raw[s][:, :], f32(flat(wh[s])), ALU.subtract).then_inc(w_lo, 1)

            def whole(f, s):
                at_least(dve, w_sign, f + 1)
                for a, lo, hi in ((0, 0, WC // 2), (1, WC // 2, WC), (2, WC, RC)):
                    src = full[s][:, lo:hi]
                    dst = second[0][:, bass.ds(f, 1), :].rearrange("p a c -> p (a c)") if a == 2 else src
                    ins = nc.vector.scalar_tensor_tensor(dst, src, coeff[:, a:a + 1], base[s][:, lo:hi], ALU.mult, ALU.add)
                ins.then_inc(w_full, 1)

            def step(f, s):
                if kind == "int" and exists(f + 1, F):
                    int_lows(f + 1, 1 - s)
                if kind == "diff" and exists(f + 1, F):
                    whole(f + 1, 1 - s)
                if kind == "ssm":
                    m = mid[s][:, :].rearrange("p (b t) -> p b t", b=BATCH)
                    src = ps[s][0].rearrange("p (b t) -> p b t", b=BATCH)
                    for j in range(1, K_CONV):
                        at_least(dve, tap, 4 * f + j)
                        nc.vector.scalar_tensor_tensor(m[:, :, j:SEQ], src[:, :, 0:SEQ - j],
                                                       M.vec[:, bass.ds(f * K_CONV + V_CW + K_CONV - 1 - j, 1)],
                                                       m[:, :, j:SEQ], ALU.mult, ALU.add).then_inc(tap, 1)
                else:
                    at_least(dve, prod, 2 * f + 2)
                    at_least(dve, first_done, f + 1)
                    sc = scales[1][:, bass.ds(f, 1)] if kind == "int" else 1.0
                    nc.vector.scalar_tensor_tensor(hidden[:, bass.ds(f, 1), :].rearrange("p a c -> p (a c)"), ps[s][1],
                                                   sc, mid[s % len(mid)][:, :], ALU.mult, ALU.mult).then_inc(second_done, 1)

            if kind == "diff":
                whole(0, 0)
            if kind == "int":
                int_lows(0, 0)
            paired_steps(dve, F, step)
            if kind != "ssm":
                dve.wait_ge(second_done, F)
    signals.close()


def ssm_parameters(nc, M, place, x_conv, dt, bc_dram, wx, wdt, block_mean, bm, cm):
    signals = Signals(nc)
    sem = lambda n: signals(f"par_{n}")
    loaded, raw_ready, squared, mean_ready, eps_added, rooted, inverse, normed = (
        sem("loaded"), sem("raw_ready"), sem("squared"), sem("mean_ready"), sem("eps_added"),
        sem("rooted"), sem("inverse"), sem("normed"))
    kept, stored, a_exp, a_done, pad_zero = sem("kept"), sem("bc_stored"), sem("a_exp"), sem("a_done"), sem("pad_zero")
    pre, magnitude, exped, logged, positive, dt_done = (sem("pre"), sem("magnitude"), sem("exped"), sem("logged"),
                                                        sem("positive"), sem("dt_done"))
    raw = place("raw", [NX, TOK])
    sq = place("sq", [NX, TOK])
    ssm = place("ssm", [P, TOK])
    log1p = M.scratch32
    ps_x = M.ps[0:NX, 0:2, :].rearrange("p a c -> p (a c)")
    ps_m = M.ps[0:NX, 2:4, :].rearrange("p a c -> p (a c)")
    ps_dt = [M.ps[:, 4 + 2 * s:6 + 2 * s, :].rearrange("p a c -> p (a c)") for s in range(2)]
    with nc.Block() as block:
        @block.sync
        def _(sp):
            sp.wait_ge(normed, 2)
            for b in range(BATCH):
                sp.dma_start(bc_dram[b, :, :], ssm[RANK:NX, b * SEQ:(b + 1) * SEQ]).then_inc(stored, 16)
            sp.wait_ge(stored, 16 * BATCH)
            sp.dma_start(bm[:, :, :], bc_dram[0:1, 0:N_ST, :].broadcast_to((P, N_ST, SEQ))).then_inc(loaded, 16)
            sp.dma_start(cm[:, :, :], bc_dram[0:1, N_ST:2 * N_ST, :].broadcast_to((P, N_ST, SEQ))).then_inc(loaded, 16)
            sp.wait_ge(loaded, 32)

        @block.tensor
        def _(pe):
            def mean(h):
                pe.wait_ge(squared, h + 1)
                nc.tensor.matmul(ps_m[:, h * HALF:(h + 1) * HALF], block_mean[:, :],
                                 sq[:, h * HALF:(h + 1) * HALF], start=True, stop=True).then_inc(mean_ready, 1)

            for h in range(2):
                for k in range(KI):
                    mm = nc.tensor.matmul(ps_x[:, h * HALF:(h + 1) * HALF], wx[:, k, :],
                                          x_conv[:, 2 * h:2 * h + 2, k * SEQ:(k + 1) * SEQ],
                                          start=(k == 0), stop=(k == KI - 1))
                mm.then_inc(raw_ready, 1)
                if h == 1:
                    mean(0)
            mean(1)
            pe.wait_ge(pad_zero, 1)
            pe.wait_ge(normed, 2)
            for f in range(KI):
                at_least(pe, magnitude, f - 1)
                at_least(pe, positive, f - 1)
                for h in range(2):
                    mm = nc.tensor.matmul(ps_dt[f % 2][:, h * HALF:(h + 1) * HALF], wdt[:, f * P:(f + 1) * P],
                                          ssm[:, h * HALF:(h + 1) * HALF], start=True, stop=True)
                mm.then_inc(pre, 1)

        @block.scalar
        def _(act):
            nc.scalar.activation(M.vec[:, V_AL:V_D], M.vec[:, V_AL:V_D], ACT.Exp).then_inc(a_exp, 1)
            for h in range(2):
                act.wait_ge(raw_ready, h + 1)
                half = slice(h * HALF, (h + 1) * HALF)
                nc.scalar.activation(sq[:, half], ps_x[:, half], ACT.Square).then_inc(squared, 1)
                nc.scalar.activation(raw[:, half], ps_x[:, half], ACT.Copy).then_inc(kept, 1)
                act.wait_ge(eps_added, h + 1)
                nc.scalar.activation(sq[:, half], sq[:, half], ACT.Sqrt).then_inc(rooted, 1)
            for f in range(KI):
                act.wait_ge(pre, f + 1)
                nc.scalar.activation(log1p[:, f * TOK:(f + 1) * TOK], ps_dt[f % 2], ACT.Abs,
                                     bias=M.vec[:, V_BDT + f:V_BDT + f + 1]).then_inc(magnitude, 1)
                act.wait_ge(magnitude, f + 1)
                nc.scalar.activation(log1p[:, f * TOK:(f + 1) * TOK], log1p[:, f * TOK:(f + 1) * TOK],
                                     ACT.Exp, scale=-1.0).then_inc(exped, 1)
            for f in range(KI):
                act.wait_ge(exped, f + 1)
                nc.scalar.activation(log1p[:, f * TOK:(f + 1) * TOK], log1p[:, f * TOK:(f + 1) * TOK],
                                     ACT.Ln, bias=1.0).then_inc(logged, 1)

        @block.vector
        def _(dve):
            nc.vector.memset(ssm[NX:P, :], 0.0).then_inc(pad_zero, 1)
            dve.wait_ge(a_exp, 1)
            nc.vector.tensor_scalar(M.vec[:, V_AL:V_D], M.vec[:, V_AL:V_D], -1.0, None, ALU.mult).then_inc(a_done, 1)
            for h in range(2):
                half = slice(h * HALF, (h + 1) * HALF)
                dve.wait_ge(mean_ready, h + 1)
                nc.vector.tensor_scalar(sq[:, half], ps_m[:, half], RMS_EPS, None, ALU.add).then_inc(eps_added, 1)
                dve.wait_ge(rooted, h + 1)
                nc.vector.reciprocal(sq[:, half], sq[:, half]).then_inc(inverse, 1)
                dve.wait_ge(inverse, h + 1)
                dve.wait_ge(kept, h + 1)
                nc.vector.tensor_tensor(ssm[0:NX, half], raw[:, half], sq[:, half], ALU.mult).then_inc(normed, 1)
            for f in range(KI):
                dve.wait_ge(magnitude, f + 1)
                bias = M.vec[:, V_BDT + f:V_BDT + f + 1]
                nc.vector.tensor_scalar(dt[:, :, f * SEQ:(f + 1) * SEQ], by_batch(ps_dt[f % 2]), bias, 0.0,
                                        ALU.add, ALU.max).then_inc(positive, 1)
            for f in range(KI):
                dve.wait_ge(logged, f + 1)
                dve.wait_ge(positive, f + 1)
                part = dt[:, :, f * SEQ:(f + 1) * SEQ]
                nc.vector.tensor_tensor(part, part, by_batch(log1p[:, f * TOK:(f + 1) * TOK]), ALU.add).then_inc(dt_done, 1)
    signals.close()


def scan_phase(nc, M, place, x_conv, dt, bc_dram, bm, cm, w_next, w_next_dram):
    signals = Signals(nc)
    sem = lambda n: signals(f"scan_{n}")
    NH, PIECES = N_ST // 2, 8
    NP = N_ST // PIECES
    W = NH * SEQ
    SLOTS = 4
    w_in = sem("next_weight_in")
    b_in, c_in = [sem("b_in0"), sem("b_in1")], [sem("c_in0"), sem("c_in1")]
    heads_zero, inflow_in, decayed, u_ready = sem("heads_zero"), sem("inflow"), sem("decayed"), sem("u_ready")
    scanned, weighted, slots_free, finished, skip_ready = sem("scanned"), sem("weighted"), sem("slots_free"), sem("finished"), sem("skip_ready")
    u, xd = ([place(f"{n}{i}", [P, SEQ]) for i in range(2)] for n in ("u", "xd"))
    slot = [M.scratch32[:, i * W:(i + 1) * W] for i in range(SLOTS)]
    decay = [M.ps[:, 2 + i, :] for i in range(2)]
    by_state = lambda ap: ap.rearrange("p (n t) -> p n t", n=NP)
    state = [M.ps[:, 4 + i, :] for i in range(4)]
    ident = M.const[:, C_ID:C_ID + P]
    ps_y = [M.ps[:, i, 0:SEQ] for i in range(2)]
    flat_x = x_conv[:, :, :].rearrange("p b c -> p (b c)")
    flat_dt = dt[:, :, :].rearrange("p b c -> p (b c)")

    def pairs(eng, body):
        body(0, 0)
        with eng.Fori(1, KI // 2) as j:
            body(0, j)
        with eng.Fori(1, BATCH) as b:
            with eng.Fori(0, KI // 2) as j:
                body(b, j)

    with nc.Block() as block:
        @block.sync
        def _(sp):
            def load(b):
                for h in range(2):
                    at_least(sp, inflow_in, b * 2 * KI - 1 + h)
                    sp.dma_start(bm[:, h * NH:(h + 1) * NH, :],
                                 bc_dram[bass.ds(b, 1), h * NH:(h + 1) * NH, :].broadcast_to((P, NH, SEQ))).then_inc(b_in[h], 16)
                for h in range(2):
                    at_least(sp, weighted, b * PIECES * KI - 4 + 4 * h)
                    sp.dma_start(cm[:, h * NH:(h + 1) * NH, :],
                                 bc_dram[bass.ds(b, 1), N_ST + h * NH:N_ST + (h + 1) * NH, :].broadcast_to((P, NH, SEQ))).then_inc(c_in[h], 16)
            sp.dma_start(w_next[:, :, :], w_next_dram).then_inc(w_in, 16)
            with sp.Fori(1, BATCH) as b:
                load(b)
            sp.wait_ge(w_in, 16)

        @block.gpsimd
        def _(pool):
            pool.sem_inc(slots_free, SLOTS)

            def body(b, j):
                for r in range(2):
                    s = b * KI + j * 2 + r
                    at_least(pool, inflow_in, s * 2 - 2)
                    nc.gpsimd.tensor_tensor(u[r][:, :], flat_dt[:, cols(s, SEQ)], flat_x[:, cols(s, SEQ)],
                                            ALU.mult).then_inc(u_ready, 1)
                    pool.wait_ge(u_ready, s + 1)
                    for h in range(2):
                        at_least(pool, b_in[h], b * 16)
                        pool.wait_ge(slots_free, s * 2 + h + 1)
                        nc.gpsimd.tensor_tensor(slot[2 * r + h].rearrange("p (n t) -> p n t", n=NH),
                                                bm[:, h * NH:(h + 1) * NH, :],
                                                u[r][:, :].rearrange("p (a t) -> p a t", a=1).broadcast_to((P, NH, SEQ)),
                                                ALU.mult).then_inc(inflow_in, 1)
            pairs(pool, body)

        @block.scalar
        def _(act):
            act.wait_ge(heads_zero, 2)

            def finish(s, r):
                nc.scalar.activation(flat_x[:, cols(s, SEQ)], ps_y[r], ACT.Copy).then_inc(finished, 1)

            def body(b, j):
                for r in range(2):
                    s = b * KI + j * 2 + r
                    nc.scalar.activation(xd[r][:, :], flat_x[:, cols(s, SEQ)], ACT.Identity,
                                         scale=M.vec[:, bass.ds(s + V_D, 1)]).then_inc(skip_ready, 1)
                    for c in range(PIECES):
                        last = c == 4 and not (isinstance(s, int) and s == 0)
                        if last:
                            act.wait_ge(slots_free, s * 2 + SLOTS)
                        at_least(act, scanned, s * PIECES + c - 1)
                        for n in range(NP):
                            ins = nc.scalar.activation(by_state(decay[c % 2])[:, n, 1:SEQ], flat_dt[:, bass.ds(s * SEQ + 1, SEQ - 1)], ACT.Exp,
                                                       scale=M.vec[:, bass.ds(s * N_ST + V_AL + c * NP + n, 1)])
                        ins.then_inc(decayed, 1)
                        if last:
                            finish(s - 1, 1 - r)
            pairs(act, body)
            act.wait_ge(slots_free, BATCH * KI * 2 + SLOTS)
            finish(BATCH * KI - 1, 1)

        @block.vector
        def _(dve):
            def part(r, c):
                return slot[2 * r + c // 4][:, (c % 4) * NP * SEQ:(c % 4 + 1) * NP * SEQ]

            def weigh(b, s, r, c):
                dve.wait_ge(scanned, s * PIECES + c + 1)
                if c % 4 == 0:
                    at_least(dve, c_in[c // 4], b * 16)
                nc.vector.tensor_tensor(part(r, c), state[c % 4], cm[:, c * NP:(c + 1) * NP, :].rearrange("p n t -> p (n t)"),
                                        ALU.mult).then_inc(weighted, 1)

            def body(b, j):
                for r in range(2):
                    s = b * KI + j * 2 + r
                    for c in range(PIECES):
                        dve.wait_ge(decayed, s * PIECES + c + 1)
                        if c % 4 == 0:
                            dve.wait_ge(inflow_in, s * 2 + c // 4 + 1)
                        at_least(dve, weighted, s * PIECES + c - 3)
                        nc.vector.tensor_tensor_scan(state[c % 4], decay[c % 2], part(r, c), 0.0, ALU.mult, ALU.add).then_inc(scanned, 1)
                        if c > 0:
                            weigh(b, s, r, c - 1)
                        elif r > 0:
                            weigh(b, s - 1, 1 - r, PIECES - 1)
                        elif not (isinstance(s, int) and s == 0):
                            weigh(None, s - 1, 1 - r, PIECES - 1)
            for d in decay:
                nc.vector.memset(by_state(d)[:, :, 0:1], 0.0).then_inc(heads_zero, 1)
            dve.wait_ge(heads_zero, 2)
            pairs(dve, body)
            weigh(None, BATCH * KI - 1, 1, PIECES - 1)

        @block.tensor
        def _(pe):
            def body(b, j):
                for r in range(2):
                    s = b * KI + j * 2 + r
                    at_least(pe, finished, s - 1)
                    pe.wait_ge(skip_ready, s + 1)
                    nc.tensor.matmul(ps_y[r], ident, xd[r][:, :], start=True, stop=False)
                    for h in range(2):
                        for n in range(NH):
                            if n % NP == 0:
                                pe.wait_ge(weighted, s * PIECES + 4 * h + n // NP + 1)
                            mm = nc.tensor.matmul(ps_y[r], ident, slot[2 * r + h][:, n * SEQ:(n + 1) * SEQ],
                                                  start=False, stop=(h == 1 and n == NH - 1))
                        mm.then_inc(slots_free, 1)
            pairs(pe, body)
    signals.close()


def key_value_phase(nc, M, place, spare, raw, K, V, ch, cl, w_kv, w_v, wq_raw, wqh, wql, wq):
    signals = Signals(nc)
    sem = lambda n: signals(f"kv_{n}")
    R = ROPE_HALF
    NF, VC = 3 * KM, GROUPS * HD
    BUFS = 4
    kinds = ["latent"] * KM + ["rotated", "plain"] * KM
    items = [("step", f) for f in range(NF)]
    for k in range(KM):
        items.insert(6 + 3 * k, ("values", k))
    RING = 3
    raw_in, q_in = [sem(f"raw_in{i}") for i in range(RING)], sem("query_weights_in")
    q_hi, q_lo = sem("query_weights_hi"), sem("query_weights_lo")
    w_hi, w_lo, prod = sem("w_hi"), sem("w_lo"), sem("products")
    plain_act, plain_dve, v_kept = sem("plain_kept_act"), sem("plain_kept_dve"), sem("values_kept")
    c_hi, c_lo = sem("c_hi"), sem("c_lo")
    turned_done, sine_done, cosine_done, rotated = sem("turned"), sem("sine"), sem("cosine"), sem("rotated")
    rows, total, coeff_done = sem("diff_rows"), sem("diff_total"), sem("coeff_done")
    vwh, vwl = place("vwh", [P, KM, VC], F32R), place("vwl", [P, KM, VC], F32R)
    wh = [place(f"wh{i}", [P, KM * P], F32R) for i in range(RING)]
    wl = [place(f"wl{i}", [P, KM * P], F32R) for i in range(RING)]
    turned = [spare(f"turned{i}", [P, TOK]) for i in range(2)]
    direct = [spare(f"direct{i}", [P, TOK]) for i in range(2)]
    table = lambda c: M.const[:, c:c + SEQ].rearrange("p (b t) -> p b t", b=1).broadcast_to((P, BATCH, SEQ))
    ps = [M.ps[:, 2 * s:2 * s + 2, :].rearrange("p a c -> p (a c)") for s in range(BUFS)]
    item_of = {it: n for n, it in enumerate(items)}

    def weight(it):
        kind, i = items[it]
        if kind == "step":
            return raw[it % RING][:, 0:KM * P], wh[i % RING][:, :], wl[i % RING][:, :]
        return raw[it % RING][:, :], vwh[:, i, :], vwl[:, i, :]

    with nc.Block() as block:
        @block.sync
        def _(sp):
            for it, (kind, i) in enumerate(items):
                if it < RING:
                    continue
                sp.wait_ge(w_lo, it - RING + 1)
                src, dst = (w_kv[:, i * KM * P:(i + 1) * KM * P], raw[it % RING][:, 0:KM * P]) if kind == "step" else (w_v[:, i, :], raw[it % RING][:, :])
                sp.dma_start(dst, src).then_inc(raw_in[it % RING], 16)
            sp.wait_ge(w_lo, len(items))
            sp.wait_ge(prod, NF)
            sp.dma_start(wq_raw[:, :], wq[:, 0:KM * HPG * HD]).then_inc(q_in, 16)
            sp.wait_ge(q_in, 16)

        @block.tensor
        def _(pe):
            def psum_free(f):
                g = f - BUFS
                if g < 0:
                    if f == BUFS - 1:
                        pe.wait_ge(coeff_done, 1)
                    return
                if g >= NF:
                    pe.wait_ge(v_kept, g - NF + 1)
                elif kinds[g] == "latent":
                    pe.wait_ge(c_lo, g + 1)
                elif kinds[g] == "rotated":
                    pe.wait_ge(cosine_done, (g - KM) // 2 + 1)
                else:
                    pe.wait_ge(plain_act, (g - KM) // 2 + 1)
                    pe.wait_ge(plain_dve, (g - KM) // 2 + 1)

            pe.wait_ge(rows, 1)
            nc.tensor.matmul(M.ps[:, 7, 0:3], M.ones[:, :], M.row_sums[:, :], start=True, stop=True).then_inc(total, 1)
            for f in range(NF):
                it = item_of[("step", f)]
                pe.wait_ge(w_hi, it + 1)
                pe.wait_ge(w_lo, it + 1)
                psum_free(f)
                if kinds[f] == "plain":
                    pe.wait_ge(c_lo, KM)
                xh, xl = (ch, cl) if kinds[f] == "plain" else (M.xh, M.xl)
                for k in range(KM):
                    for w, x in ((wh, xh), (wh, xl), (wl, xh)):
                        for h in range(2):
                            mm = nc.tensor.matmul(ps[f % BUFS][:, h * HALF:(h + 1) * HALF], w[f % RING][:, k * P:(k + 1) * P],
                                                  x[:, k, h * HALF:(h + 1) * HALF],
                                                  start=(k == 0 and w is wh and x is xh), stop=(k == KM - 1 and w is wl))
                mm.then_inc(prod, 1)
            pe.wait_ge(w_lo, len(items))
            for t in range(TT):
                f = NF + t
                psum_free(f)
                for k in range(KM):
                    for c, w in ((ch, vwh), (ch, vwl), (cl, vwh)):
                        for h in range(2):
                            mm = nc.tensor.matmul(ps[f % BUFS][:, h * HALF:(h + 1) * HALF], c[:, k, t * P:(t + 1) * P],
                                                  w[:, k, h * HALF:(h + 1) * HALF],
                                                  start=(k == 0 and w is vwh and c is ch), stop=(k == KM - 1 and c is cl))
                mm.then_inc(prod, 1)

        @block.scalar
        def _(act):
            def high(it):
                kind, i = items[it]
                at_least(act, raw_in[it % RING], it // RING * 16)
                if kind == "step":
                    at_least(act, prod, i - RING + 1)
                src, hi, _ = weight(it)
                nc.scalar.activation(hi, src, ACT.Copy).then_inc(w_hi, 1)

            def evacuate(f):
                act.wait_ge(prod, f + 1)
                src = ps[f % BUFS]
                if f >= NF:
                    if f == NF + TT // 2:
                        act.wait_ge(rotated, 4 * KM)
                    nc.scalar.activation(V[:, f - NF, :], src, ACT.Copy).then_inc(v_kept, 1)
                elif kinds[f] == "latent":
                    nc.scalar.activation(ch[:, f, :], src, ACT.Copy).then_inc(c_hi, 1)
                elif kinds[f] == "rotated":
                    j = (f - KM) // 2
                    at_least(act, rotated, 4 * (j - 1))
                    for q in range(4):
                        o = (q ^ 1) * R
                        nc.scalar.activation(turned[j % 2][q * R:(q + 1) * R, :], src[o:o + R, :], ACT.Copy).then_inc(turned_done, 1)
                else:
                    j = (f - KM) // 2
                    nc.scalar.activation(K[R:2 * R, 2 * j, :], src[0:R, :], ACT.Copy)
                    nc.scalar.activation(K[3 * R:4 * R, 2 * j, :], src[R:2 * R, :], ACT.Copy).then_inc(plain_act, 1)

            done = 0
            for f in range(NF + TT):
                while done < len(items) and (done <= (item_of[("step", f + 2)] if f + 2 < NF else len(items) - 1)):
                    high(done)
                    done += 1
                evacuate(f)
                if f == NF + TT // 2:
                    act.wait_ge(q_in, 16)
                    nc.scalar.activation(wqh[:, :, :].rearrange("p k o -> p (k o)"), wq_raw[:, :], ACT.Copy).then_inc(q_hi, 1)

        @block.gpsimd
        def _(pool):
            def low(it):
                pool.wait_ge(w_hi, it + 1)
                src, hi, lo = weight(it)
                nc.gpsimd.tensor_tensor(lo, src, f32(hi), ALU.subtract).then_inc(w_lo, 1)

            done = 0
            for f in range(NF):
                while done < len(items) and (done <= (item_of[("step", f + 2)] if f + 2 < NF else len(items) - 1)):
                    low(done)
                    done += 1
                if kinds[f] == "rotated":
                    j = (f - KM) // 2
                    pool.wait_ge(turned_done, 4 * j + 4)
                    nc.gpsimd.tensor_tensor(by_batch(turned[j % 2][:, :]), by_batch(turned[j % 2][:, :]), table(C_SINK),
                                            ALU.mult).then_inc(sine_done, 1)
            pool.wait_ge(q_hi, 1)
            nc.gpsimd.tensor_tensor(wql[:, :, :].rearrange("p k o -> p (k o)"), wq_raw[:, :],
                                    f32(wqh[:, :, :].rearrange("p k o -> p (k o)")), ALU.subtract).then_inc(q_lo, 1)

        @block.vector
        def _(dve):
            def add_turned(j):
                dve.wait_ge(cosine_done, j + 1)
                dve.wait_ge(sine_done, j + 1)
                for q in range(4):
                    rows, to = slice(q * R, (q + 1) * R), (q % 2) * 2 * R
                    nc.vector.tensor_tensor(K[to:to + R, 2 * j + q // 2, :], direct[j % 2][rows, :], turned[j % 2][rows, :],
                                            ALU.add).then_inc(rotated, 1)

            nc.vector.tensor_reduce(M.row_sums[:, :], M.diff_sums[:, :, :], AX_X, ALU.add).then_inc(rows, 1)
            dve.wait_ge(total, 1)
            nc.vector.tensor_scalar(M.coeff[:, :], M.ps[:, 7, 0:3], 1.0 / N_DIFF, None, ALU.mult).then_inc(coeff_done, 1)
            for f in range(NF):
                src = ps[f % BUFS]
                if kinds[f] == "latent":
                    dve.wait_ge(c_hi, f + 1)
                    nc.vector.tensor_tensor(cl[:, f, :], src, f32(ch[:, f, :]), ALU.subtract).then_inc(c_lo, 1)
                elif kinds[f] == "rotated":
                    j = (f - KM) // 2
                    dve.wait_ge(turned_done, 4 * j + 4)
                    at_least(dve, rotated, 4 * (j - 1))
                    nc.vector.tensor_tensor(by_batch(direct[j % 2][:, :]), by_batch(src), table(C_COSK), ALU.mult).then_inc(cosine_done, 1)
                else:
                    j = (f - KM) // 2
                    dve.wait_ge(prod, f + 1)
                    nc.vector.tensor_copy(K[R:2 * R, 2 * j + 1, :], src[2 * R:3 * R, :])
                    nc.vector.tensor_copy(K[3 * R:4 * R, 2 * j + 1, :], src[3 * R:4 * R, :]).then_inc(plain_dve, 1)
                    add_turned(j)
            dve.wait_ge(rotated, 4 * KM)
    signals.close()


def attention_phase(nc, M, place, raw, wqh, wql, K, V, acc, wq, wo):
    signals = Signals(nc)
    sem = lambda n: signals(f"att_{n}")
    U = GROUPS * BATCH
    SCALE = float(HD) ** -0.5
    raw_in, wq_hi, wq_lo, wo_hi, wo_lo = sem("raw_in"), sem("wq_hi"), sem("wq_lo"), sem("wo_hi"), sem("wo_lo")
    q_prod, q_turned, q_sine, q_cosine, q_done = (sem("q_prod"), sem("q_turned"), sem("q_sine"), sem("q_cosine"), sem("q_done"))
    scored, masked, maxed, neg_max, exped, inverse, normed = (sem("scored"), sem("masked"), sem("maxed"), sem("neg_max"),
                                                              sem("exped"), sem("inverse"), sem("normed"))
    flipped, p_kept_act, p_kept_dve, v_here, summed, o_hi, o_lo, o_prod, added = (
        sem("flipped"), sem("p_kept_act"), sem("p_kept_dve"), sem("v_here"), sem("summed"), sem("o_hi"), sem("o_lo"),
        sem("o_prod"), sem("added"))
    zeroed = sem("acc_zeroed")
    QC = HPG * HD
    woh, wol = place("woh", [P, HPG, DM], F32R), place("wol", [P, HPG, DM], F32R)
    q = place("q", [P, HPG, SEQ])
    direct, turned = place("direct", [P, HPG * SEQ]), place("turned", [P, HPG * SEQ])
    pa, pb = place("pa", [P, HPG, P]), place("pb", [P, HPG, SEQ])
    pt = place("pt", [P, 3, HALF])
    oh, ol = place("oh", [P, QT, HALF], F32R), place("ol", [P, QT, HALF], F32R)
    vs = place("vs", [P, QT, HD])
    mx, nm, sums, inv = (place(n, [P, 8]) for n in ("mx", "nm", "sums", "inv"))
    ident = M.const[:, C_ID:C_ID + P]
    ps_q = M.ps[:, 0:2, :].rearrange("p a c -> p (a c)")
    s0 = M.ps[:, 2, :].rearrange("p (h k) -> p h k", h=HPG)
    s1 = M.ps[:, 3:5, :].rearrange("p a (h k) -> p (a h) k", k=SEQ)
    X = [M.ps[:, 5 + i, :] for i in range(3)]
    flat = lambda t: t[:, :, :].rearrange("p a c -> p (a c)")
    heads = lambda ap: ap.rearrange("p (h t) -> p h t", h=HPG)
    over_heads = lambda c, w: M.const[:, c:c + w].rearrange("p (h t) -> p h t", h=1).broadcast_to((P, HPG, w))

    def groups(eng, body):
        for b in range(BATCH):
            body(0, b)
        with eng.Fori(1, GROUPS - 1) as g:
            for b in range(BATCH):
                body(g, b)
        for b in range(BATCH):
            body(GROUPS - 1, b)

    def more(g, b):
        return not (isinstance(g, int) and g == GROUPS - 1 and b == BATCH - 1)

    def after(g, b):
        return (g, b + 1) if b < BATCH - 1 else (g + 1, 0)

    with nc.Block() as block:
        @block.sync
        def _(sp):
            def load(g):
                if not isinstance(g, int):
                    sp.wait_ge(wo_lo, g)
                    sp.dma_start(raw[:, :], wq[:, cols(g, KM * QC)]).then_inc(raw_in, 16)
                at_least(sp, wq_lo, g)
                sp.dma_start(raw[:, :], wo[:, cols(g, HPG * DM)]).then_inc(raw_in, 16)
            load(0)
            with sp.Fori(1, GROUPS) as g:
                load(g)

        @block.tensor
        def _(pe):
            def queries(g, b):
                v = g * BATCH + b
                if b == 0:
                    at_least(pe, wq_hi, g)
                    at_least(pe, wq_lo, g)
                at_least(pe, q_turned, v)
                at_least(pe, q_cosine, v)
                for h in range(HPG):
                    for k in range(KM):
                        for w, x in ((wqh, M.xh), (wqh, M.xl), (wql, M.xh)):
                            mm = nc.tensor.matmul(ps_q[:, h * SEQ:(h + 1) * SEQ], w[:, k, h * HD:(h + 1) * HD],
                                                  x[:, k, b * SEQ:(b + 1) * SEQ],
                                                  start=(k == 0 and w is wqh and x is M.xh), stop=(k == KM - 1 and w is wql))
                mm.then_inc(q_prod, 1)

            def scores(g, b):
                v = g * BATCH + b
                pe.wait_ge(q_done, v + 1)
                at_least(pe, exped, v)
                keys = K[:, bass.ds(g, 1), :].rearrange("p a t -> p (a t)")
                for h in range(HPG):
                    nc.tensor.matmul(s0[:, h, :], q[:, h, 0:P], keys[:, b * SEQ:b * SEQ + P], start=True, stop=True)
                for h in range(HPG):
                    mm = nc.tensor.matmul(s1[:, h, :], q[:, h, P:SEQ], keys[:, b * SEQ:(b + 1) * SEQ], start=True, stop=True)
                mm.then_inc(scored, 1)

            def output(g, b):
                v = g * BATCH + b
                if b == 0:
                    pe.wait_ge(wo_hi, g + 1)
                    pe.wait_ge(wo_lo, g + 1)
                pe.wait_ge(o_lo, v * 2 + 2)
                for t in range(QT):
                    for h in range(HPG):
                        part = slice(h * P, (h + 1) * P)
                        nc.tensor.matmul(X[t], oh[:, t, part], woh[:, h, :], start=(h == 0), stop=False)
                        nc.tensor.matmul(X[t], oh[:, t, part], wol[:, h, :], start=False, stop=False)
                        mm = nc.tensor.matmul(X[t], ol[:, t, part], woh[:, h, :], start=False, stop=(h == HPG - 1))
                    mm.then_inc(o_prod, 1)

            def attend(g, b):
                v = g * BATCH + b
                pe.wait_ge(normed, v + 1)
                for h in range(HPG):
                    mm = nc.tensor.transpose(X[2][:, h * P:(h + 1) * P], pa[:, h, :], ident)
                mm.then_inc(flipped, 1)
                for i in range(QT):
                    at_least(pe, added, v * 2 - 1 + i)
                    for h in range(HPG):
                        mm = nc.tensor.transpose(X[i][:, h * P:(h + 1) * P], pb[:, h, i * P:(i + 1) * P], ident)
                    mm.then_inc(flipped, 1)
                pe.wait_ge(v_here, v + 1)
                pe.wait_ge(p_kept_act, v * 2 + 1)
                nc.tensor.matmul(X[2], vs[:, 0, :], pt[:, 0, :], start=True, stop=True).then_inc(summed, 1)
                pe.wait_ge(p_kept_dve, v + 1)
                nc.tensor.matmul(X[0], vs[:, 0, :], pt[:, 1, :], start=True, stop=False)
                pe.wait_ge(p_kept_act, v * 2 + 2)
                nc.tensor.matmul(X[0], vs[:, 1, :], pt[:, 2, :], start=False, stop=True).then_inc(summed, 1)

            def body(g, b):
                if more(g, b):
                    queries(*after(g, b))
                if b > 0:
                    output(g, b - 1)
                elif not (isinstance(g, int) and g == 0):
                    output(g - 1, BATCH - 1)
                attend(g, b)
                if more(g, b):
                    scores(*after(g, b))

            queries(0, 0)
            scores(0, 0)
            groups(pe, body)
            output(GROUPS - 1, BATCH - 1)

        @block.scalar
        def _(act):
            def turn(g, b):
                v = g * BATCH + b
                act.wait_ge(q_prod, v + 1)
                at_least(act, q_done, v)
                nc.scalar.activation(turned[0:64, :], ps_q[64:128, :], ACT.Copy)
                nc.scalar.activation(turned[64:128, :], ps_q[0:64, :], ACT.Copy).then_inc(q_turned, 1)

            def exps(g, b):
                v = g * BATCH + b
                act.wait_ge(neg_max, v + 1)
                at_least(act, flipped, v * 3)
                at_least(act, inverse, v)
                for h in range(HPG):
                    nc.scalar.activation(pa[:, h, :], s0[:, h, :], ACT.Exp, bias=nm[:, h:h + 1], scale=SCALE,
                                         accum_out=sums[:, h:h + 1])
                for h in range(HPG):
                    ins = nc.scalar.activation(pb[:, h, :], s1[:, h, :], ACT.Exp, bias=nm[:, 4 + h:5 + h], scale=SCALE,
                                               accum_out=sums[:, 4 + h:5 + h])
                ins.then_inc(exped, 1)

            def query_weights(g):
                at_least(act, raw_in, g * 32)
                at_least(act, q_prod, g * BATCH)
                nc.scalar.activation(flat(wqh), raw[:, :], ACT.Copy).then_inc(wq_hi, 1)

            def output_weights(g):
                act.wait_ge(raw_in, g * 32 + 16)
                at_least(act, o_prod, g * BATCH * QT)
                nc.scalar.activation(flat(woh), raw[:, :], ACT.Copy).then_inc(wo_hi, 1)

            def body(g, b):
                v = g * BATCH + b
                if more(g, b):
                    turn(*after(g, b))
                if b == 2 and not (isinstance(g, int) and g == GROUPS - 1):
                    query_weights(g + 1)
                at_least(act, summed, v * 2)
                act.wait_ge(flipped, v * 3 + 1)
                nc.scalar.activation(pt[:, 0, :], X[2], ACT.Copy).then_inc(p_kept_act, 1)
                act.wait_ge(flipped, v * 3 + 3)
                nc.scalar.activation(pt[:, 2, :], X[1], ACT.Copy).then_inc(p_kept_act, 1)
                at_least(act, o_prod, v * QT)
                for t, x in ((0, X[2]), (1, X[0])):
                    act.wait_ge(summed, v * 2 + t + 1)
                    nc.scalar.activation(oh[:, t, :], x, ACT.Copy).then_inc(o_hi, 1)
                if b == 0:
                    output_weights(g)
                if more(g, b):
                    exps(*after(g, b))

            turn(0, 0)
            exps(0, 0)
            groups(act, body)

        @block.gpsimd
        def _(pool):
            def sine(g, b):
                v = g * BATCH + b
                pool.wait_ge(q_turned, v + 1)
                nc.gpsimd.tensor_tensor(heads(turned[:, :]), heads(turned[:, :]), over_heads(C_SIN, SEQ), ALU.mult).then_inc(q_sine, 1)

            def query_weights(g):
                pool.wait_ge(wq_hi, g)
                nc.gpsimd.tensor_tensor(flat(wql), raw[:, :], f32(flat(wqh)), ALU.subtract).then_inc(wq_lo, 1)

            def output_weights(g):
                pool.wait_ge(wo_hi, g + 1)
                nc.gpsimd.tensor_tensor(flat(wol), raw[:, :], f32(flat(woh)), ALU.subtract).then_inc(wo_lo, 1)

            def body(g, b):
                if more(g, b):
                    sine(*after(g, b))
                if b == 2 and not (isinstance(g, int) and g == GROUPS - 1):
                    query_weights(g + 1)
                if b == 0:
                    output_weights(g)

            sine(0, 0)
            groups(pool, body)

        @block.vector
        def _(dve):
            def cosine(g, b):
                v = g * BATCH + b
                dve.wait_ge(q_turned, v + 1)
                nc.vector.tensor_tensor(heads(direct[:, :]), heads(ps_q), over_heads(C_COS, SEQ), ALU.mult).then_inc(q_cosine, 1)

            def rotate(g, b):
                v = g * BATCH + b
                dve.wait_ge(q_cosine, v + 1)
                dve.wait_ge(q_sine, v + 1)
                at_least(dve, scored, v)
                nc.vector.tensor_tensor(flat(q), direct[:, :], turned[:, :], ALU.add).then_inc(q_done, 1)

            def maxima(g, b):
                v = g * BATCH + b
                dve.wait_ge(scored, v + 1)
                nc.vector.tensor_tensor(s0, s0, over_heads(C_MASK, P), ALU.add).then_inc(masked, 1)
                nc.vector.tensor_tensor(s1[:, :, P:SEQ], s1[:, :, P:SEQ], over_heads(C_MASK, P), ALU.add).then_inc(masked, 1)
                dve.wait_ge(masked, v * 2 + 2)
                at_least(dve, exped, v)
                nc.vector.tensor_reduce(mx[:, 0:4], s0, AX_X, ALU.max).then_inc(maxed, 1)
                nc.vector.tensor_reduce(mx[:, 4:8], s1, AX_X, ALU.max).then_inc(maxed, 1)
                dve.wait_ge(maxed, v * 2 + 2)
                nc.vector.tensor_scalar(nm[:, :], mx[:, :], -SCALE, None, ALU.mult).then_inc(neg_max, 1)

            def probabilities(g, b):
                v = g * BATCH + b
                dve.wait_ge(exped, v + 1)
                at_least(dve, normed, v)
                nc.vector.reciprocal(inv[:, :], sums[:, :]).then_inc(inverse, 1)
                dve.wait_ge(inverse, v + 1)
                for h in range(HPG):
                    nc.vector.tensor_scalar(pa[:, h, :], pa[:, h, :], inv[:, h:h + 1], None, ALU.mult)
                for h in range(HPG):
                    ins = nc.vector.tensor_scalar(pb[:, h, :], pb[:, h, :], inv[:, 4 + h:5 + h], None, ALU.mult)
                ins.then_inc(normed, 1)

            def accumulate(v, b):
                for t in range(QT):
                    dve.wait_ge(o_prod, v * QT + t + 1)
                    nc.vector.tensor_tensor(acc[:, QT * b + t, :], X[t], acc[:, QT * b + t, :], ALU.add).then_inc(added, 1)

            def body(g, b):
                v = g * BATCH + b
                at_least(dve, summed, v * 2)
                nc.vector.tensor_copy(vs[:, :, :], V[:, QT * b:QT * b + QT, cols(g, HD)]).then_inc(v_here, 1)
                if more(g, b):
                    cosine(*after(g, b))
                if not (isinstance(v, int) and v == 0):
                    accumulate(v - 1, (b - 1) % BATCH)
                dve.wait_ge(flipped, v * 3 + 2)
                nc.vector.tensor_copy(pt[:, 1, :], X[0]).then_inc(p_kept_dve, 1)
                if more(g, b):
                    rotate(*after(g, b))
                for t, x in ((0, X[2]), (1, X[0])):
                    dve.wait_ge(o_hi, v * 2 + t + 1)
                    nc.vector.tensor_tensor(ol[:, t, :], x, f32(oh[:, t, :]), ALU.subtract).then_inc(o_lo, 1)
                if more(g, b):
                    maxima(*after(g, b))
                    probabilities(*after(g, b))

            nc.vector.memset(flat(acc), 0.0).then_inc(zeroed, 1)
            dve.wait_ge(zeroed, 1)
            cosine(0, 0)
            rotate(0, 0)
            maxima(0, 0)
            probabilities(0, 0)
            groups(dve, body)
            accumulate(U - 1, BATCH - 1)
    signals.close()


def program(nc, D, out, stop_after=None, taps=None):
    M = type("Memory", (), {})()
    M.ps = nc.alloc_psum_tensor("psum", [P, 8, HALF], F32)
    base = (nc.sbuf_base + 31) // 32 * 32
    end = nc.sbuf_usable_end // 32 * 32
    resident = Places(nc, "res", base, base + 6 * KB)
    M.const = resident("const", [P, C_END])
    M.ones = resident("ones", [P, P])
    M.half = resident("half", [P, 1])
    M.diff_sums = resident("diff_sums", [P, 3, N_SUMS])
    M.row_sums = resident("row_sums", [P, 3])
    M.coeff = resident("coeff", [P, 3])
    z = resident.at
    at = lambda tag, kb: Places(nc, tag, z + kb * KB, end)
    M.x = at("tok", 0)("x", [P, TT, DM])
    opnd = at("opnd", 16)
    M.xh, M.xl = opnd("xh", [P, KM, TOK], F32R), opnd("xl", [P, KM, TOK], F32R)
    M.scratch32 = at("scratch", 16)("s", [P, 8 * TOK])

    mamba = at("ssm", 48)
    x_conv = mamba("x_conv", [P, BATCH, KI * SEQ])
    gate = mamba("gate", [P, BATCH, KI * SEQ])
    dt = mamba("dt", [P, BATCH, KI * SEQ])
    M.vec = mamba("vec", [P, V_END])
    free = (mamba.at - z + KB - 1) // KB
    par = at("par", free)
    wx, wdt, block_mean = par("wx", [P, KI, NX]), par("wdt", [P, D_IN]), par("block_mean", [NX, NX])
    ssm_in = at("in", free + 8)
    in_raw = [ssm_in(f"raw{i}", [P, 2 * KM * P]) for i in range(2)]
    w_res = at("w_out", free)("w", [P, KI, DM])
    scan_places = at("scan", free + 19)
    bm, cm = scan_places("bm", [P, N_ST, SEQ]), scan_places("cm", [P, N_ST, SEQ])
    top = 190
    gu = at("gu", top)
    gu_raw = [gu(f"raw{i}", [P, 2 * KM * P], I32) for i in range(2)]
    sc = [gu("gate_s", [P, F0]), gu("up_s", [P, F0])]
    kv = Places(nc, "kvr", end - 12 * KB, end)
    kv_raw = [kv(f"raw{i}", [P, GROUPS * HD]) for i in range(3)]
    query = at("query", 176)
    wq_raw, wqh, wql = query("raw", [P, KM * HPG * HD]), query("wqh", [P, KM, HPG * HD], F32R), query("wql", [P, KM, HPG * HD], F32R)
    RC = (2 * KM * P + DM)
    mlp1 = at("mlp1", 48)
    hidden1, down1 = mlp1("hidden", [P, F1, TOK]), mlp1("down", [P, F1, DM])
    mlp_raw, mlp_base = [mlp1(f"raw{i}", [P, RC]) for i in range(2)], [mlp1(f"base{i}", [P, RC]) for i in range(2)]

    def step_weights(buffers, dram, width):
        return [(b[:, 0:width], dram[:, i * width:(i + 1) * width]) for i, b in enumerate(buffers)]

    load_inputs(nc, M, D["x"], D["const"])
    if stop_after == "load": return M
    tokens = D["x"].rearrange("(t p) c -> p t c", p=P)
    finish_phase(nc, "n0", M, at("n0", free), 0, norm_only=True,
                 x_loads=[(t, M.x[:, t:u, :], tokens[:, t:u, :]) for t, u in ((1, 2), (2, 4), (4, TT))],
                 ahead=step_weights(in_raw, D["w_in"], 2 * KM * P) + [(M.vec[:, :], D["vec"]), (M.const[:, P:], D["const"][:, P:])])
    if stop_after == "n0": return M
    widen_phase(nc, "in", M, ssm_in, KI, "ssm", D["w_in"], x_conv=x_conv, gate=gate, raw=in_raw,
                ahead=[(wx[:, :, :], D["w_x"]), (wdt[:, :], D["w_dt"]), (block_mean[:, :], D["block_mean"])])
    M.x_conv, M.gate, M.dt = x_conv, gate, dt
    if stop_after == "in": return M
    ssm_parameters(nc, M, par, x_conv, dt, D["bc"], wx, wdt, block_mean, bm, cm)
    if stop_after == "par": return M
    scan_phase(nc, M, scan_places, x_conv, dt, D["bc"], bm, cm, w_res, D["w_out"])
    if stop_after == "scan": return M
    tile_of = lambda a: (lambda t, s: a[:, t // QT, :].rearrange("p (d c) -> p d c", d=KI)[:, :, s * P:(s + 1) * P])
    finish_phase(nc, "fa", M, Stretches(nc, (z + 112 * KB, z + free * KB), (z + (free + 16) * KB, z + top * KB), (gu.at, end)), KI,
                 hidden=tile_of(x_conv), gate=tile_of(gate), w_raw=w_res,
                 ahead=step_weights(gu_raw, D["w_gu"], 2 * KM * P) + [(sc[0][:, :], D["gate_s"]), (sc[1][:, :], D["up_s"])])
    if stop_after == "fa": return M

    mlp = at("mlp0", 48)
    hidden = mlp("hidden", [P, F0, TOK])
    down = mlp("down", [P, F0, DM], I32)
    scale_row = mlp("down_s", [P, DM])
    mlp0 = mlp.at
    widen_phase(nc, "mi", M, Places(nc, "mi", mlp0, z + top * KB), F0, "int", D["w_gu"], hidden=hidden, scales=sc, raw=gu_raw,
                ahead=[(down[:, :, :], D["w_down"]), (scale_row[:, :], D["down_s"].broadcast_to((P, DM)))],
                diff=dict(pairs=[(D["dw1"], D["dm1"]), (D["dw3"], D["dm3"]), (D["dw2"], D["dm2"])], sums=M.diff_sums))
    plain = lambda a: (lambda t, s: a[:, :, t * P:(t + 1) * P])
    finish_phase(nc, "fb", M, Places(nc, "fb", mlp0, end - 12 * KB), F0, hidden=plain(hidden), w_raw=down, out_scale=scale_row,
                 ahead=step_weights(kv_raw, D["w_kv"], KM * P))
    if stop_after == "fb": return M

    att = at("att", 48)
    ch, cl = att("ch", [P, KM, TOK], F32R), att("cl", [P, KM, TOK], F32R)
    K, V = att("k", [P, GROUPS, TOK]), att("v", [P, TT, GROUPS * HD])
    M.K, M.V, M.ch = K, V, ch
    key_value_phase(nc, M, at("kv", 144), at("kvv", 128), kv_raw, K, V, ch, cl, D["w_kv"], D["w_upv"],
                    wq_raw, wqh, wql, D["w_q"])
    if stop_after == "kv": return M
    acc = at("acc", 48)("acc", [P, TT, DM])
    place = Stretches(nc, (z + 64 * KB, z + 80 * KB), (z + 144 * KB, z + 176 * KB), (query.at, end))
    attention_phase(nc, M, place, wq_raw, wqh, wql, K, V, acc, D["w_q"], D["w_o"])
    M.acc = acc
    if stop_after == "att": return M
    finish_phase(nc, "fc", M, at("fc", 80), 0, acc=acc,
                 ahead=step_weights(mlp_raw, D["w_mlp"], RC) + step_weights(mlp_base, D["b_mlp"], RC))
    if stop_after == "fc": return M

    widen_phase(nc, "md", M, mlp1, F1, "diff", D["w_mlp"], D["b_mlp"], hidden=hidden1, coeff=M.coeff, second=(down1,),
                raw=mlp_raw, base=mlp_base)
    M.hidden, M.down = hidden1, down1
    if stop_after == "md": return M
    last = Stretches(nc, (z + 16 * KB, z + 48 * KB), (z + 132 * KB, end))
    finish_phase(nc, "fd", M, last, F1, hidden=plain(hidden1), w_raw=down1, last_out=out)
    return M




def shape_constants():
    c = np.zeros((P, C_END), np.float32)
    c[:, C_ID:C_ID + P] = np.eye(P, dtype=np.float32)
    inv = 1.0 / 10000.0 ** (np.arange(0, HD, 2, dtype=np.float32) / HD)
    freqs = np.outer(np.arange(SEQ, dtype=np.float32), inv.astype(np.float32)).astype(np.float32)
    cos, sin = np.cos(freqs).T.astype(np.float32), np.sin(freqs).T.astype(np.float32)
    c[:, C_COS:C_COS + SEQ] = np.concatenate([cos, cos])
    c[:, C_SIN:C_SIN + SEQ] = np.concatenate([-sin, sin])
    kc, ks = cos[:ROPE_HALF], sin[:ROPE_HALF]
    c[:, C_COSK:C_COSK + SEQ] = np.concatenate([kc, kc, kc, kc])
    c[:, C_SINK:C_SINK + SEQ] = np.concatenate([-ks, ks, -ks, ks])
    c[:, C_MASK:C_MASK + P] = np.where(np.arange(P)[None, :] > np.arange(P)[:, None], NEG, 0.0)
    m = np.zeros((NX, NX), np.float32)
    for lo, hi in ((0, RANK), (RANK, RANK + N_ST), (RANK + N_ST, NX)):
        m[lo:hi, lo:hi] = 1.0 / (hi - lo)
    return c, m


def stationary(w, tiles=None):
    o, i = w.shape
    return w.reshape(o // P, P, i // P, P).transpose(3, 0, 2, 1)


def rows_padded(w, n):
    return np.concatenate([w, np.zeros((n - w.shape[0],) + w.shape[1:], w.dtype)])


def contraction_major(w):
    o, i = w.shape
    return np.ascontiguousarray(w.T.reshape(i // P, P, o).transpose(1, 0, 2))


def lay_out(a):
    flat = lambda w: np.ascontiguousarray(w.reshape(P, -1))
    per_channel = lambda v: v.reshape(KI, P, -1).transpose(1, 0, 2).reshape(P, -1)
    c, m = shape_constants()
    L = {"x": a["L0_attn_hidden_states"].reshape(TOK, DM), "const": c, "block_mean": m}
    L["vec"] = np.ascontiguousarray(np.concatenate(
        [per_channel(a["L0_attn_conv_w"]), per_channel(a["L0_attn_conv_b"]), per_channel(a["L0_attn_b_dt"])]
        + [per_channel(a["L0_attn_A_log"])] * BATCH + [per_channel(a["L0_attn_D"])] * BATCH, axis=1))
    w = a["L0_attn_W_in"]
    L["w_in"] = flat(np.stack([stationary(w[:D_IN]), stationary(w[D_IN:])], axis=2))
    L["w_x"] = contraction_major(a["L0_attn_W_x"])
    L["w_dt"] = rows_padded(np.ascontiguousarray(a["L0_attn_W_dt"].T), P)
    L["w_out"] = contraction_major(a["L0_attn_W_out"])
    g, u = (rows_padded(a[f"L0_ffn_{n}_w"], F0 * P) for n in ("gate", "up"))
    L["w_gu"] = flat(np.stack([stationary(g), stationary(u)], axis=2))
    L["w_down"] = contraction_major(rows_padded(a["L0_ffn_down_w"].T, F0 * P).T)
    for n in ("gate", "up"):
        L[f"{n}_s"] = np.ascontiguousarray(rows_padded(a[f"L0_ffn_{n}_s"], F0 * P).reshape(F0, P).T)
    L["down_s"] = a["L0_ffn_down_s"].reshape(1, DM)
    dk, kr, upk = (stationary(a[f"L1_attn_{n}"]).reshape(P, KM, -1) for n in ("Wdk", "Wkr", "Wupk"))
    L["w_kv"] = np.ascontiguousarray(np.concatenate([dk, np.stack([kr, upk], axis=2).reshape(P, 2 * KM, -1)], axis=1)).reshape(P, -1)
    L["w_upv"] = contraction_major(a["L1_attn_Wupv"])
    L["w_q"] = np.ascontiguousarray(a["L1_attn_Wq"].reshape(GROUPS, HPG * HD, KM, P).transpose(3, 0, 2, 1)).reshape(P, -1)
    L["w_o"] = np.ascontiguousarray(a["L1_attn_Wo"].T.reshape(GROUPS, HPG, P, DM).transpose(2, 0, 1, 3)).reshape(P, -1)
    for name, w1, w3, w2 in (("w_mlp", "w1", "w3", "w2"), ("b_mlp", "mean_w1", "mean_w3", "mean_w2")):
        s1, s3 = (stationary(a[f"L1_ffn_{n}"]).reshape(P, F1, -1) for n in (w1, w3))
        s2 = contraction_major(a[f"L1_ffn_{w2}"])
        L[name] = np.ascontiguousarray(np.concatenate([s1, s3, s2], axis=2)).reshape(P, -1)
    for n in ("1", "2", "3"):
        L[f"dw{n}"] = a[f"L1_ffn_w{n}"].reshape(P, -1)
        L[f"dm{n}"] = a[f"L1_ffn_mean_w{n}"].reshape(P, -1)
    return L


def kernel(**inputs):
    import concourse.bacc as bacc
    from concourse.bass_utils import run_bass_kernel_spmd

    nc = bacc.Bacc("TRN2", target_bir_lowering=False, num_devices=1)
    arrays = lay_out({n: np.asarray(v) for n, v in inputs.items()})
    D = {n: nc.dram_tensor(f"in_{n}", v.shape, mybir.dt.from_np(v.dtype), kind="ExternalInput").ap() for n, v in arrays.items()}
    D["bc"] = nc.dram_tensor("bc_rows", (BATCH, 2 * N_ST, SEQ), F32).ap()
    out = nc.dram_tensor("out", (TOK, DM), F32, kind="ExternalOutput").ap()
    program(nc, D, out)
    r = run_bass_kernel_spmd(nc, [{f"in_{n}": v for n, v in arrays.items()}], core_ids=[0])
    return r.results[0]["out"].reshape(BATCH, SEQ, DM)
```
